# Optimizing a Trainium2 kernel written in Bass

```python
import numpy as np
import jax
import jax.numpy as jnp

def _softmax(x, axis=-1):
    return jax.nn.softmax(x, axis=axis)

def _gelu(x):
    return jax.nn.gelu(x, approximate=True)

def _silu(x):
    return jax.nn.silu(x)

def _sigmoid(x):
    return jax.nn.sigmoid(x)

def _layernorm(x, axis=-1, eps=1e-05):
    m = jnp.mean(x, axis=axis, keepdims=True)
    v = jnp.var(x, axis=axis, keepdims=True)
    return (x - m) / jnp.sqrt(v + eps)

def _scatter_add(tgt, idx, src, axis=0):
    return tgt.at[idx].add(src)

def _segment_sum(src, seg, n):
    return jax.ops.segment_sum(src, seg, n)
kernel_name = 'mk_macaron_d1_jaxref_r8_d34b66'

def setup_inputs(seed: int=0):
    np.random.seed(seed)
    _w = jnp.asarray

    def _L0_attn_setup():
        import jax, jax.numpy as jnp
        import numpy as np
        from jax import lax
        H, KVH, D, CHUNK = (32, 8, 128, 128)
        ROPE_THETA = 10000.0
        RMS_EPS = 1e-05

        def _rope_tables(L):
            inv_freq = 1.0 / ROPE_THETA ** (jnp.arange(0, D, 2, dtype=jnp.float32) / D)
            ang = jnp.arange(L, dtype=jnp.float32)[:, None] * inv_freq
            cos = jnp.concatenate([jnp.cos(ang), jnp.cos(ang)], axis=-1)[:, None, :]
            sin = jnp.concatenate([jnp.sin(ang), jnp.sin(ang)], axis=-1)[:, None, :]
            return (cos, sin)

        def _apply_rope(x, cos, sin):
            half = D // 2
            rot = jnp.concatenate([-x[..., half:], x[..., :half]], axis=-1)
            return x * cos + rot * sin
        key = jax.random.key(seed)
        ks = jax.random.split(key, 10)
        B, L, HID = (1, 512, 512)
        s = lambda fan: 1.0 / np.sqrt(fan)
        return {'hidden_states': jax.random.normal(ks[0], (B, L, HID), jnp.float32), 'Wq': jax.random.normal(ks[1], (H * D, HID), jnp.float32) * s(HID), 'Wk': jax.random.normal(ks[2], (KVH * D, HID), jnp.float32) * s(HID), 'Wv': jax.random.normal(ks[3], (KVH * D, HID), jnp.float32) * s(HID), 'Wo': jax.random.normal(ks[4], (HID, H * D), jnp.float32) * s(H * D), 'Wg': jax.random.normal(ks[5], (H * D, HID), jnp.float32) * (s(HID) * 2 ** (-2.5)), 'Win': jax.random.normal(ks[6], (H, HID), jnp.float32) * s(HID), 'dt_bias': jnp.zeros((H,), jnp.float32), 'A_log_bias': jnp.log(jax.random.uniform(ks[7], (H,), jnp.float32, 1.0, 16.0)), 'gnorm_w': jnp.ones((D,), jnp.float32)}
    _L0_attn_in = _L0_attn_setup()

    def _L0_ffn_setup():
        import jax, jax.numpy as jnp
        import numpy as np
        K_TOP = 8
        key = jax.random.key(seed)
        k1, k2, k3 = jax.random.split(key, 3)
        B, S, H, E = (4, 512, 512, 64)
        hidden_states = jax.random.normal(k1, (B, S, H), dtype=jnp.float32)
        router_weight = jax.random.normal(k2, (E, H), dtype=jnp.float32)
        router_bias = jnp.zeros((E,), dtype=jnp.float32)
        expert_bias = jax.random.normal(k3, (E, H), dtype=jnp.float32) * 0.1
        return {'hidden_states': hidden_states, 'router_weight': router_weight, 'router_bias': router_bias, 'expert_bias': expert_bias}
    _L0_ffn_in = _L0_ffn_setup()
    _d = {'L0_attn_hidden_states': _L0_attn_in['hidden_states'], 'L0_attn_Wq': _L0_attn_in['Wq'], 'L0_attn_Wk': _L0_attn_in['Wk'], 'L0_attn_Wv': _L0_attn_in['Wv'], 'L0_attn_Wo': _L0_attn_in['Wo'], 'L0_attn_Wg': _L0_attn_in['Wg'], 'L0_attn_Win': _L0_attn_in['Win'], 'L0_attn_dt_bias': _L0_attn_in['dt_bias'], 'L0_attn_A_log_bias': _L0_attn_in['A_log_bias'], 'L0_attn_gnorm_w': _L0_attn_in['gnorm_w'], 'L0_ffn_router_weight': _L0_ffn_in['router_weight'], 'L0_ffn_router_bias': _L0_ffn_in['router_bias'], 'L0_ffn_expert_bias': _L0_ffn_in['expert_bias']}
    _x0 = _d['L0_attn_hidden_states']
    _d['L0_attn_hidden_states'] = jax.random.normal(jax.random.fold_in(jax.random.key(seed), 1), (1, 2048, 512), dtype=_x0.dtype)
    del _x0
    return _d

def reference(L0_attn_hidden_states, L0_attn_Wq, L0_attn_Wk, L0_attn_Wv, L0_attn_Wo, L0_attn_Wg, L0_attn_Win, L0_attn_dt_bias, L0_attn_A_log_bias, L0_attn_gnorm_w, L0_ffn_router_weight, L0_ffn_router_bias, L0_ffn_expert_bias):

    def _L0_attn_ref(hidden_states, Wq, Wk, Wv, Wo, Wg, Win, dt_bias, A_log_bias, gnorm_w):
        import jax, jax.numpy as jnp
        import numpy as np
        from jax import lax
        H, KVH, D, CHUNK = (32, 8, 128, 128)
        ROPE_THETA = 10000.0
        RMS_EPS = 1e-05

        def _rope_tables(L):
            inv_freq = 1.0 / ROPE_THETA ** (jnp.arange(0, D, 2, dtype=jnp.float32) / D)
            ang = jnp.arange(L, dtype=jnp.float32)[:, None] * inv_freq
            cos = jnp.concatenate([jnp.cos(ang), jnp.cos(ang)], axis=-1)[:, None, :]
            sin = jnp.concatenate([jnp.sin(ang), jnp.sin(ang)], axis=-1)[:, None, :]
            return (cos, sin)

        def _apply_rope(x, cos, sin):
            half = D // 2
            rot = jnp.concatenate([-x[..., half:], x[..., :half]], axis=-1)
            return x * cos + rot * sin
        B, L, HID = hidden_states.shape
        NC = L // CHUNK
        q = (hidden_states @ Wq.T).reshape(B, L, H, D)
        k = (hidden_states @ Wk.T).reshape(B, L, KVH, D)
        v = (hidden_states @ Wv.T).reshape(B, L, KVH, D)
        cos, sin = _rope_tables(L)
        q = _apply_rope(q, cos, sin)
        k = _apply_rope(k, cos, sin)
        k = jnp.repeat(k, H // KVH, axis=2)
        v = jnp.repeat(v, H // KVH, axis=2)
        dt = jax.nn.softplus(hidden_states @ Win.T + dt_bias)
        A = -jnp.exp(A_log_bias)
        g = dt * A

        def chunked(t):
            return t.transpose(0, 2, 1, 3).reshape(B, H, NC, CHUNK, D)
        qc, kc = (chunked(q), chunked(k))
        xc = chunked(v * dt[..., None])
        gc = g.transpose(0, 2, 1).reshape(B, H, NC, CHUNK)
        G = jnp.cumsum(gc, axis=-1)
        scores = jnp.einsum('bhnid,bhnjd->bhnij', qc, kc)
        idx = jnp.arange(CHUNK)
        causal = idx[:, None] >= idx[None, :]
        decay = jnp.where(causal, jnp.exp(G[..., :, None] - G[..., None, :]), 0.0)
        y_intra = jnp.einsum('bhnij,bhnjd->bhnid', scores * decay, xc)
        Glast = G[..., -1:]
        k_dec = kc * jnp.exp(Glast - G)[..., None]
        cstates = jnp.einsum('bhnjd,bhnje->bhnde', k_dec, xc)
        chunk_decay = jnp.exp(G[..., -1])

        def step(state, inp):
            dec, cs = inp
            return (state * dec + cs, state)
        init = jnp.zeros((B, H, D, D), hidden_states.dtype)
        _, prev = lax.scan(step, init, (chunk_decay.transpose(2, 0, 1)[..., None, None], cstates.transpose(2, 0, 1, 3, 4)))
        prev = prev.transpose(1, 2, 0, 3, 4)
        y_inter = jnp.einsum('bhnid,bhnde->bhnie', qc * jnp.exp(G)[..., None], prev)
        y = (y_intra + y_inter).reshape(B, H, L, D).transpose(0, 2, 1, 3)
        rms = jnp.sqrt(jnp.mean(jnp.square(y), axis=-1, keepdims=True) + RMS_EPS)
        y = y / rms * gnorm_w
        gate = (hidden_states @ Wg.T).reshape(B, L, H, D)
        y = y * (gate * jax.nn.sigmoid(gate))
        return y.reshape(B, L, H * D) @ Wo.T

    def _L0_ffn_ref(hidden_states, router_weight, router_bias, expert_bias):
        import jax, jax.numpy as jnp
        import numpy as np
        K_TOP = 8
        B, S, H = hidden_states.shape
        E = router_weight.shape[0]
        T = B * S
        flat = hidden_states.reshape(T, H)
        logits = jnp.einsum('th,eh->te', flat, router_weight) + router_bias
        scores = jax.nn.softmax(logits, axis=-1)
        topk_w, topk_idx = jax.lax.top_k(scores, K_TOP)
        w_sum = topk_w.sum(axis=-1, keepdims=True)
        w_dense = jnp.zeros((T, E), dtype=scores.dtype).at[jnp.arange(T)[:, None], topk_idx].add(topk_w)
        bias_mix = jnp.einsum('te,eh->th', w_dense, expert_bias)
        out = flat * w_sum + bias_mix
        return out.reshape(B, S, H)
    x = L0_attn_hidden_states
    x = x + 0.5 * _L0_ffn_ref(_layernorm(x, axis=-1), L0_ffn_router_weight, L0_ffn_router_bias, L0_ffn_expert_bias)
    x = x + _L0_attn_ref(_layernorm(x, axis=-1), L0_attn_Wq, L0_attn_Wk, L0_attn_Wv, L0_attn_Wo, L0_attn_Wg, L0_attn_Win, L0_attn_dt_bias, L0_attn_A_log_bias, L0_attn_gnorm_w)
    x = x + 0.5 * _L0_ffn_ref(_layernorm(x, axis=-1), L0_ffn_router_weight, L0_ffn_router_bias, L0_ffn_expert_bias)
    return x

_drawn_inputs = setup_inputs


def setup_inputs(seed=0):
    import zlib

    import numpy as np

    out = dict(_drawn_inputs(seed))
    spreads = {'L0_attn_dt_bias': (0.0, 0.8),
     'L0_attn_gnorm_w': (1.0, 0.6),
     'L0_ffn_router_bias': (0.0, 0.8)}
    factors = {'L0_attn_Win': 2.755, 'L0_attn_A_log_bias': 3.496}
    for name, (base, spread) in spreads.items():
        noise = np.random.default_rng([zlib.crc32(name.encode()), seed]).standard_normal(out[name].shape)
        drawn = base * np.exp(spread * noise) if base else spread * noise
        out[name] = jnp.asarray(drawn.astype(out[name].dtype))
    for name, factor in factors.items():
        out[name] = (out[name] * factor).astype(out[name].dtype)
    return out
```

```python
from contextlib import ExitStack

import numpy as np

import concourse.bass as bass
from concourse import mybir

F32 = mybir.dt.float32
BF16 = mybir.dt.bfloat16
ALU = mybir.AluOpType
ACT = mybir.ActivationFunctionType
AX = mybir.AxisListType

P = 128
HID = 512
KT = HID // P
H, KVH = 32, 8
G = H // KVH
L = 2048
NCH = L // P
BLK = 4
TB = BLK * P
NB = L // TB
NE = 64
TOPK = 8
EPS = 1e-5
GW = G * P
NPIECE = 2 + 3 * G
PK, PQ, PV_, PG, PO = 0, 1, 1 + G, 2 + G, 2 + 2 * G
NFILL = 2 + 2 * G
BIGNEG = -30000.0

FILLS = {0: {"A": 0, "B": 1, "C": 2}, 1: {"A": 3, "B": 4, "C": 5}, 2: {"A": 6, "B": 7}, 3: {"A": 8, "C": 9}}


def ring_order(last):
    seq = []
    for n in range(NCH):
        b, s = divmod(n, BLK)
        fills = {} if last and b == NB - 1 else FILLS[s]
        for slot in "ABC":
            if slot in fills:
                seq.append(("F", b, fills[slot]))
        if n:
            seq.append(("W", n - 1))
    seq.append(("W", NCH - 1))
    return {u: r for r, u in enumerate(seq)}


def turn_order(last):
    seq = []
    for n in range(NCH):
        b, s = divmod(n, BLK)
        if n:
            seq.append(("Z", n - 1))
        if s == 1 and not (last and b == NB - 1):
            seq.append(("K", b))
    seq.append(("Z", NCH - 1))
    return {u: r for r, u in enumerate(seq)}


def build(nc, x, cos, sin, masks, wall, rwt, rb, eb2, wint, dtb, alog, gn, out):
    with ExitStack() as ctx:
        def sb(name, shape, dt=F32):
            return ctx.enter_context(nc.sbuf_tensor(name, shape, dt))

        class Sem:

            def __init__(self, name, per=0, base=0):
                self.s = ctx.enter_context(nc.semaphore(name))
                self.per, self.base = per, base

        def wait(eng, sem, g, idx):
            v = g * sem.per + (sem.base + idx + 1)
            if isinstance(v, int) and v <= 0:
                return
            eng.wait_ge(sem.s, v)

        opened = {}

        def open_sems(eng, name):
            for sem in opened[name]:
                eng.sem_inc(sem.s, 1)

        def inc(ins, sem, by=1):
            ins.then_inc(sem.s, by)

        ACC = sb("ACC", [P, NCH, HID])
        XTH = sb("XTH", [P, KT, L], BF16)
        XTL = sb("XTL", [P, KT, L], BF16)
        COS = sb("COS", [P, L])
        SIN = sb("SIN", [P, L])
        WH = sb("WH", [P, NPIECE, HID], BF16)
        WL = sb("WL", [P, NPIECE, HID], BF16)
        STAGE = sb("STAGE", [P, 2, HID])
        EG = sb("EG", [P, KVH, NCH, G])
        WJ = sb("WJ", [P, KVH, NCH, G])
        DT = sb("DT", [P, KVH, NCH, G])
        DCH = sb("DCH", [P, KVH, NCH, G])
        GH = sb("GH", [P, KVH, NCH, G], BF16)
        GL = sb("GL", [P, KVH, NCH, G], BF16)
        MASKS = sb("MASKS", [P, 3, P])
        MB = sb("MB", [P, 3, P], BF16)
        NEGM = sb("NEGM", [P, GW], BF16)
        ONES = sb("ONES", [P, P])
        HALF = sb("HALF", [P, G])
        EPSC = sb("EPSC", [P, G])
        GNH = sb("GNH", [P, 1])
        RWT = sb("RWT", [P, KT, NE])
        RB = sb("RB", [P, NE])
        EBH = sb("EBH", [P, HID], BF16)
        EBL = sb("EBL", [P, HID], BF16)

        BANK = [ctx.enter_context(nc.psum_tensor(f"B{i}", [P, 512], F32)) for i in range(8)]
        RING = BANK[0:2]
        B_S, B_D, B_PV, B_IN, B_CS, B_T = BANK[2:8]

        ffn = ExitStack()

        def fb(name, shape, dt=F32):
            return ffn.enter_context(nc.sbuf_tensor(name, shape, dt))

        def head(st, name, shape, dt=F32):
            return st.enter_context(nc.sbuf_tensor(name, shape, dt))

        def ffn_memory():
            m = {}
            for name, shape, dt in (
                    ("XN", [P, BLK, HID], F32), ("XNT", [P, BLK, HID], F32), ("BS", [P, BLK, 6], F32), ("MV", [P, BLK, 2], F32),
                    ("VE", [P, BLK], F32), ("RSTD", [P, BLK], F32), ("LG", [P, BLK, NE], F32), ("MX", [P, BLK, TOPK], F32),
                    ("MR", [P, BLK, NE], F32), ("NM", [P, BLK], F32), ("EX", [P, BLK, NE], F32), ("SUM", [P, BLK], F32),
                    ("MK", [P, BLK, NE], F32), ("WU", [P, BLK, NE], F32), ("S8", [P, BLK], F32), ("RC", [P, BLK], F32),
                    ("HRC", [P, BLK], F32), ("WS", [P, BLK], F32), ("WN", [P, BLK, NE], F32), ("WHL", [P, BLK, 2 * NE], BF16),
                    ("WT", [P, BLK, P], BF16), ("WINF", [P, KT, H], F32), ("WINH", [P, KT, H], BF16), ("WINL", [P, KT, H], BF16),
                    ("DTB", [P, H], F32), ("ALOG", [P, H], F32), ("EBF", [P, HID], F32), ("NEGF", [P, GW], F32),
                    ("GN", [P, 1], F32), ("SP", [P, 6, NCH * H], F32)):
                m[name] = head(ffn, name, shape, dt)
            return m

        m = ffn_memory()
        XN, XNT, BS, MV, VE, RSTD, LG, MX, MR, NM, EX, SUM, MK, WU, S8, RC, HRC, WS, WN, WHL, WT = (m[k] for k in (
            "XN XNT BS MV VE RSTD LG MX MR NM EX SUM MK WU S8 RC HRC WS WN WHL WT".split()))
        WINF, WINH, WINL, DTB, ALOG, EBF, NEGF, GN, SP = (m[k] for k in "WINF WINH WINL DTB ALOG EBF NEGF GN SP".split())
        ffn.close()

        QH = sb("QH", [P, 2, G, TB], BF16)
        QL = sb("QL", [P, 2, G, TB], BF16)
        KH = sb("KH", [P, 2, TB], BF16)
        KL = sb("KL", [P, 2, TB], BF16)
        KDH = sb("KDH", [P, 2, TB], BF16)
        KDL = sb("KDL", [P, 2, TB], BF16)
        VF = sb("VF", [P, 2, TB])
        VH = sb("VH", [P, 2, TB], BF16)
        VL = sb("VL", [P, 2, TB], BF16)
        G2 = sb("G2", [P, BLK, GW])
        QS = sb("QS", [P, 2, TB])
        QF = sb("QF", [P, 2, TB])
        KF = sb("KF", [P, TB])
        TH = sb("TH", [P, GW])
        MH = sb("MH", [P, G, P], BF16)
        ML = sb("ML", [P, G, P], BF16)
        DEC = sb("DEC", [P, GW])
        PF = sb("PF", [P, GW])
        PH = sb("PH", [P, 2, GW], BF16)
        PL = sb("PL", [P, 2, GW], BF16)
        WVF = sb("WVF", [P, G, P])
        WVH = sb("WVH", [P, GW], BF16)
        WVL = sb("WVL", [P, GW], BF16)
        YF = sb("YF", [P, GW])
        SQ = sb("SQ", [P, G, P])
        SS = sb("SS", [P, G])
        RM = sb("RM", [P, G])
        RR = sb("RR", [P, G])
        ZF = sb("ZF", [P, GW])
        ZTH = sb("ZTH", [P, GW], BF16)
        ZTL = sb("ZTL", [P, GW], BF16)
        ST = sb("ST", [P, GW])
        STH = sb("STH", [P, GW], BF16)
        STL = sb("STL", [P, GW], BF16)

        LTF, TRIF, IDF = MASKS[:, 0, :], MASKS[:, 1, :], MASKS[:, 2, :]
        LTB, TRIB, IDB = MB[:, 0, :], MB[:, 1, :], MB[:, 2, :]

        n_ring, n_turn = len(ring_order(False)), len(turn_order(False))
        ring_full = Sem("ring_full", n_ring, NFILL)
        ring_free = Sem("ring_free", n_ring, NFILL)
        turn_free = Sem("turn_free", n_turn, 1)
        scores_full = Sem("scores_full", NCH)
        logdecay_full = Sem("logdecay_full", NCH)
        inter_full = Sem("inter_full", NCH, 1)
        intra_full = Sem("intra_full", NCH, 1)
        cs_full = Sem("cs_full", NCH, 1)
        zt_full = Sem("zt_full", NCH, 1)
        kt_full = Sem("kt_full", NB)
        swap_ready = Sem("swap_ready", NB * 5)
        qh_ready = Sem("qh_ready", NB * 5)
        v_ready = Sem("v_ready", NB)
        tanh_ready = Sem("tanh_ready", NCH)
        decay_ready = Sem("decay_ready", NCH)
        ph_ready = Sem("ph_ready", NCH)
        wvh_ready = Sem("wvh_ready", NCH)
        sth_ready = Sem("sth_ready", NCH, 1)
        sq_ready = Sem("sq_ready", NCH, 1)
        zth_ready = Sem("zth_ready", NCH)
        kdh_ready = Sem("kdh_ready", NB)
        wh_ready = Sem("wh_ready", NPIECE)
        qf_ready = Sem("qf_ready", NB * 5)
        p_ready = Sem("p_ready", NCH)
        inter_read = Sem("inter_read", NCH, 1)
        y_ready = Sem("y_ready", NCH, 1)
        ss_ready = Sem("ss_ready", NCH, 1)
        z_ready = Sem("z_ready", NCH, 1)
        st_ready = Sem("st_ready", NCH, 1)
        stl_ready = Sem("stl_ready", NCH, 1)
        sin_ready = Sem("sin_ready", NB * 5)
        ql_ready = Sem("ql_ready", NB * 5)
        m_ready = Sem("m_ready", NCH)
        wvf_ready = Sem("wvf_ready", NCH, 1)
        wvl_ready = Sem("wvl_ready", NCH)
        pl_ready = Sem("pl_ready", NCH)
        rm_ready = Sem("rm_ready", NCH, 1)
        rr_ready = Sem("rr_ready", NCH)
        wo_scaled = Sem("wo_scaled", G)
        wl_ready = Sem("wl_ready", NPIECE)
        w_landed = [Sem(f"w_landed{i}") for i in range(2)]

        opened.update(tensor=(cs_full, inter_full, intra_full, zt_full), scalar=(sq_ready, sth_ready), gpsimd=(rm_ready, wvf_ready),
                      vector=(inter_read, ss_ready, st_ready, stl_ready, y_ready, z_ready))

        f_bs, f_mv, f_ve, f_rstd, f_xn = (Sem(n, 2) for n in ("f_bs", "f_mv", "f_ve", "f_rstd", "f_xn"))
        f_tp, f_xnt, f_lg, f_l, f_mx, f_mr, f_nm, f_ex = (Sem(n, k) for n, k in (
            ("f_tp", 4), ("f_xnt", 4), ("f_lg", 1), ("f_l", 1), ("f_mx", 1), ("f_mr", 1), ("f_nm", 1), ("f_ex", 1)))
        f_gate = Sem("f_gate", 9)
        f_wt, f_wtc, f_mix, f_ax, f_acc = (Sem(n, k) for n, k in (
            ("f_wt", 1), ("f_wtc", 1), ("f_mix", 4), ("f_ax", 4), ("f_acc", 4)))
        f_tp2, f_xth, f_xtl, f_dt = (Sem(n, 4) for n in ("f_tp2", "f_xth", "f_xtl", "f_dt"))
        x_landed = [Sem(f"x_landed{i}") for i in range(NB)]
        c_landed = Sem("c_landed")
        rope_landed = Sem("rope_landed")
        out_sent = Sem("out_sent")
        const_pool, const_dve, const_act = Sem("const_pool"), Sem("const_dve"), Sem("const_act")
        prep_dve, prep_act, prep_pe, prep_abs = Sem("prep_dve"), Sem("prep_act"), Sem("prep_pe"), Sem("prep_abs")
        prep_chain = Sem("prep_chain")
        attn_done = Sem("attn_done")

        block = ctx.enter_context(nc.Block())

        def mm3(out_, ah, al, bh, bl, first, last):
            nc.tensor.matmul(out_, ah, bh, start=first, stop=False)
            nc.tensor.matmul(out_, ah, bl, start=False, stop=False)
            return nc.tensor.matmul(out_, al, bh, start=False, stop=last)

        def v_done(eng, g, b):
            wait(eng, ring_free, g, ring_order(False)[("F", b - 1, PV_)] if b else -1)

        def kd_done(eng, g, b):
            wait(eng, turn_free, g, turn_order(False)[("K", b - 1)] if b else -1)

        @block.sync
        def _(sp):
            for k in range(NB):
                inc(sp.dma_start(ACC[:, k * BLK:(k + 1) * BLK, :], x[k]), x_landed[k], 16)
                if k == 0:
                    for dst, src in ((MASKS[:, :, :], masks[:, 0:3 * P]), (NEGF[:, :], masks[:, 3 * P:]), (RWT[:, :, :], rwt),
                                     (RB[:, :], rb), (EBF[:, :], eb2), (WINF[:, :, :], wint), (DTB[:, :], dtb),
                                     (ALOG[:, :], alog), (GN[:, :], gn)):
                        inc(sp.dma_start(dst, src), c_landed, 16)
            inc(sp.dma_start(COS[:, :], cos), rope_landed, 16)
            inc(sp.dma_start(SIN[:, :], sin), rope_landed, 16)

            def load_weights(g):
                for i in range(NPIECE):
                    if not (isinstance(g, int) and g == 0 and i < 2):
                        wait(sp, wl_ready, g, i - 2)
                    inc(sp.dma_start(STAGE[:, i % 2, :], wall[g, i] if isinstance(g, int)
                                     else wall[bass.ds(g, 1), i].rearrange("a p n -> (a p) n")), w_landed[i % 2], 16)
            load_weights(0)
            with sp.Fori(1, KVH) as g:
                load_weights(g)
            for k in range(NB):
                wait(sp, f_acc, NB + k, 3)
                inc(sp.dma_start(out[k], ACC[:, k * BLK:(k + 1) * BLK, :]), out_sent, 16)
            sp.wait_ge(out_sent.s, 16 * NB)

        def ffn_dve(dve, blk, f, first):
            A = ACC[:, blk * BLK:(blk + 1) * BLK, :]

            def stats(k):
                for i in range(BLK):
                    ins = nc.vector.bn_stats(BS[:, i, :], A[:, i, :])
                inc(ins, f_bs)
                wait(dve, f_bs, f, k)
                for i in range(BLK):
                    ins = nc.vector.bn_aggr(MV[:, i, :], BS[:, i, :])
                inc(ins, f_mv)

            def normalise(k):
                wait(dve, f_rstd, f, k)
                for i in range(BLK):
                    ins = nc.vector.tensor_scalar(XN[:, i, :], A[:, i, :], MV[:, i, 0:1], RSTD[:, i:i + 1],
                                                  ALU.subtract, ALU.mult)
                inc(ins, f_xn)
            once = 0 if first else NB - f
            stats(once)
            normalise(once)
            wait(dve, f_lg, f, 0)
            inc(nc.vector.tensor_tensor(LG[:, :, :], BANK[4][:, 0:BLK * NE].rearrange("p (b e) -> p b e", b=BLK),
                                        RB[:, None, :].broadcast_to([P, BLK, NE]), ALU.add), f_l)
            wait(dve, f_l, f, 0)
            for i in range(BLK):
                ins = nc.vector.max(MX[:, i, :], LG[:, i, :])
            inc(ins, f_mx)
            wait(dve, f_mx, f, 0)
            inc(nc.vector.tensor_scalar(NM[:, :], MX[:, :, 0], -1.0, None, ALU.mult), f_nm)
            for i in range(BLK):
                ins = nc.vector.match_replace(MR[:, i, :], MX[:, i, :], LG[:, i, :], -3.0e38)
            inc(ins, f_mr)
            wait(dve, f_mr, f, 0)
            step = [0]

            def chain(ins):
                inc(ins, f_gate)
                wait(dve, f_gate, f, step[0])
                step[0] += 1
            chain(nc.vector.tensor_tensor(MK[:, :, :], LG[:, :, :], MR[:, :, :], ALU.not_equal))
            wait(dve, f_ex, f, 0)
            chain(nc.vector.tensor_reduce(SUM[:, :], EX[:, :, :], AX.X, ALU.add))
            chain(nc.vector.tensor_tensor(WU[:, :, :], MK[:, :, :], EX[:, :, :], ALU.mult))
            chain(nc.vector.tensor_reduce(S8[:, :], WU[:, :, :], AX.X, ALU.add))
            chain(nc.vector.reciprocal(RC[:, :], SUM[:, :]))
            chain(nc.vector.tensor_scalar(HRC[:, :], RC[:, :], 0.5, None, ALU.mult))
            nc.vector.tensor_tensor(WS[:, :], S8[:, :], HRC[:, :], ALU.mult)
            chain(nc.vector.tensor_tensor(WN[:, :, :], WU[:, :, :], HRC[:, :, None].broadcast_to([P, BLK, NE]), ALU.mult))
            chain(nc.vector.tensor_copy(WHL[:, :, 0:NE], WN[:, :, :]))
            inc(nc.vector.tensor_tensor(WHL[:, :, NE:2 * NE], WN[:, :, :], WHL[:, :, 0:NE], ALU.subtract), f_gate)
            for i in range(BLK):
                inc(nc.vector.scalar_tensor_tensor(A[:, i, :], XN[:, i, :], WS[:, i:i + 1], A[:, i, :],
                                                   ALU.mult, ALU.add), f_ax)
            for i in range(BLK):
                wait(dve, f_ax, f, i)
                wait(dve, f_mix, f, i)
                inc(nc.vector.tensor_tensor(A[:, i, :], A[:, i, :], BANK[i][:, :], ALU.add), f_acc)
            if first:
                wait(dve, f_acc, f, 3)
                stats(1)
                wait(dve, f_ax, f, 3)
                normalise(1)
                for i in range(BLK):
                    wait(dve, f_xth, f, i)
                    tok = blk * TB + i * P
                    inc(nc.vector.tensor_tensor(XTL[:, :, tok:tok + P], BANK[i][:, :].rearrange("p (k t) -> p k t", k=KT),
                                                XTH[:, :, tok:tok + P], ALU.subtract), f_xtl)

        def ffn_pool(pool, f, first):
            for k in (0, 1) if first else (NB - f,):
                wait(pool, f_mv, f, k)
                inc(nc.gpsimd.tensor_tensor(VE[:, :], MV[:, :, 1], EPSC[:, :], ALU.add), f_ve)
                wait(pool, f_ve, f, k)
                inc(nc.gpsimd.tensor_tensor(RSTD[:, :], VE[:, :], HALF[:, 0:BLK], ALU.pow), f_rstd)

        def ffn_pe(pe, blk, f, first, prev_first):
            wait(pe, f_xn, f, 0 if first else NB - f)
            for i in range(BLK):
                if prev_first:
                    wait(pe, f_xtl, f, i - 4)
                else:
                    wait(pe, f_acc, f, i - 4)
                for k in range(KT):
                    ins = nc.tensor.transpose(BANK[i][:, k * P:(k + 1) * P], XN[:, i, k * P:(k + 1) * P], IDF)
                inc(ins, f_tp)
            wait(pe, f_l, f, -1)
            for i in range(BLK):
                wait(pe, f_xnt, f, i)
                for k in range(KT):
                    ins = nc.tensor.matmul(BANK[4][:, i * NE:(i + 1) * NE], XNT[:, i, k * P:(k + 1) * P], RWT[:, k, :],
                                           start=(k == 0), stop=(k == KT - 1))
            inc(ins, f_lg)
            wait(pe, f_gate, f, 8)
            WTP = BANK[5][:, 0:256].bitcast(BF16)
            for i in range(BLK):
                ins = nc.tensor.transpose(WTP[:, i * P:(i + 1) * P], WHL[:, i, :], IDB)
            inc(ins, f_wt)
            wait(pe, f_wtc, f, 0)
            for i in range(BLK):
                nc.tensor.matmul(BANK[i][:, :], WT[:, i, :], EBH[:, :], start=True, stop=False)
                inc(nc.tensor.matmul(BANK[i][:, :], WT[:, i, :], EBL[:, :], start=False, stop=True), f_mix)
            if first:
                wait(pe, f_xn, f, 1)
                for i in range(BLK):
                    wait(pe, f_acc, f, i)
                    for k in range(KT):
                        ins = nc.tensor.transpose(BANK[i][:, k * P:(k + 1) * P], XN[:, i, k * P:(k + 1) * P], IDF)
                    inc(ins, f_tp2)
                for i in range(BLK):
                    wait(pe, f_xtl, f, i)
                    tok = blk * TB + i * P
                    for k in range(KT):
                        ins = mm3(BANK[6][:, (blk * BLK + i) * H:(blk * BLK + i + 1) * H],
                                  XTH[:, k, tok:tok + P], XTL[:, k, tok:tok + P], WINH[:, k, :], WINL[:, k, :],
                                  k == 0, k == KT - 1)
                    inc(ins, f_dt)

        def ffn_act(act, blk, f, first):
            for i in range(BLK):
                wait(act, f_tp, f, i)
                inc(nc.scalar.activation(XNT[:, i, :], BANK[i][:, :], ACT.Copy), f_xnt)
            wait(act, f_nm, f, 0)
            wait(act, f_l, f, 0)
            for i in range(BLK):
                ins = nc.scalar.activation(EX[:, i, :], LG[:, i, :], ACT.Exp, bias=NM[:, i:i + 1])
            inc(ins, f_ex)
            wait(act, f_wt, f, 0)
            inc(nc.scalar.activation(WT[:, :, :], BANK[5][:, 0:256].bitcast(BF16).rearrange("p (b t) -> p b t", b=BLK),
                                     ACT.Copy), f_wtc)
            if first:
                for i in range(BLK):
                    wait(act, f_tp2, f, i)
                    inc(nc.scalar.activation(XTH[:, :, blk * TB + i * P:blk * TB + (i + 1) * P],
                                             BANK[i][:, :].rearrange("p (k t) -> p k t", k=KT), ACT.Copy), f_xth)

        @block.tensor
        def _(pe):
            open_sems(pe, "tensor")
            pe.wait_ge(const_dve.s, 7)
            pe.wait_ge(const_act.s, 2)
            for k in range(NB):
                ffn_pe(pe, k, k, True, True)
            pe.wait_ge(prep_dve.s, 1)
            for j, lhs in enumerate((TRIF, LTF, ONES[:, :])):
                inc(nc.tensor.matmul(BANK[2 + j][:, :], lhs, SP[:, 5, :], start=True, stop=True), prep_pe)

            def wkt(piece, k):
                return WH[:, piece, k * P:(k + 1) * P], WL[:, piece, k * P:(k + 1) * P]

            def fill(g, b, item, use, fresh, gw):
                bank = RING[use % 2]
                wait(pe, ring_free, g, use - 2)
                t0 = b % NB * TB
                if fresh:
                    piece = item if item <= PV_ else PG + KT - 1
                    wait(pe, wh_ready, gw, piece)
                    wait(pe, wl_ready, gw, piece)
                if item < PV_:
                    for k in range(KT):
                        wh, wl = wkt(item, k)
                        ins = mm3(bank[:, :], wh, wl, XTH[:, k, t0:t0 + TB], XTL[:, k, t0:t0 + TB], k == 0, k == KT - 1)
                elif item == PV_:
                    for s in range(BLK):
                        for k in range(KT):
                            t = t0 + s * P
                            wh, wl = wkt(item, k)
                            ins = mm3(bank[:, s * P:(s + 1) * P], XTH[:, k, t:t + P], XTL[:, k, t:t + P], wh, wl,
                                      k == 0, k == KT - 1)
                else:
                    t = t0 + (item - PG) * P
                    for k in range(KT):
                        ins = mm3(bank[:, :], XTH[:, k, t:t + P], XTL[:, k, t:t + P], WH[:, PG + k, :], WL[:, PG + k, :],
                                  k == 0, k == KT - 1)
                inc(ins, ring_full)

            def turn_keys(g, b, use):
                wait(pe, turn_free, g, use - 1)
                wait(pe, qf_ready, g, 5 * b)
                for s in range(BLK):
                    ins = nc.tensor.transpose(B_T[:, s * P:(s + 1) * P], KF[:, s * P:(s + 1) * P], IDF)
                inc(ins, kt_full)

            def scores(g, n):
                b, s = divmod(n, BLK)
                par, t = b % 2, s * P
                if s == 0:
                    wait(pe, qh_ready, g, 5 * b + 4)
                    wait(pe, ql_ready, g, 5 * b + 4)
                wait(pe, p_ready, g, n - 1)
                inc(mm3(B_S[:, :], KH[:, par, t:t + P], KL[:, par, t:t + P], QH[:, par, :, t:t + P], QL[:, par, :, t:t + P],
                        True, True), scores_full)
                wait(pe, m_ready, g, n)
                wait(pe, decay_ready, g, n - 1)
                nc.tensor.matmul(B_D[:, :], IDB, NEGM[:, :], start=True, stop=False)
                nc.tensor.matmul(B_D[:, :], LTB, MH[:, :, :], start=False, stop=False)
                inc(nc.tensor.matmul(B_D[:, :], LTB, ML[:, :, :], start=False, stop=True), logdecay_full)

            def attend(g, n):
                b, s = divmod(n, BLK)
                par, t = b % 2, s * P
                wait(pe, inter_read, g, n - 1)
                wait(pe, sth_ready, g, n - 1)
                wait(pe, stl_ready, g, n - 1)
                for h in range(G):
                    c = slice(h * P, (h + 1) * P)
                    ins = mm3(B_IN[:, c], QH[:, par, h, t:t + P], QL[:, par, h, t:t + P], STH[:, c], STL[:, c], True, True)
                inc(ins, inter_full)
                wait(pe, y_ready, g, n - 1)
                wait(pe, ph_ready, g, n)
                wait(pe, pl_ready, g, n)
                if s == 0:
                    wait(pe, v_ready, g, b)
                    v_done(pe, g, b)
                for h in range(G):
                    c = slice(h * P, (h + 1) * P)
                    ins = mm3(B_PV[:, c], PH[:, n % 2, c], PL[:, n % 2, c], VH[:, par, t:t + P], VL[:, par, t:t + P], True, True)
                inc(ins, intra_full)
                wait(pe, st_ready, g, n - 1)
                wait(pe, wvh_ready, g, n)
                wait(pe, wvl_ready, g, n)
                if s == 0:
                    wait(pe, kdh_ready, g, b)
                    kd_done(pe, g, b)
                inc(mm3(B_CS[:, :], KDH[:, par, t:t + P], KDL[:, par, t:t + P], WVH[:, :], WVL[:, :], True, True), cs_full)

            def turn_z(g, n, use):
                wait(pe, turn_free, g, use - 1)
                wait(pe, z_ready, g, n)
                for h in range(G):
                    ins = nc.tensor.transpose(B_T[:, h * P:(h + 1) * P], ZF[:, h * P:(h + 1) * P], IDF)
                inc(ins, zt_full)

            def project_out(g, n, use, turn_use):
                wait(pe, ring_free, g, use - 2)
                wait(pe, zth_ready, g, n)
                wait(pe, turn_free, g, turn_use)
                if n == 0:
                    wait(pe, wh_ready, g, NPIECE - 1)
                    wait(pe, wl_ready, g, NPIECE - 1)
                for h in range(G):
                    c = slice(h * P, (h + 1) * P)
                    ins = mm3(RING[use % 2][:, :], ZTH[:, c], ZTL[:, c], WH[:, PO + h, :], WL[:, PO + h, :], h == 0, h == G - 1)
                inc(ins, ring_full)

            for item in range(NFILL):
                fill(0, 0, item, item - NFILL, True, 0)
            turn_keys(0, 0, -1)
            scores(0, 0)

            def group(g, last):
                ring, turn = ring_order(last), turn_order(last)
                for n in range(NCH):
                    b, s = divmod(n, BLK)
                    end = last and b == NB - 1

                    def slot(x):
                        if x in FILLS[s] and not end:
                            item = FILLS[s][x]
                            fill(g, b + 1, item, ring[("F", b, item)], b == NB - 1, g + 1)
                    if not (last and n == NCH - 1):
                        scores(g, n + 1)
                    slot("A")
                    attend(g, n)
                    slot("B")
                    if n:
                        turn_z(g, n - 1, turn[("Z", n - 1)])
                    slot("C")
                    if s == 1 and not end:
                        turn_keys(g, b + 1, turn[("K", b)])
                    if n:
                        project_out(g, n - 1, ring[("W", n - 1)], turn[("Z", n - 1)])
                turn_z(g, NCH - 1, turn[("Z", NCH - 1)])
                project_out(g, NCH - 1, ring[("W", NCH - 1)], turn[("Z", NCH - 1)])

            with pe.Fori(0, KVH - 1) as g:
                group(g, False)
            group(KVH - 1, True)
            pe.wait_ge(attn_done.s, 1)
            for k in range(NB):
                ffn_pe(pe, k, k + NB, False, k == 0)

        @block.scalar
        def _(act):
            open_sems(act, "scalar")
            act.wait_ge(c_landed.s, 16 * 9)
            nc.scalar.activation(EBH[:, :], EBF[:, :], ACT.Copy).then_inc(const_act.s, 1)
            nc.scalar.activation(WINH[:, :, :], WINF[:, :, :], ACT.Copy).then_inc(const_act.s, 1)
            for k in range(NB):
                ffn_act(act, k, k, True)
            act.wait_ge(prep_abs.s, 1)
            nc.scalar.activation(SP[:, 2, :], SP[:, 1, :], ACT.Exp, scale=-1.0).then_inc(prep_act.s, 1)
            nc.scalar.activation(ALOG[:, :], ALOG[:, :], ACT.Exp).then_inc(prep_act.s, 1)

            def split_hi(g, i):
                act.wait_ge(w_landed[i % 2].s, (g * (NPIECE // 2) + (i // 2 + 1)) * 16)
                if i >= PO:
                    wait(act, wo_scaled, g, i - PO)
                inc(nc.scalar.activation(WH[:, i, :], STAGE[:, i % 2, :], ACT.Copy), wh_ready)

            def last_use(g, i):
                order = ring_order(False)
                if i <= PV_:
                    wait(act, ring_full, g, order[("F", NB - 2, i)])
                elif i < PO:
                    wait(act, ring_full, g, order[("F", NB - 2, NFILL - 1)])
                else:
                    wait(act, ring_full, g, order[("W", NCH - 1)])

            def swap(g, b, j, use):
                sl = (j + 1) % 2
                wait(act, ring_full, g, use)
                wait(act, qf_ready, g, 5 * b + j - (2 if j else 1))
                bank = RING[use % 2]
                nc.scalar.activation(QS[0:64, sl, :], bank[64:128, :], ACT.Copy)
                inc(nc.scalar.activation(QS[64:128, sl, :], bank[0:64, :], ACT.Copy), swap_ready)

            def hi(g, b, j):
                wait(act, qf_ready, g, 5 * b + j)
                wait(act, inter_full, g, 4 * (b - 1) - 1)
                if j:
                    ins = nc.scalar.activation(QH[:, b % 2, j - 1, :], QF[:, (j - 1) % 2, :], ACT.Copy)
                else:
                    ins = nc.scalar.activation(KH[:, b % 2, :], KF[:, :], ACT.Copy)
                inc(ins, qh_ready)

            def values(g, b, use):
                wait(act, ring_full, g, use)
                wait(act, intra_full, g, 4 * (b - 1) - 1)
                wait(act, wvf_ready, g, 4 * (b - 1) - 1)
                nc.scalar.activation(VF[:, b % 2, :], RING[use % 2][:, :], ACT.Copy)
                inc(nc.scalar.activation(VH[:, b % 2, :], RING[use % 2][:, :], ACT.Copy), v_ready)

            def gate(g, b, s, use, before):
                wait(act, ring_full, g, use)
                wait(act, ring_free, g, before)
                inc(nc.scalar.activation(TH[:, :], RING[use % 2][:, :], ACT.Tanh, scale=0.5), tanh_ready)

            def keys_hi(g, b):
                wait(act, kt_full, g, b)
                wait(act, cs_full, g, 4 * (b - 1) - 1)
                inc(nc.scalar.activation(KDH[:, b % 2, :], B_T[:, :], ACT.Copy), kdh_ready)

            def decay(g, n):
                wait(act, logdecay_full, g, n)
                wait(act, p_ready, g, n - 1)
                inc(nc.scalar.activation(DEC[:, :], B_D[:, :], ACT.Exp), decay_ready)

            def p_hi(g, n):
                wait(act, p_ready, g, n)
                wait(act, intra_full, g, n - 2)
                inc(nc.scalar.activation(PH[:, n % 2, :], PF[:, :], ACT.Copy), ph_ready)

            def wv_hi(g, n):
                wait(act, wvf_ready, g, n)
                wait(act, cs_full, g, n - 1)
                inc(nc.scalar.activation(WVH[:, :], WVF[:, :, :].rearrange("p h e -> p (h e)"), ACT.Copy), wvh_ready)

            def state_hi(g, n):
                wait(act, st_ready, g, n)
                wait(act, inter_full, g, n)
                inc(nc.scalar.activation(STH[:, :], ST[:, :], ACT.Copy), sth_ready)

            def square(g, n):
                wait(act, y_ready, g, n)
                wait(act, ss_ready, g, n - 1)
                inc(nc.scalar.activation(SQ[:, :, :].rearrange("p h e -> p (h e)"), YF[:, :], ACT.Square, scale=float(P) ** -0.5), sq_ready)

            def zt_hi(g, n, before):
                wait(act, zt_full, g, n)
                wait(act, ring_full, g, before)
                inc(nc.scalar.activation(ZTH[:, :], B_T[:, :], ACT.Copy), zth_ready)

            for i in range(NPIECE):
                split_hi(0, i)
            for j, dst in enumerate((EG, WJ, DCH)):
                act.wait_ge(prep_pe.s, j + 1)
                nc.scalar.activation(dst[:, :, :, :].rearrange("p g c h -> p (g c h)"),
                                     BANK[2 + j][:, :], ACT.Exp).then_inc(prep_act.s, 1)
            for item in range(NFILL):
                use = item - NFILL
                if item < PV_:
                    swap(0, 0, item, use)
                    hi(0, 0, item)
                elif item == PV_:
                    values(0, 0, use)
                else:
                    gate(0, 0, item - PG, use, use - 1)
            keys_hi(0, 0)
            decay(0, 0)
            p_hi(0, 0)
            wv_hi(0, 0)

            def group(g, last):
                ring = ring_order(last)
                for n in range(NCH):
                    b, s = divmod(n, BLK)
                    end = last and b == NB - 1

                    def slot(x, part):
                        if x not in FILLS[s] or end:
                            return
                        item = FILLS[s][x]
                        use = ring[("F", b, item)]
                        if item < PV_:
                            (swap(g, b + 1, item, use) if part == 0 else hi(g, b + 1, item))
                        elif part == 0 and item == PV_:
                            values(g, b + 1, use)
                        elif part == 0:
                            gate(g, b + 1, item - PG, use, use - 1)
                    nxt = not (last and n == NCH - 1)
                    if nxt:
                        decay(g, n + 1)
                    slot("A", 0)
                    if nxt:
                        p_hi(g, n + 1)
                    slot("A", 1)
                    state_hi(g, n)
                    square(g, n)
                    slot("B", 0)
                    if nxt:
                        wv_hi(g, n + 1)
                    slot("B", 1)
                    if n:
                        zt_hi(g, n - 1, ring[("W", n - 2)] if n > 1 else -1)
                    slot("C", 0)
                    slot("C", 1)
                    if s == 1 and not end:
                        keys_hi(g, b + 1)
                    if not last:
                        if b == NB - 2 and s >= 2:
                            pieces = range(3 * (s - 2), 3 * (s - 1))
                        elif b == NB - 1 and s < 2:
                            pieces = range(PG + 2 * s, PG + 2 * s + 2)
                        else:
                            pieces = ()
                        for i in pieces:
                            last_use(g, i)
                            split_hi(g + 1, i)
                zt_hi(g, NCH - 1, ring[("W", NCH - 2)])
                if not last:
                    for i in range(PO, NPIECE):
                        last_use(g, i)
                        split_hi(g + 1, i)

            with act.Fori(0, KVH - 1) as g:
                group(g, False)
            group(KVH - 1, True)
            act.wait_ge(attn_done.s, 1)
            for k in range(NB):
                ffn_act(act, k, k + NB, False)

        @block.gpsimd
        def _(pool):
            open_sems(pool, "gpsimd")
            nc.gpsimd.memset(HALF[:, :], -0.5).then_inc(const_pool.s, 1)
            nc.gpsimd.memset(EPSC[:, :], EPS).then_inc(const_pool.s, 1)
            pool.wait_ge(const_pool.s, 2)
            for k in range(NB):
                ffn_pool(pool, k, True)

            def split_lo(g, i):
                if i >= PO:
                    pool.wait_ge(w_landed[i % 2].s, (g * (NPIECE // 2) + (i // 2 + 1)) * 16)
                    inc(nc.gpsimd.tensor_tensor(STAGE[:, i % 2, :], STAGE[:, i % 2, :], GNH[:, 0:1].broadcast_to([P, HID]), ALU.mult), wo_scaled)
                wait(pool, wh_ready, g, i)
                inc(nc.gpsimd.tensor_tensor(WL[:, i, :], STAGE[:, i % 2, :], WH[:, i, :], ALU.subtract), wl_ready)

            def times_sin(g, b, j):
                sl = (j + 1) % 2
                wait(pool, swap_ready, g, 5 * b + j)
                t0 = b % NB * TB
                inc(nc.gpsimd.tensor_tensor(QS[:, sl, :], QS[:, sl, :], SIN[:, t0:t0 + TB], ALU.mult), sin_ready)

            def lo(g, b, j):
                wait(pool, qh_ready, g, 5 * b + j)
                if j:
                    ins = nc.gpsimd.tensor_tensor(QL[:, b % 2, j - 1, :], QF[:, (j - 1) % 2, :], QH[:, b % 2, j - 1, :], ALU.subtract)
                else:
                    ins = nc.gpsimd.tensor_tensor(KL[:, b % 2, :], KF[:, :], KH[:, b % 2, :], ALU.subtract)
                inc(ins, ql_ready)

            def tab(T, g, n):
                flat = T[:, :, :, :].rearrange("p g c h -> p (g c h)")
                if isinstance(g, int):
                    return flat[:, (g * NCH + n) * G:(g * NCH + n + 1) * G]
                return flat[:, bass.ds(g * (NCH * G) + n * G, G)]

            def masked_g(g, n):
                wait(pool, logdecay_full, g, n - 1)
                tri = TRIB[:, None, :].broadcast_to([P, G, P])
                nc.gpsimd.tensor_tensor(MH[:, :, :], tri, tab(GH, g, n)[:, :, None].broadcast_to([P, G, P]), ALU.mult)
                inc(nc.gpsimd.tensor_tensor(ML[:, :, :], tri, tab(GL, g, n)[:, :, None].broadcast_to([P, G, P]), ALU.mult), m_ready)

            def weighted_v(g, n):
                b, s = divmod(n, BLK)
                wait(pool, wvh_ready, g, n - 1)
                wait(pool, wvl_ready, g, n - 1)
                if s == 0:
                    wait(pool, v_ready, g, b)
                inc(nc.gpsimd.tensor_tensor(WVF[:, :, :], VF[:, b % 2, None, s * P:(s + 1) * P].broadcast_to([P, G, P]),
                                            tab(WJ, g, n)[:, :, None].broadcast_to([P, G, P]), ALU.mult), wvf_ready)

            def wv_lo(g, n):
                wait(pool, wvh_ready, g, n)
                wait(pool, cs_full, g, n - 1)
                inc(nc.gpsimd.tensor_tensor(WVL[:, :], WVF[:, :, :].rearrange("p h e -> p (h e)"), WVH[:, :], ALU.subtract), wvl_ready)

            def p_lo(g, n):
                wait(pool, ph_ready, g, n)
                inc(nc.gpsimd.tensor_tensor(PL[:, n % 2, :], PF[:, :], PH[:, n % 2, :], ALU.subtract), pl_ready)

            def inv_rms(g, n):
                wait(pool, ss_ready, g, n)
                inc(nc.gpsimd.tensor_tensor(RM[:, :], SS[:, :], EPSC[:, :], ALU.add), rm_ready)
                wait(pool, rm_ready, g, n)
                wait(pool, z_ready, g, n - 1)
                inc(nc.gpsimd.tensor_tensor(RR[:, :], RM[:, :], HALF[:, :], ALU.pow), rr_ready)

            pool.wait_ge(const_dve.s, 7)
            for i in range(NPIECE):
                split_lo(0, i)
            pool.wait_ge(rope_landed.s, 32)
            pool.wait_ge(prep_dve.s, 5)
            masked_g(0, 0)
            for item in range(PV_):
                times_sin(0, 0, item)
                lo(0, 0, item)
            masked_g(0, 1)
            p_lo(0, 0)
            weighted_v(0, 0)
            wv_lo(0, 0)

            def group(g, last):
                for n in range(NCH):
                    b, s = divmod(n, BLK)
                    end = last and b == NB - 1

                    def slot(x, part):
                        if x in FILLS[s] and not end and FILLS[s][x] < PV_:
                            (times_sin if part == 0 else lo)(g, b + 1, FILLS[s][x])
                    nxt = not (last and n == NCH - 1)
                    slot("A", 0)
                    if nxt:
                        p_lo(g, n + 1)
                    if not (last and n >= NCH - 2):
                        masked_g(g, n + 2)
                    slot("A", 1)
                    if nxt:
                        weighted_v(g, n + 1)
                    slot("B", 0)
                    if nxt:
                        wv_lo(g, n + 1)
                    slot("B", 1)
                    inv_rms(g, n)
                    slot("C", 0)
                    slot("C", 1)
                    if not last:
                        if b == NB - 2 and s >= 2:
                            pieces = range(3 * (s - 2), 3 * (s - 1))
                        elif b == NB - 1 and s < 2:
                            pieces = range(PG + 2 * s, PG + 2 * s + 2)
                        else:
                            pieces = ()
                        for i in pieces:
                            split_lo(g + 1, i)
                if not last:
                    for i in range(PO, NPIECE):
                        split_lo(g + 1, i)

            with pool.Fori(0, KVH - 1) as g:
                group(g, False)
            group(KVH - 1, True)
            pool.wait_ge(attn_done.s, 1)
            for f in range(NB, 2 * NB):
                ffn_pool(pool, f, False)

        @block.vector
        def _(dve):
            open_sems(dve, "vector")
            dve.wait_ge(c_landed.s, 16 * 9)
            nc.vector.tensor_copy(MB[:, :, :], MASKS[:, :, :]).then_inc(const_dve.s, 1)
            nc.vector.tensor_copy(NEGM[:, :], NEGF[:, :]).then_inc(const_dve.s, 1)
            nc.vector.memset(ONES[:, :], 1.0).then_inc(const_dve.s, 1)
            nc.vector.tensor_scalar(GNH[:, :], GN[:, :], 0.5, None, ALU.mult).then_inc(const_dve.s, 1)
            dve.wait_ge(const_act.s, 2)
            nc.vector.tensor_tensor(EBL[:, :], EBF[:, :], EBH[:, :], ALU.subtract).then_inc(const_dve.s, 1)
            nc.vector.tensor_tensor(WINL[:, :, :], WINF[:, :, :], WINH[:, :, :], ALU.subtract).then_inc(const_dve.s, 2)
            for k in range(NB):
                dve.wait_ge(x_landed[k].s, 16)
                ffn_dve(dve, k, k, True)

            wait(dve, f_dt, NB - 1, 3)
            by_chunk = BANK[6][:, :].rearrange("p (c g h) -> p g c h", c=NCH, g=KVH)
            def spt(i):
                return SP[:, i, :]

            def spv(i):
                return SP[:, i, :].rearrange("p (g c h) -> p g c h", g=KVH, c=NCH)
            cnt = [0]
            def link(ins):
                ins.then_inc(prep_chain.s, 1)
                cnt[0] += 1
                dve.wait_ge(prep_chain.s, cnt[0])
            for g in range(KVH):
                ins = nc.vector.tensor_tensor(spv(0)[:, g], by_chunk[:, g],
                                              DTB[:, None, g * G:(g + 1) * G].broadcast_to([P, NCH, G]), ALU.add)
            link(ins)
            nc.vector.scalar_tensor_tensor(spt(1), spt(0), -1.0, spt(0), ALU.mult, ALU.max).then_inc(prep_abs.s, 1)
            dve.wait_ge(prep_act.s, 2)
            link(nc.vector.tensor_scalar(spt(3), spt(2), 2.0, None, ALU.add))
            link(nc.vector.reciprocal(spt(4), spt(3)))
            link(nc.vector.tensor_tensor(spt(3), spt(2), spt(4), ALU.mult))
            link(nc.vector.tensor_tensor(spt(4), spt(3), spt(3), ALU.mult))
            link(nc.vector.tensor_scalar(spt(5), spt(4), 1.0 / 17, None, ALU.mult))
            for d in (15, 13, 11, 9, 7, 5, 3):
                link(nc.vector.scalar_tensor_tensor(spt(5), spt(5), 1.0 / d, spt(4), ALU.add, ALU.mult))
            link(nc.vector.scalar_tensor_tensor(spt(5), spt(5), 1.0, spt(3), ALU.add, ALU.mult))
            link(nc.vector.tensor_scalar(spt(0), spt(0), 0.0, None, ALU.max))
            dtf = DT[:, :, :, :].rearrange("p g c h -> p (g c h)")
            link(nc.vector.scalar_tensor_tensor(dtf, spt(5), 2.0, spt(0), ALU.mult, ALU.add))
            for g in range(KVH):
                ins = nc.vector.scalar_tensor_tensor(spv(5)[:, g], DT[:, g], -1.0,
                                                     ALOG[:, None, g * G:(g + 1) * G].broadcast_to([P, NCH, G]),
                                                     ALU.mult, ALU.mult)
            ins.then_inc(prep_dve.s, 1)
            dve.wait_ge(prep_dve.s, 1)
            ghf, glf = (T[:, :, :, :].rearrange("p g c h -> p (g c h)") for T in (GH, GL))
            nc.vector.tensor_copy(ghf, spt(5)).then_inc(prep_dve.s, 1)
            dve.wait_ge(prep_dve.s, 2)
            nc.vector.tensor_tensor(glf, spt(5), ghf, ALU.subtract).then_inc(prep_dve.s, 1)
            dve.wait_ge(prep_act.s, 5)
            nc.vector.tensor_tensor(WJ[:, :, :, :].rearrange("p g c h -> p (g c h)"),
                                    WJ[:, :, :, :].rearrange("p g c h -> p (g c h)"), dtf, ALU.mult).then_inc(prep_dve.s, 1)
            nc.vector.memset(EG[:, :, 0, :], 0.0)
            nc.vector.memset(DCH[:, :, 0, :], 0.0)
            nc.vector.memset(ST[:, :], 0.0)
            nc.vector.memset(STH[:, :], 0.0)
            nc.vector.memset(STL[:, :], 0.0).then_inc(prep_dve.s, 1)
            dve.wait_ge(prep_dve.s, 5)
            dve.wait_ge(rope_landed.s, 32)

            def tab(T, g, n):
                flat = T[:, :, :, :].rearrange("p g c h -> p (g c h)")
                if isinstance(g, int):
                    return flat[:, (g * NCH + n) * G:(g * NCH + n + 1) * G]
                return flat[:, bass.ds(g * (NCH * G) + n * G, G)]

            def rotate(g, b, j, use, part):
                dst = QF[:, (j - 1) % 2, :] if j else KF[:, :]
                t0 = b % NB * TB
                if part == 0:
                    wait(dve, swap_ready, g, 5 * b + j)
                    wait(dve, qh_ready, g, 5 * b + j - 2)
                    wait(dve, ql_ready, g, 5 * b + j - 2)
                    if j == 0:
                        wait(dve, kt_full, g, b - 1)
                    inc(nc.vector.tensor_tensor(dst, RING[use % 2][:, :], COS[:, t0:t0 + TB], ALU.mult), ring_free)
                else:
                    wait(dve, ring_free, g, use)
                    wait(dve, sin_ready, g, 5 * b + j)
                    inc(nc.vector.tensor_tensor(dst, dst, QS[:, (j + 1) % 2, :], ALU.add), qf_ready)

            def v_lo(g, b, use):
                wait(dve, v_ready, g, b)
                wait(dve, intra_full, g, 4 * (b - 1) - 1)
                inc(nc.vector.tensor_tensor(VL[:, b % 2, :], RING[use % 2][:, :], VH[:, b % 2, :], ALU.subtract), ring_free)

            def silu2(g, b, s, use):
                wait(dve, tanh_ready, g, 4 * b + s)
                wait(dve, z_ready, g, 4 * (b - 1) + s)
                inc(nc.vector.scalar_tensor_tensor(G2[:, s, :], TH[:, :], 1.0, RING[use % 2][:, :], ALU.add, ALU.mult), ring_free)

            def keys_lo(g, b):
                wait(dve, kdh_ready, g, b)
                wait(dve, cs_full, g, 4 * (b - 1) - 1)
                inc(nc.vector.tensor_tensor(KDL[:, b % 2, :], B_T[:, :], KDH[:, b % 2, :], ALU.subtract), turn_free)

            def decayed(g, n):
                wait(dve, scores_full, g, n)
                wait(dve, decay_ready, g, n)
                wait(dve, ph_ready, g, n - 1)
                wait(dve, pl_ready, g, n - 1)
                dt = tab(DT, g, n)
                for h in range(G):
                    c = slice(h * P, (h + 1) * P)
                    ins = nc.vector.scalar_tensor_tensor(PF[:, c], B_S[:, c], dt[:, h:h + 1], DEC[:, c], ALU.mult, ALU.mult)
                inc(ins, p_ready)

            def combine(g, n):
                wait(dve, inter_full, g, n)
                wait(dve, sq_ready, g, n - 1)
                wait(dve, z_ready, g, n - 1)
                y = YF[:, :].rearrange("p (h e) -> p h e", h=G)
                inc(nc.vector.tensor_tensor(y, B_IN[:, :].rearrange("p (h e) -> p h e", h=G),
                                            tab(EG, g, n)[:, :, None].broadcast_to([P, G, P]), ALU.mult), inter_read)
                wait(dve, inter_read, g, n)
                wait(dve, intra_full, g, n)
                inc(nc.vector.tensor_tensor(YF[:, :], B_PV[:, :], YF[:, :], ALU.add), y_ready)

            def update_state(g, n):
                wait(dve, cs_full, g, n)
                wait(dve, sth_ready, g, n - 1)
                wait(dve, stl_ready, g, n - 1)
                dc = tab(DCH, g, n)
                for h in range(G):
                    c = slice(h * P, (h + 1) * P)
                    ins = nc.vector.scalar_tensor_tensor(ST[:, c], ST[:, c], dc[:, h:h + 1], B_CS[:, c], ALU.mult, ALU.add)
                inc(ins, st_ready)

            def state_lo(g, n):
                wait(dve, sth_ready, g, n)
                inc(nc.vector.tensor_tensor(STL[:, :], ST[:, :], STH[:, :], ALU.subtract), stl_ready)

            def sum_squares(g, n):
                wait(dve, sq_ready, g, n)
                wait(dve, rm_ready, g, n - 1)
                inc(nc.vector.tensor_reduce(SS[:, :], SQ[:, :, :], AX.X, ALU.add), ss_ready)

            def gated(g, n):
                wait(dve, rr_ready, g, n)
                wait(dve, zt_full, g, n - 1)
                if n % BLK == 0:
                    gates_done(g, n // BLK)
                for h in range(G):
                    c = slice(h * P, (h + 1) * P)
                    ins = nc.vector.scalar_tensor_tensor(ZF[:, c], YF[:, c], RR[:, h:h + 1], G2[:, n % BLK, c], ALU.mult, ALU.mult)
                inc(ins, z_ready)

            def gates_done(g, b):
                wait(dve, ring_free, g, ring_order(False)[("F", b - 1, NFILL - 1)] if b else -1)

            def zt_lo(g, n, before):
                wait(dve, zth_ready, g, n)
                wait(dve, ring_full, g, before)
                inc(nc.vector.tensor_tensor(ZTL[:, :], B_T[:, :], ZTH[:, :], ALU.subtract), turn_free)

            def add_out(g, n, use):
                wait(dve, ring_full, g, use)
                inc(nc.vector.tensor_tensor(ACC[:, n, :], ACC[:, n, :], RING[use % 2][:, :], ALU.add), ring_free)

            for item in range(NFILL):
                use = item - NFILL
                if item < PV_:
                    rotate(0, 0, item, use, 0)
                    rotate(0, 0, item, use, 1)
                elif item == PV_:
                    v_lo(0, 0, use)
                else:
                    silu2(0, 0, item - PG, use)
            keys_lo(0, 0)
            decayed(0, 0)

            def group(g, last):
                ring = ring_order(last)
                for n in range(NCH):
                    b, s = divmod(n, BLK)
                    end = last and b == NB - 1

                    def slot(x, part):
                        if x not in FILLS[s] or end:
                            return
                        item = FILLS[s][x]
                        use = ring[("F", b, item)]
                        if item < PV_:
                            rotate(g, b + 1, item, use, part)
                        elif part == 0 and item == PV_:
                            v_lo(g, b + 1, use)
                        elif part == 0:
                            silu2(g, b + 1, item - PG, use)
                    if not (last and n == NCH - 1):
                        decayed(g, n + 1)
                    slot("A", 0)
                    slot("A", 1)
                    combine(g, n)
                    update_state(g, n)
                    sum_squares(g, n)
                    state_lo(g, n)
                    slot("B", 0)
                    slot("B", 1)
                    gated(g, n)
                    if n:
                        zt_lo(g, n - 1, ring[("W", n - 2)] if n > 1 else -1)
                    slot("C", 0)
                    slot("C", 1)
                    if s == 1 and not end:
                        keys_lo(g, b + 1)
                    if n:
                        add_out(g, n - 1, ring[("W", n - 1)])
                zt_lo(g, NCH - 1, ring[("W", NCH - 2)])
                add_out(g, NCH - 1, ring[("W", NCH - 1)])

            with dve.Fori(0, KVH - 1) as g:
                group(g, False)
            group(KVH - 1, True)
            wait(dve, ring_free, KVH - 1, ring_order(True)[("W", NCH - 1)])
            nc.vector.engine_nop().then_inc(attn_done.s, 1)
            for k in range(NB):
                ffn_dve(dve, k, k + NB, False)


def constants():
    f = np.float32
    inv = f(1.0) / np.power(f(10000.0), np.arange(0, P, 2, dtype=f) / f(P), dtype=f)
    ang = np.arange(L, dtype=f)[None, :] * np.concatenate([inv, inv])[:, None]
    cos, sin = np.cos(ang, dtype=f), np.sin(ang, dtype=f)
    sin[:P // 2] *= f(-1.0)
    t = np.arange(P)
    masks = np.concatenate([(t[:, None] > t[None, :]), (t[:, None] <= t[None, :]), (t[:, None] == t[None, :])], 1).astype(f)
    neg = np.tile(np.where(t[None, :] < t[:, None], f(BIGNEG), f(0)), (1, G))
    return cos, sin, np.concatenate([masks, neg], 1).astype(f)


def kernel(**inputs):
    import concourse.bacc as bacc
    from concourse.bass_utils import run_bass_kernel_spmd

    a = {k.replace("L0_attn_", "").replace("L0_ffn_", ""): np.asarray(v) for k, v in inputs.items()}

    def by_tile(w):
        return w.reshape(w.shape[0], KT, P).transpose(2, 1, 0)
    cos, sin, masks = constants()
    wall = np.empty((KVH, NPIECE, P, HID), a["Wq"].dtype)
    for g in range(KVH):
        wall[g, PK] = by_tile(a["Wk"][g * P:(g + 1) * P]).reshape(P, HID)
        wall[g, PV_] = by_tile(a["Wv"][g * P:(g + 1) * P]).reshape(P, HID)
        for h in range(G):
            c = slice((g * G + h) * P, (g * G + h + 1) * P)
            wall[g, PQ + h] = by_tile(a["Wq"][c]).reshape(P, HID)
            wall[g, PO + h] = a["Wo"][:, c].T
        wall[g, PG:PG + KT] = by_tile(a["Wg"][g * GW:(g + 1) * GW]).transpose(1, 0, 2)
    rep = lambda v: np.broadcast_to(v[None, :], (P, v.shape[0]))
    xs = a["hidden_states"].reshape(NB, BLK, P, HID).transpose(0, 2, 1, 3)
    arrays = {
        "x": xs, "cos": cos, "sin": sin, "masks": masks, "wall": wall, "rwt": by_tile(a["router_weight"]), "rb": rep(a["router_bias"]),
        "eb2": np.concatenate([a["expert_bias"]] * 2, 0), "wint": by_tile(a["Win"]), "dtb": rep(a["dt_bias"]),
        "alog": rep(a["A_log_bias"]), "gn": a["gnorm_w"].reshape(P, 1),
    }
    arrays = {f"in_{k}": np.ascontiguousarray(v) for k, v in arrays.items()}
    nc = bacc.Bacc("TRN2", target_bir_lowering=False, num_devices=1)
    aps = [nc.dram_tensor(k, v.shape, mybir.dt.from_np(v.dtype), kind="ExternalInput").ap() for k, v in arrays.items()]
    o = nc.dram_tensor("out", (NB, P, BLK, HID), F32, kind="ExternalOutput").ap()
    build(nc, *aps, o)
    r = run_bass_kernel_spmd(nc, [arrays], core_ids=[0])
    return r.results[0]["out"].transpose(0, 2, 1, 3).reshape(1, L, HID)
```

```python
from contextlib import ExitStack

import numpy as np

import concourse.bass as bass
from concourse import mybir

F32 = mybir.dt.float32
BF16 = mybir.dt.bfloat16
ALU = mybir.AluOpType
ACT = mybir.ActivationFunctionType
AX = mybir.AxisListType

P = 128
HID = 512
KT = HID // P
H, KVH = 32, 8
G = H // KVH
L = 2048
NCH = L // P
BLK = 4
TB = BLK * P
NB = L // TB
NE = 64
TOPK = 8
EPS = 1e-5
GW = G * P
NPIECE = 2 + 3 * G
PK, PQ, PV_, PG, PO = 0, 1, 1 + G, 2 + G, 2 + 2 * G
NFILL = 2 + 2 * G
BIGNEG = -30000.0

FILLS = {0: {"A": 0, "B": 1, "C": 2}, 1: {"A": 3, "B": 4, "C": 5}, 2: {"A": 6, "B": 7}, 3: {"A": 8, "C": 9}}
MID = {10: (2,), 11: (4,), 12: (6,), 13: (8, 9)}
END = {9: (0, 1), 10: (3,), 11: (5,), 12: (7,)}
FIRST = len(FILLS[0])


def steps(last):
    return range(1, NCH if last else NCH + 1)


def filled(n, last):
    return {} if last and n // BLK == NB - 1 else FILLS[n % BLK]


def ring_order(last):
    seq = []
    for n in steps(last):
        f = filled(n, last)
        seq += [("F", n // BLK, f[x]) for x in "ABC" if x in f] + [("W", n - 1)]
    if last:
        seq.append(("W", NCH - 1))
    order = {u: r for r, u in enumerate(seq)}
    order[("W", -1)] = -1
    return order


def turn_order(last):
    seq = []
    for n in steps(last):
        seq.append(("Z", n - 1))
        if n % BLK == 1 and filled(n, last):
            seq.append(("K", n // BLK))
    if last:
        seq.append(("Z", NCH - 1))
    return {u: r for r, u in enumerate(seq)}


def cs_event(n):
    return n - (n + 1) // NCH


def in_event(n):
    return n - n // NCH - 1


def build(nc, x, cos, sin, masks, wall, rwt, rb, eb2, wint, dtb, alog, gn, out):
    with ExitStack() as ctx:
        def sb(name, shape, dt=F32):
            return ctx.enter_context(nc.sbuf_tensor(name, shape, dt))

        class Sem:

            def __init__(self, name, per=0, before=0, free=0):
                self.sem = ctx.enter_context(nc.semaphore(name))
                self.per, self.base, self.free = per, before + free, free

            def at(self, g, idx):
                assert self.base + idx >= 0 or (isinstance(g, int) and g * self.per + self.base + idx >= 0), "waits are above zero"
                return g * self.per + (self.base + idx + 1)

        ACC = sb("ACC", [P, NCH, HID])
        XTH = sb("XTH", [P, KT, L], BF16)
        XTL = sb("XTL", [P, KT, L], BF16)
        COS = sb("COS", [P, L])
        SIN = sb("SIN", [P, L])
        WH = sb("WH", [P, NPIECE, HID], BF16)
        WL = sb("WL", [P, NPIECE, HID], BF16)
        STAGE = sb("STAGE", [P, 2, HID])
        STAGEO = sb("STAGEO", [P, 2, HID])
        EG = sb("EG", [P, KVH, NCH, G])
        WJ = sb("WJ", [P, KVH, NCH, G])
        DT = sb("DT", [P, KVH, NCH, G])
        DCH = sb("DCH", [P, KVH, NCH, G])
        GH = sb("GH", [P, KVH, NCH, G], BF16)
        GL = sb("GL", [P, KVH, NCH, G], BF16)
        IDF = sb("IDF", [P, P])
        MB = sb("MB", [P, 3, P], BF16)
        NEGM = sb("NEGM", [P, GW], BF16)
        HALF = sb("HALF", [P, G])
        EPSC = sb("EPSC", [P, G])
        GNH = sb("GNH", [P, 1])
        RWT = sb("RWT", [P, KT, NE])
        RB = sb("RB", [P, NE])
        EBH = sb("EBH", [P, HID], BF16)
        EBL = sb("EBL", [P, HID], BF16)

        BANK = [ctx.enter_context(nc.psum_tensor(f"B{i}", [P, 512], F32)) for i in range(8)]
        RING = BANK[0:2]
        B_S, B_D, B_PV, B_IN, B_CS, B_T = BANK[2:8]

        ffn = ExitStack()

        def fb(name, shape, dt=F32):
            return ffn.enter_context(nc.sbuf_tensor(name, shape, dt))

        def head(st, name, shape, dt=F32):
            return st.enter_context(nc.sbuf_tensor(name, shape, dt))

        def ffn_memory():
            m = {}
            for name, shape, dt in (
                    ("XN", [P, BLK, HID], F32), ("XNT", [P, BLK, HID], F32), ("BS", [P, BLK, 6], F32), ("MV", [P, BLK, 2], F32),
                    ("VE", [P, BLK], F32), ("RSTD", [P, BLK], F32), ("LG", [P, BLK, NE], F32), ("MX", [P, BLK, TOPK], F32),
                    ("MR", [P, BLK, NE], F32), ("NM", [P, BLK], F32), ("EX", [P, BLK, NE], F32), ("SUM", [P, BLK], F32),
                    ("MK", [P, BLK, NE], F32), ("WU", [P, BLK, NE], F32), ("S8", [P, BLK], F32), ("RC", [P, BLK], F32),
                    ("HRC", [P, BLK], F32), ("WS", [P, BLK], F32), ("WN", [P, BLK, NE], F32), ("WHL", [P, BLK, 2 * NE], BF16),
                    ("WT", [P, BLK, P], BF16), ("WINF", [P, KT, H], F32), ("WINH", [P, KT, H], BF16), ("WINL", [P, KT, H], BF16),
                    ("DTB", [P, H], F32), ("ALOG", [P, H], F32), ("EBF", [P, HID], F32), ("NEGF", [P, GW], F32),
                    ("GN", [P, 1], F32), ("SP", [P, 6, NCH * H], F32), ("MASKS", [P, 3, P], F32), ("ONES", [P, P], F32)):
                m[name] = head(ffn, name, shape, dt)
            return m

        m = ffn_memory()
        XN, XNT, BS, MV, VE, RSTD, LG, MX, MR, NM, EX, SUM, MK, WU, S8, RC, HRC, WS, WN, WHL, WT = (m[k] for k in (
            "XN XNT BS MV VE RSTD LG MX MR NM EX SUM MK WU S8 RC HRC WS WN WHL WT".split()))
        WINF, WINH, WINL, DTB, ALOG, EBF, NEGF, GN, SP, MASKS, ONES = (
            m[k] for k in "WINF WINH WINL DTB ALOG EBF NEGF GN SP MASKS ONES".split())
        ffn.close()

        QH = sb("QH", [P, 2, G, TB], BF16)
        QL = sb("QL", [P, 2, G, TB], BF16)
        KH = sb("KH", [P, 2, TB], BF16)
        KL = sb("KL", [P, 2, TB], BF16)
        KDH = sb("KDH", [P, 2, TB], BF16)
        KDL = sb("KDL", [P, 2, TB], BF16)
        VF = sb("VF", [P, 2, TB])
        VH = sb("VH", [P, 2, TB], BF16)
        VL = sb("VL", [P, 2, TB], BF16)
        G2 = sb("G2", [P, BLK + 1, GW])
        QS = sb("QS", [P, 2, TB])
        QF = sb("QF", [P, 2, TB])
        KF = sb("KF", [P, TB])
        TH = sb("TH", [P, GW])
        MH = sb("MH", [P, G, P], BF16)
        ML = sb("ML", [P, G, P], BF16)
        PF = sb("PF", [P, GW])
        PH = sb("PH", [P, 2, GW], BF16)
        PL = sb("PL", [P, 2, GW], BF16)
        WVF = sb("WVF", [P, G, P])
        WVH = sb("WVH", [P, GW], BF16)
        WVL = sb("WVL", [P, GW], BF16)
        YF = sb("YF", [P, GW])
        SQ = sb("SQ", [P, G, P])
        SS = sb("SS", [P, G])
        RM = sb("RM", [P, G])
        RR = sb("RR", [P, G])
        ZTH = sb("ZTH", [P, GW], BF16)
        ZTL = sb("ZTL", [P, GW], BF16)
        ST = sb("ST", [P, GW])
        STH = sb("STH", [P, GW], BF16)
        STL = sb("STL", [P, GW], BF16)

        LTF, TRIF = MASKS[:, 0, :], MASKS[:, 1, :]
        LTB, TRIB, IDB = MB[:, 0, :], MB[:, 1, :], MB[:, 2, :]

        n_ring, n_turn = len(ring_order(False)) - 1, len(turn_order(False))
        ring_full = Sem("ring_full", n_ring, NFILL + FIRST)
        ring_free = Sem("ring_free", n_ring, NFILL + FIRST, free=2)
        turn_free = Sem("turn_free", n_turn, 1, free=1)
        scores_full = Sem("scores_full", NCH)
        logdecay_full = Sem("logdecay_full", NCH, free=1)
        inter_full = Sem("inter_full", NCH - 1, free=5)
        intra_full = Sem("intra_full", NCH, free=5)
        cs_full = Sem("cs_full", NCH - 1, free=4)
        zt_full = Sem("zt_full", NCH, free=1)
        kt_full = Sem("kt_full", NB, free=1)
        swap_ready = Sem("swap_ready", NB * 5)
        qh_ready = Sem("qh_ready", NB * 5, free=2)
        v_ready = Sem("v_ready", NB)
        tanh_ready = Sem("tanh_ready", NCH)
        decay_ready = Sem("decay_ready", NCH, free=1)
        ph_ready = Sem("ph_ready", NCH, free=1)
        wvh_ready = Sem("wvh_ready", NCH - 1, free=1)
        sth_ready = Sem("sth_ready", NCH - 1, free=1)
        sq_ready = Sem("sq_ready", NCH, free=1)
        zth_ready = Sem("zth_ready", NCH)
        kdh_ready = Sem("kdh_ready", NB)
        qf_ready = Sem("qf_ready", NB * 5, free=1)
        p_ready = Sem("p_ready", NCH, free=1)
        inter_read = Sem("inter_read", NCH - 1, free=1)
        y_ready = Sem("y_ready", NCH, free=1)
        ss_ready = Sem("ss_ready", NCH, free=1)
        z_ready = Sem("z_ready", NCH, free=5)
        st_ready = Sem("st_ready", NCH - 1, free=1)
        stl_ready = Sem("stl_ready", NCH - 1, free=1)
        sin_ready = Sem("sin_ready", NB * 5)
        ql_ready = Sem("ql_ready", NB * 5, free=2)
        m_ready = Sem("m_ready", NCH)
        wvf_ready = Sem("wvf_ready", NCH - 1, free=4)
        wvl_ready = Sem("wvl_ready", NCH - 1, free=1)
        pl_ready = Sem("pl_ready", NCH, free=1)
        rm_ready = Sem("rm_ready", NCH, free=1)
        rr_ready = Sem("rr_ready", NCH)
        wh_ready, wl_ready = Sem("wh_ready", PO), Sem("wl_ready", PO, free=2)
        woh_ready, wol_ready = Sem("woh_ready", G), Sem("wol_ready", G, free=2)
        w_landed = [Sem(f"w_landed{i}") for i in range(2)]
        wo_landed = [Sem(f"wo_landed{i}") for i in range(2)]

        f_bs, f_mv, f_ve, f_rstd, f_xn = (Sem(n, 2) for n in ("f_bs", "f_mv", "f_ve", "f_rstd", "f_xn"))
        f_tp, f_xnt, f_lg, f_mx, f_mr, f_nm, f_ex = (Sem(n, k) for n, k in (
            ("f_tp", 4), ("f_xnt", 4), ("f_lg", 1), ("f_mx", 1), ("f_mr", 1), ("f_nm", 1), ("f_ex", 1)))
        f_gate = Sem("f_gate", 9)
        f_l = Sem("f_l", 1, free=1)
        f_wt, f_wtc, f_mix, f_ax, f_acc = (Sem(n, k) for n, k in (
            ("f_wt", 1), ("f_wtc", 1), ("f_mix", 4), ("f_ax", 4), ("f_acc", 4)))
        f_tp2, f_xth, f_dt = (Sem(n, 4) for n in ("f_tp2", "f_xth", "f_dt"))
        f_xtl = Sem("f_xtl", 4, free=4)
        x_landed = [Sem(f"x_landed{i}") for i in range(NB)]
        c_landed = Sem("c_landed")
        rope_landed = Sem("rope_landed")
        out_sent = Sem("out_sent")
        const_pool, const_dve, const_act = Sem("const_pool"), Sem("const_dve"), Sem("const_act")
        prep_dve, prep_act, prep_pe, prep_abs = Sem("prep_dve"), Sem("prep_act"), Sem("prep_pe"), Sem("prep_abs")
        prep_chain = Sem("prep_chain")
        attn_done = Sem("attn_done")

        block = ctx.enter_context(nc.Block())

        def mm3(out_, ah, al, bh, bl, first, last):
            nc.tensor.matmul(out_, ah, bh, start=first, stop=False)
            nc.tensor.matmul(out_, ah, bl, start=False, stop=False)
            return nc.tensor.matmul(out_, al, bh, start=False, stop=last)

        def bank(use):
            return RING[(use + NFILL + FIRST) % 2]

        def v_use(b):
            return ring_order(False)[("F", b - 1, PV_)] if b else PV_ - NFILL - FIRST

        def gate_use(b):
            return ring_order(False)[("F", b - 1, NFILL - 1)] if b else -1 - FIRST

        def k_use(b):
            return turn_order(False)[("K", b - 1)] if b else -1

        @block.sync
        def _(sp):
            for k in range(NB):
                sp.dma_start(ACC[:, k * BLK:(k + 1) * BLK, :], x[k]).then_inc(x_landed[k].sem, 16)
                if k == 0:
                    for dst, src in ((MASKS[:, :, :], masks[:, 0:3 * P]), (IDF[:, :], masks[:, 2 * P:3 * P]), (NEGF[:, :], masks[:, 3 * P:]), (RWT[:, :, :], rwt),
                                     (RB[:, :], rb), (EBF[:, :], eb2), (WINF[:, :, :], wint), (DTB[:, :], dtb),
                                     (ALOG[:, :], alog), (GN[:, :], gn)):
                        sp.dma_start(dst, src).then_inc(c_landed.sem, 16)
            sp.dma_start(COS[:, :], cos).then_inc(rope_landed.sem, 16)
            sp.dma_start(SIN[:, :], sin).then_inc(rope_landed.sem, 16)

            def load_weights(g):
                for i in range(NPIECE):
                    stage, landed, free, k = (STAGE, w_landed, wl_ready, i) if i < PO else (STAGEO, wo_landed, wol_ready, i - PO)
                    sp.wait_ge(free.sem, free.at(g, k - 2))
                    sp.dma_start(stage[:, k % 2, :], wall[g, i] if isinstance(g, int)
                                     else wall[bass.ds(g, 1), i].rearrange("a p n -> (a p) n")).then_inc(landed[k % 2].sem, 16)
            load_weights(0)
            with sp.Fori(1, KVH) as g:
                load_weights(g)
            for k in range(NB):
                sp.wait_ge(f_acc.sem, f_acc.at(NB + k, 3))
                sp.dma_start(out[k], ACC[:, k * BLK:(k + 1) * BLK, :]).then_inc(out_sent.sem, 16)
            sp.wait_ge(out_sent.sem, 16 * NB)

        def ffn_dve(dve, blk, f, first):
            A = ACC[:, blk * BLK:(blk + 1) * BLK, :]

            def stats(k):
                for i in range(BLK):
                    ins = nc.vector.bn_stats(BS[:, i, :], A[:, i, :])
                ins.then_inc(f_bs.sem, 1)
                dve.wait_ge(f_bs.sem, f_bs.at(f, k))
                for i in range(BLK):
                    ins = nc.vector.bn_aggr(MV[:, i, :], BS[:, i, :])
                ins.then_inc(f_mv.sem, 1)

            def normalise(k):
                dve.wait_ge(f_rstd.sem, f_rstd.at(f, k))
                for i in range(BLK):
                    ins = nc.vector.tensor_scalar(XN[:, i, :], A[:, i, :], MV[:, i, 0:1], RSTD[:, i:i + 1],
                                                  ALU.subtract, ALU.mult)
                ins.then_inc(f_xn.sem, 1)
            once = 0 if first else NB - f
            stats(once)
            normalise(once)
            dve.wait_ge(f_lg.sem, f_lg.at(f, 0))
            nc.vector.tensor_tensor(LG[:, :, :], BANK[4][:, 0:BLK * NE].rearrange("p (b e) -> p b e", b=BLK),
                                        RB[:, None, :].broadcast_to([P, BLK, NE]), ALU.add).then_inc(f_l.sem, 1)
            dve.wait_ge(f_l.sem, f_l.at(f, 0))
            for i in range(BLK):
                ins = nc.vector.max(MX[:, i, :], LG[:, i, :])
            ins.then_inc(f_mx.sem, 1)
            dve.wait_ge(f_mx.sem, f_mx.at(f, 0))
            nc.vector.tensor_scalar(NM[:, :], MX[:, :, 0], -1.0, None, ALU.mult).then_inc(f_nm.sem, 1)
            for i in range(BLK):
                ins = nc.vector.match_replace(MR[:, i, :], MX[:, i, :], LG[:, i, :], -3.0e38)
            ins.then_inc(f_mr.sem, 1)
            dve.wait_ge(f_mr.sem, f_mr.at(f, 0))
            step = [0]

            def chain(ins):
                ins.then_inc(f_gate.sem, 1)
                dve.wait_ge(f_gate.sem, f_gate.at(f, step[0]))
                step[0] += 1
            chain(nc.vector.tensor_tensor(MK[:, :, :], LG[:, :, :], MR[:, :, :], ALU.not_equal))
            dve.wait_ge(f_ex.sem, f_ex.at(f, 0))
            chain(nc.vector.tensor_reduce(SUM[:, :], EX[:, :, :], AX.X, ALU.add))
            chain(nc.vector.tensor_tensor(WU[:, :, :], MK[:, :, :], EX[:, :, :], ALU.mult))
            chain(nc.vector.tensor_reduce(S8[:, :], WU[:, :, :], AX.X, ALU.add))
            chain(nc.vector.reciprocal(RC[:, :], SUM[:, :]))
            chain(nc.vector.tensor_scalar(HRC[:, :], RC[:, :], 0.5, None, ALU.mult))
            nc.vector.tensor_tensor(WS[:, :], S8[:, :], HRC[:, :], ALU.mult)
            chain(nc.vector.tensor_tensor(WN[:, :, :], WU[:, :, :], HRC[:, :, None].broadcast_to([P, BLK, NE]), ALU.mult))
            chain(nc.vector.tensor_copy(WHL[:, :, 0:NE], WN[:, :, :]))
            nc.vector.tensor_tensor(WHL[:, :, NE:2 * NE], WN[:, :, :], WHL[:, :, 0:NE], ALU.subtract).then_inc(f_gate.sem, 1)
            for i in range(BLK):
                nc.vector.scalar_tensor_tensor(A[:, i, :], XN[:, i, :], WS[:, i:i + 1], A[:, i, :],
                                                   ALU.mult, ALU.add).then_inc(f_ax.sem, 1)
            for i in range(BLK):
                dve.wait_ge(f_ax.sem, f_ax.at(f, i))
                dve.wait_ge(f_mix.sem, f_mix.at(f, i))
                nc.vector.tensor_tensor(A[:, i, :], A[:, i, :], BANK[i][:, :], ALU.add).then_inc(f_acc.sem, 1)
            if first:
                dve.wait_ge(f_acc.sem, f_acc.at(f, 3))
                stats(1)
                dve.wait_ge(f_ax.sem, f_ax.at(f, 3))
                normalise(1)
                for i in range(BLK):
                    dve.wait_ge(f_xth.sem, f_xth.at(f, i))
                    tok = blk * TB + i * P
                    nc.vector.tensor_tensor(XTL[:, :, tok:tok + P], BANK[i][:, :].rearrange("p (k t) -> p k t", k=KT),
                                                XTH[:, :, tok:tok + P], ALU.subtract).then_inc(f_xtl.sem, 1)

        def ffn_pool(pool, f, first):
            for k in (0, 1) if first else (NB - f,):
                pool.wait_ge(f_mv.sem, f_mv.at(f, k))
                nc.gpsimd.tensor_tensor(VE[:, :], MV[:, :, 1], EPSC[:, :], ALU.add).then_inc(f_ve.sem, 1)
                pool.wait_ge(f_ve.sem, f_ve.at(f, k))
                nc.gpsimd.tensor_tensor(RSTD[:, :], VE[:, :], HALF[:, 0:BLK], ALU.pow).then_inc(f_rstd.sem, 1)

        def ffn_pe(pe, blk, f, first, prev_first):
            pe.wait_ge(f_xn.sem, f_xn.at(f, 0 if first else NB - f))
            for i in range(BLK):
                if prev_first:
                    pe.wait_ge(f_xtl.sem, f_xtl.at(f, i - 4))
                else:
                    pe.wait_ge(f_acc.sem, f_acc.at(f, i - 4))
                for k in range(KT):
                    ins = nc.tensor.transpose(BANK[i][:, k * P:(k + 1) * P], XN[:, i, k * P:(k + 1) * P], IDF[:, :])
                ins.then_inc(f_tp.sem, 1)
            pe.wait_ge(f_l.sem, f_l.at(f, -1))
            for i in range(BLK):
                pe.wait_ge(f_xnt.sem, f_xnt.at(f, i))
                for k in range(KT):
                    ins = nc.tensor.matmul(BANK[4][:, i * NE:(i + 1) * NE], XNT[:, i, k * P:(k + 1) * P], RWT[:, k, :],
                                           start=(k == 0), stop=(k == KT - 1))
            ins.then_inc(f_lg.sem, 1)
            pe.wait_ge(f_gate.sem, f_gate.at(f, 8))
            WTP = BANK[5][:, 0:256].bitcast(BF16)
            for i in range(BLK):
                ins = nc.tensor.transpose(WTP[:, i * P:(i + 1) * P], WHL[:, i, :], IDB)
            ins.then_inc(f_wt.sem, 1)
            pe.wait_ge(f_wtc.sem, f_wtc.at(f, 0))
            for i in range(BLK):
                nc.tensor.matmul(BANK[i][:, :], WT[:, i, :], EBH[:, :], start=True, stop=False)
                nc.tensor.matmul(BANK[i][:, :], WT[:, i, :], EBL[:, :], start=False, stop=True).then_inc(f_mix.sem, 1)
            if first:
                pe.wait_ge(f_xn.sem, f_xn.at(f, 1))
                for i in range(BLK):
                    pe.wait_ge(f_acc.sem, f_acc.at(f, i))
                    for k in range(KT):
                        ins = nc.tensor.transpose(BANK[i][:, k * P:(k + 1) * P], XN[:, i, k * P:(k + 1) * P], IDF[:, :])
                    ins.then_inc(f_tp2.sem, 1)
                for i in range(BLK):
                    pe.wait_ge(f_xtl.sem, f_xtl.at(f, i))
                    tok = blk * TB + i * P
                    for k in range(KT):
                        ins = mm3(BANK[6][:, (blk * BLK + i) * H:(blk * BLK + i + 1) * H],
                                  XTH[:, k, tok:tok + P], XTL[:, k, tok:tok + P], WINH[:, k, :], WINL[:, k, :],
                                  k == 0, k == KT - 1)
                    ins.then_inc(f_dt.sem, 1)

        def ffn_act(act, blk, f, first):
            for i in range(BLK):
                act.wait_ge(f_tp.sem, f_tp.at(f, i))
                nc.scalar.activation(XNT[:, i, :], BANK[i][:, :], ACT.Copy).then_inc(f_xnt.sem, 1)
            act.wait_ge(f_nm.sem, f_nm.at(f, 0))
            act.wait_ge(f_l.sem, f_l.at(f, 0))
            for i in range(BLK):
                ins = nc.scalar.activation(EX[:, i, :], LG[:, i, :], ACT.Exp, bias=NM[:, i:i + 1])
            ins.then_inc(f_ex.sem, 1)
            act.wait_ge(f_wt.sem, f_wt.at(f, 0))
            nc.scalar.activation(WT[:, :, :], BANK[5][:, 0:256].bitcast(BF16).rearrange("p (b t) -> p b t", b=BLK),
                                     ACT.Copy).then_inc(f_wtc.sem, 1)
            if first:
                for i in range(BLK):
                    act.wait_ge(f_tp2.sem, f_tp2.at(f, i))
                    nc.scalar.activation(XTH[:, :, blk * TB + i * P:blk * TB + (i + 1) * P],
                                             BANK[i][:, :].rearrange("p (k t) -> p k t", k=KT), ACT.Copy).then_inc(f_xth.sem, 1)

        @block.tensor
        def _(pe):
            for signal in (cs_full, inter_full, intra_full, kt_full, logdecay_full, zt_full):
                pe.sem_inc(signal.sem, signal.free)
            pe.wait_ge(const_dve.sem, 7)
            pe.wait_ge(const_act.sem, 2)
            for k in range(NB):
                ffn_pe(pe, k, k, True, True)
            pe.wait_ge(prep_dve.sem, 1)
            for j, lhs in enumerate((TRIF, LTF, ONES[:, :])):
                nc.tensor.matmul(BANK[2 + j][:, :], lhs, SP[:, 5, :], start=True, stop=True).then_inc(prep_pe.sem, 1)

            def wkt(piece, k):
                return WH[:, piece, k * P:(k + 1) * P], WL[:, piece, k * P:(k + 1) * P]

            def fill(g, b, item, use, fresh, gw):
                out_bank = bank(use)
                pe.wait_ge(ring_free.sem, ring_free.at(g, use - 2))
                t0 = b % NB * TB
                if fresh:
                    piece = item if item <= PV_ else PG + KT - 1
                    pe.wait_ge(wh_ready.sem, wh_ready.at(gw, piece))
                    pe.wait_ge(wl_ready.sem, wl_ready.at(gw, piece))
                if item < PV_:
                    for k in range(KT):
                        wh, wl = wkt(item, k)
                        ins = mm3(out_bank[:, :], wh, wl, XTH[:, k, t0:t0 + TB], XTL[:, k, t0:t0 + TB], k == 0, k == KT - 1)
                elif item == PV_:
                    for s in range(BLK):
                        for k in range(KT):
                            t = t0 + s * P
                            wh, wl = wkt(item, k)
                            ins = mm3(out_bank[:, s * P:(s + 1) * P], XTH[:, k, t:t + P], XTL[:, k, t:t + P], wh, wl,
                                      k == 0, k == KT - 1)
                else:
                    t = t0 + (item - PG) * P
                    for k in range(KT):
                        ins = mm3(out_bank[:, :], XTH[:, k, t:t + P], XTL[:, k, t:t + P], WH[:, PG + k, :], WL[:, PG + k, :],
                                  k == 0, k == KT - 1)
                ins.then_inc(ring_full.sem, 1)

            def turn_keys(g, b, use):
                pe.wait_ge(turn_free.sem, turn_free.at(g, use - 1))
                pe.wait_ge(qf_ready.sem, qf_ready.at(g, 5 * b))
                for s in range(BLK):
                    ins = nc.tensor.transpose(B_T[:, s * P:(s + 1) * P], KF[:, s * P:(s + 1) * P], IDF[:, :])
                ins.then_inc(kt_full.sem, 1)

            def scores(g, n):
                b, s = divmod(n, BLK)
                par, t = b % 2, s * P
                if s == 0:
                    pe.wait_ge(qh_ready.sem, qh_ready.at(g, 5 * b + 4))
                    pe.wait_ge(ql_ready.sem, ql_ready.at(g, 5 * b + 4))
                pe.wait_ge(p_ready.sem, p_ready.at(g, n - 1))
                mm3(B_S[:, :], KH[:, par, t:t + P], KL[:, par, t:t + P], QH[:, par, :, t:t + P], QL[:, par, :, t:t + P],
                        True, True).then_inc(scores_full.sem, 1)
                pe.wait_ge(m_ready.sem, m_ready.at(g, n))
                pe.wait_ge(decay_ready.sem, decay_ready.at(g, n - 1))
                nc.tensor.matmul(B_D[:, :], IDB, NEGM[:, :], start=True, stop=False)
                nc.tensor.matmul(B_D[:, :], LTB, MH[:, :, :], start=False, stop=False)
                nc.tensor.matmul(B_D[:, :], LTB, ML[:, :, :], start=False, stop=True).then_inc(logdecay_full.sem, 1)

            def attend(g, n):
                b, s = divmod(n, BLK)
                par, t = b % 2, s * P
                if n % NCH:
                    pe.wait_ge(inter_read.sem, inter_read.at(g, in_event(n - 1)))
                    pe.wait_ge(sth_ready.sem, sth_ready.at(g, cs_event(n - 1)))
                    pe.wait_ge(stl_ready.sem, stl_ready.at(g, cs_event(n - 1)))
                    for h in range(G):
                        c = slice(h * P, (h + 1) * P)
                        ins = mm3(B_IN[:, c], QH[:, par, h, t:t + P], QL[:, par, h, t:t + P], STH[:, c], STL[:, c], True, True)
                    ins.then_inc(inter_full.sem, 1)
                pe.wait_ge(y_ready.sem, y_ready.at(g, n - 1))
                pe.wait_ge(ph_ready.sem, ph_ready.at(g, n))
                pe.wait_ge(pl_ready.sem, pl_ready.at(g, n))
                if s == 0:
                    pe.wait_ge(v_ready.sem, v_ready.at(g, b))
                    pe.wait_ge(ring_free.sem, ring_free.at(g, v_use(b)))
                for h in range(G):
                    c = slice(h * P, (h + 1) * P)
                    ins = mm3(B_PV[:, c], PH[:, n % 2, c], PL[:, n % 2, c], VH[:, par, t:t + P], VL[:, par, t:t + P], True, True)
                ins.then_inc(intra_full.sem, 1)
                if n % NCH == NCH - 1:
                    return
                pe.wait_ge(st_ready.sem, st_ready.at(g, cs_event(n - 1)))
                pe.wait_ge(wvh_ready.sem, wvh_ready.at(g, cs_event(n)))
                pe.wait_ge(wvl_ready.sem, wvl_ready.at(g, cs_event(n)))
                if s == 0:
                    pe.wait_ge(kdh_ready.sem, kdh_ready.at(g, b))
                    pe.wait_ge(turn_free.sem, turn_free.at(g, k_use(b)))
                mm3(B_CS[:, :], KDH[:, par, t:t + P], KDL[:, par, t:t + P], WVH[:, :], WVL[:, :], True, True).then_inc(cs_full.sem, 1)

            def turn_z(g, n, use):
                pe.wait_ge(turn_free.sem, turn_free.at(g, use - 1))
                pe.wait_ge(z_ready.sem, z_ready.at(g, n))
                for h in range(G):
                    ins = nc.tensor.transpose(B_T[:, h * P:(h + 1) * P], YF[:, h * P:(h + 1) * P], IDF[:, :])
                ins.then_inc(zt_full.sem, 1)

            def project_out(g, n, use, turn_use):
                pe.wait_ge(ring_free.sem, ring_free.at(g, use - 2))
                pe.wait_ge(zth_ready.sem, zth_ready.at(g, n))
                pe.wait_ge(turn_free.sem, turn_free.at(g, turn_use))
                if n % NCH == 0:
                    pe.wait_ge(woh_ready.sem, woh_ready.at(g, n // NCH * G + G - 1))
                    pe.wait_ge(wol_ready.sem, wol_ready.at(g, n // NCH * G + G - 1))
                for h in range(G):
                    c = slice(h * P, (h + 1) * P)
                    ins = mm3(bank(use)[:, :], ZTH[:, c], ZTL[:, c], WH[:, PO + h, :], WL[:, PO + h, :], h == 0, h == G - 1)
                ins.then_inc(ring_full.sem, 1)

            for item in range(NFILL):
                fill(0, 0, item, item - NFILL - FIRST, True, 0)
            turn_keys(0, 0, -1)
            scores(0, 0)

            def step(g, n, last, first=False):
                b, s = divmod(n, BLK)
                ring, turn = ring_order(last), turn_order(last)

                def slot(x):
                    if x in filled(n, last):
                        item = filled(n, last)[x]
                        fill(g, b + 1, item, item - FIRST if first else ring[("F", b, item)], b == NB - 1, g + 1)
                if not (last and n == NCH - 1):
                    scores(g, n + 1)
                slot("A")
                if not first:
                    turn_z(g, n - 1, turn[("Z", n - 1)])
                attend(g, n)
                slot("B")
                slot("C")
                if s == 1 and filled(n, last):
                    turn_keys(g, b + 1, turn[("K", b)])
                if not first:
                    project_out(g, n - 1, ring[("W", n - 1)], turn[("Z", n - 1)])

            step(0, 0, False, True)
            with pe.Fori(0, KVH - 1) as g:
                for n in steps(False):
                    step(g, n, False)
            for n in steps(True):
                step(KVH - 1, n, True)
            turn_z(KVH - 1, NCH - 1, turn_order(True)[("Z", NCH - 1)])
            project_out(KVH - 1, NCH - 1, ring_order(True)[("W", NCH - 1)], turn_order(True)[("Z", NCH - 1)])
            pe.wait_ge(attn_done.sem, 1)
            for k in range(NB):
                ffn_pe(pe, k, k + NB, False, k == 0)

        @block.scalar
        def _(act):
            for signal in (decay_ready, ph_ready, qh_ready, sq_ready, sth_ready, wvh_ready):
                act.sem_inc(signal.sem, signal.free)
            act.wait_ge(c_landed.sem, 16 * 10)
            nc.scalar.activation(EBH[:, :], EBF[:, :], ACT.Copy).then_inc(const_act.sem, 1)
            nc.scalar.activation(WINH[:, :, :], WINF[:, :, :], ACT.Copy).then_inc(const_act.sem, 1)
            for k in range(NB):
                ffn_act(act, k, k, True)
            act.wait_ge(prep_abs.sem, 1)
            nc.scalar.activation(SP[:, 2, :], SP[:, 1, :], ACT.Exp, scale=-1.0).then_inc(prep_act.sem, 1)
            nc.scalar.activation(ALOG[:, :], ALOG[:, :], ACT.Exp).then_inc(prep_act.sem, 1)

            def split_hi(g, i):
                if i < PO:
                    act.wait_ge(w_landed[i % 2].sem, g * (PO // 2 * 16) + (i // 2 + 1) * 16)
                    nc.scalar.activation(WH[:, i, :], STAGE[:, i % 2, :], ACT.Copy).then_inc(wh_ready.sem, 1)
                else:
                    k = i - PO
                    act.wait_ge(wo_landed[k % 2].sem, g * (G // 2 * 16) + (k // 2 + 1) * 16)
                    nc.scalar.activation(WH[:, i, :], STAGEO[:, k % 2, :], ACT.Copy, scale=GNH[:, 0:1]).then_inc(woh_ready.sem, 1)

            def last_use(g, i):
                order = ring_order(False)
                act.wait_ge(ring_full.sem, ring_full.at(g, order[("F", NB - 2, i if i <= PV_ else NFILL - 1)]))

            def swap(g, b, j, use):
                sl = (j + 1) % 2
                act.wait_ge(ring_full.sem, ring_full.at(g, use))
                act.wait_ge(qf_ready.sem, qf_ready.at(g, 5 * b + j - (2 if j else 1)))
                nc.scalar.activation(QS[0:64, sl, :], bank(use)[64:128, :], ACT.Copy)
                nc.scalar.activation(QS[64:128, sl, :], bank(use)[0:64, :], ACT.Copy).then_inc(swap_ready.sem, 1)

            def hi(g, b, j):
                act.wait_ge(qf_ready.sem, qf_ready.at(g, 5 * b + j))
                act.wait_ge(inter_full.sem, inter_full.at(g, in_event(4 * (b - 1) - 1)))
                if j:
                    ins = nc.scalar.activation(QH[:, b % 2, j - 1, :], QF[:, (j - 1) % 2, :], ACT.Copy)
                else:
                    ins = nc.scalar.activation(KH[:, b % 2, :], KF[:, :], ACT.Copy)
                ins.then_inc(qh_ready.sem, 1)

            def values(g, b, use):
                act.wait_ge(ring_full.sem, ring_full.at(g, use))
                act.wait_ge(intra_full.sem, intra_full.at(g, 4 * (b - 1) - 1))
                act.wait_ge(wvf_ready.sem, wvf_ready.at(g, cs_event(4 * (b - 1) - 1)))
                nc.scalar.activation(VF[:, b % 2, :], bank(use)[:, :], ACT.Copy)
                nc.scalar.activation(VH[:, b % 2, :], bank(use)[:, :], ACT.Copy).then_inc(v_ready.sem, 1)

            def gate(g, b, s, use, before):
                act.wait_ge(ring_full.sem, ring_full.at(g, use))
                act.wait_ge(ring_free.sem, ring_free.at(g, before))
                nc.scalar.activation(TH[:, :], bank(use)[:, :], ACT.Tanh, scale=0.5).then_inc(tanh_ready.sem, 1)

            def keys_hi(g, b):
                act.wait_ge(kt_full.sem, kt_full.at(g, b))
                act.wait_ge(cs_full.sem, cs_full.at(g, cs_event(4 * (b - 1) - 1)))
                nc.scalar.activation(KDH[:, b % 2, :], B_T[:, :], ACT.Copy).then_inc(kdh_ready.sem, 1)

            def decay(g, n):
                act.wait_ge(logdecay_full.sem, logdecay_full.at(g, n))
                act.wait_ge(ph_ready.sem, ph_ready.at(g, n - 1))
                act.wait_ge(pl_ready.sem, pl_ready.at(g, n - 1))
                nc.scalar.activation(PF[:, :], B_D[:, :], ACT.Exp).then_inc(decay_ready.sem, 1)

            def p_hi(g, n):
                act.wait_ge(p_ready.sem, p_ready.at(g, n))
                act.wait_ge(intra_full.sem, intra_full.at(g, n - 2))
                nc.scalar.activation(PH[:, n % 2, :], PF[:, :], ACT.Copy).then_inc(ph_ready.sem, 1)

            def wv_hi(g, n):
                if n % NCH == NCH - 1:
                    return
                act.wait_ge(wvf_ready.sem, wvf_ready.at(g, cs_event(n)))
                act.wait_ge(cs_full.sem, cs_full.at(g, cs_event(n - 1)))
                nc.scalar.activation(WVH[:, :], WVF[:, :, :].rearrange("p h e -> p (h e)"), ACT.Copy).then_inc(wvh_ready.sem, 1)

            def state_hi(g, n):
                if n % NCH == NCH - 1:
                    return
                act.wait_ge(st_ready.sem, st_ready.at(g, cs_event(n)))
                act.wait_ge(inter_full.sem, inter_full.at(g, in_event(n)))
                nc.scalar.activation(STH[:, :], ST[:, :], ACT.Copy).then_inc(sth_ready.sem, 1)

            def square(g, n):
                act.wait_ge(y_ready.sem, y_ready.at(g, n))
                act.wait_ge(ss_ready.sem, ss_ready.at(g, n - 1))
                nc.scalar.activation(SQ[:, :, :].rearrange("p h e -> p (h e)"), YF[:, :], ACT.Square,
                                         scale=float(P) ** -0.5).then_inc(sq_ready.sem, 1)

            def zt_hi(g, n, before):
                act.wait_ge(zt_full.sem, zt_full.at(g, n))
                act.wait_ge(ring_full.sem, ring_full.at(g, before))
                nc.scalar.activation(ZTH[:, :], B_T[:, :], ACT.Copy).then_inc(zth_ready.sem, 1)

            for i in range(PO):
                split_hi(0, i)
            for j, dst in enumerate((EG, WJ, DCH)):
                act.wait_ge(prep_pe.sem, j + 1)
                nc.scalar.activation(dst[:, :, :, :].rearrange("p g c h -> p (g c h)"),
                                     BANK[2 + j][:, :], ACT.Exp).then_inc(prep_act.sem, 1)
            for item in range(NFILL):
                use = item - NFILL - FIRST
                if item < PV_:
                    swap(0, 0, item, use)
                if 0 < item <= PV_:
                    hi(0, 0, item - 1)
                if item == PV_:
                    values(0, 0, use)
                elif item > PV_:
                    gate(0, 0, item - PG, use, use - 1)
            keys_hi(0, 0)
            decay(0, 0)
            p_hi(0, 0)
            wv_hi(0, 0)

            def step(g, n, last, first=False):
                b, s = divmod(n, BLK)
                ring = ring_order(last)

                def slot(x, part):
                    if x not in filled(n, last):
                        return
                    item = filled(n, last)[x]
                    use = item - FIRST if first else ring[("F", b, item)]
                    if item < PV_:
                        (swap(g, b + 1, item, use) if part == 0 else hi(g, b + 1, item))
                    elif part == 0 and item == PV_:
                        values(g, b + 1, use)
                    elif part == 0:
                        gate(g, b + 1, item - PG, use, use - 1)

                def next_weights(when):
                    for i in () if last else when.get(n, ()):
                        last_use(g, i)
                        split_hi(g + 1, i)
                nxt = not (last and n == NCH - 1)
                if nxt:
                    decay(g, n + 1)
                if n == 1:
                    act.wait_ge(ring_full.sem, ring_full.at(g, -1))
                    for i in range(PO, PO + 2):
                        split_hi(g, i)
                if nxt:
                    p_hi(g, n + 1)
                slot("A", 0)
                if not first:
                    zt_hi(g, n - 1, ring[("W", n - 2)])
                if nxt:
                    wv_hi(g, n + 1)
                next_weights(MID)
                square(g, n)
                state_hi(g, n)
                slot("B", 0)
                slot("A", 1)
                if n == 1:
                    for i in range(PO + 2, NPIECE):
                        split_hi(g, i)
                slot("C", 0)
                slot("B", 1)
                slot("C", 1)
                if s == 1 and filled(n, last):
                    keys_hi(g, b + 1)
                next_weights(END)

            step(0, 0, False, True)
            with act.Fori(0, KVH - 1) as g:
                for n in steps(False):
                    step(g, n, False)
            for n in steps(True):
                step(KVH - 1, n, True)
            zt_hi(KVH - 1, NCH - 1, ring_order(True)[("W", NCH - 2)])
            act.wait_ge(attn_done.sem, 1)
            for k in range(NB):
                ffn_act(act, k, k + NB, False)

        @block.gpsimd
        def _(pool):
            for signal in (pl_ready, ql_ready, wl_ready, wvf_ready, wvl_ready, rm_ready):
                pool.sem_inc(signal.sem, signal.free)
            nc.gpsimd.memset(HALF[:, :], -0.5).then_inc(const_pool.sem, 1)
            nc.gpsimd.memset(EPSC[:, :], EPS).then_inc(const_pool.sem, 1)
            pool.wait_ge(const_pool.sem, 2)
            for k in range(NB):
                ffn_pool(pool, k, True)

            def split_lo(g, i):
                pool.wait_ge(wh_ready.sem, wh_ready.at(g, i))
                nc.gpsimd.tensor_tensor(WL[:, i, :], STAGE[:, i % 2, :], WH[:, i, :], ALU.subtract).then_inc(wl_ready.sem, 1)

            def times_sin(g, b, j):
                sl = (j + 1) % 2
                pool.wait_ge(swap_ready.sem, swap_ready.at(g, 5 * b + j))
                t0 = b % NB * TB
                nc.gpsimd.tensor_tensor(QS[:, sl, :], QS[:, sl, :], SIN[:, t0:t0 + TB], ALU.mult).then_inc(sin_ready.sem, 1)

            def lo(g, b, j):
                pool.wait_ge(qh_ready.sem, qh_ready.at(g, 5 * b + j))
                if j:
                    ins = nc.gpsimd.tensor_tensor(QL[:, b % 2, j - 1, :], QF[:, (j - 1) % 2, :], QH[:, b % 2, j - 1, :], ALU.subtract)
                else:
                    ins = nc.gpsimd.tensor_tensor(KL[:, b % 2, :], KF[:, :], KH[:, b % 2, :], ALU.subtract)
                ins.then_inc(ql_ready.sem, 1)

            def tab(T, g, n):
                flat = T[:, :, :, :].rearrange("p g c h -> p (g c h)")
                if isinstance(g, int):
                    return flat[:, (g * NCH + n) * G:(g * NCH + n + 1) * G]
                return flat[:, bass.ds(g * (NCH * G) + n * G, G)]

            def masked_g(g, n):
                pool.wait_ge(logdecay_full.sem, logdecay_full.at(g, n - 1))
                tri = TRIB[:, None, :].broadcast_to([P, G, P])
                nc.gpsimd.tensor_tensor(MH[:, :, :], tri, tab(GH, g, n)[:, :, None].broadcast_to([P, G, P]), ALU.mult)
                nc.gpsimd.tensor_tensor(ML[:, :, :], tri, tab(GL, g, n)[:, :, None].broadcast_to([P, G, P]), ALU.mult).then_inc(m_ready.sem, 1)

            def weighted_v(g, n):
                if n % NCH == NCH - 1:
                    return
                b, s = divmod(n, BLK)
                pool.wait_ge(wvh_ready.sem, wvh_ready.at(g, cs_event(n - 1)))
                pool.wait_ge(wvl_ready.sem, wvl_ready.at(g, cs_event(n - 1)))
                if s == 0:
                    pool.wait_ge(v_ready.sem, v_ready.at(g, b))
                nc.gpsimd.tensor_tensor(WVF[:, :, :], VF[:, b % 2, None, s * P:(s + 1) * P].broadcast_to([P, G, P]),
                                            tab(WJ, g, n)[:, :, None].broadcast_to([P, G, P]), ALU.mult).then_inc(wvf_ready.sem, 1)

            def wv_lo(g, n):
                if n % NCH == NCH - 1:
                    return
                pool.wait_ge(wvh_ready.sem, wvh_ready.at(g, cs_event(n)))
                pool.wait_ge(cs_full.sem, cs_full.at(g, cs_event(n - 1)))
                nc.gpsimd.tensor_tensor(WVL[:, :], WVF[:, :, :].rearrange("p h e -> p (h e)"), WVH[:, :], ALU.subtract).then_inc(wvl_ready.sem, 1)

            def p_lo(g, n):
                pool.wait_ge(ph_ready.sem, ph_ready.at(g, n))
                nc.gpsimd.tensor_tensor(PL[:, n % 2, :], PF[:, :], PH[:, n % 2, :], ALU.subtract).then_inc(pl_ready.sem, 1)

            def inv_rms(g, n):
                pool.wait_ge(ss_ready.sem, ss_ready.at(g, n))
                nc.gpsimd.tensor_tensor(RM[:, :], SS[:, :], EPSC[:, :], ALU.add).then_inc(rm_ready.sem, 1)
                pool.wait_ge(rm_ready.sem, rm_ready.at(g, n))
                pool.wait_ge(z_ready.sem, z_ready.at(g, n - 1))
                nc.gpsimd.tensor_tensor(RR[:, :], RM[:, :], HALF[:, :], ALU.pow).then_inc(rr_ready.sem, 1)

            pool.wait_ge(const_dve.sem, 7)
            for i in range(PO):
                split_lo(0, i)
            pool.wait_ge(rope_landed.sem, 32)
            pool.wait_ge(prep_dve.sem, 4)
            masked_g(0, 0)
            for item in range(PV_):
                times_sin(0, 0, item)
                if item:
                    lo(0, 0, item - 1)
            lo(0, 0, PV_ - 1)
            masked_g(0, 1)
            p_lo(0, 0)
            weighted_v(0, 0)
            wv_lo(0, 0)

            def step(g, n, last):
                b, s = divmod(n, BLK)

                def slot(x, part):
                    if filled(n, last).get(x, PV_) < PV_:
                        (times_sin if part == 0 else lo)(g, b + 1, filled(n, last)[x])
                nxt = not (last and n == NCH - 1)
                if not (last and n >= NCH - 2):
                    masked_g(g, n + 2)
                if nxt:
                    p_lo(g, n + 1)
                    weighted_v(g, n + 1)
                slot("A", 0)
                if nxt:
                    wv_lo(g, n + 1)
                for i in () if last else MID.get(n, ()):
                    split_lo(g + 1, i)
                inv_rms(g, n)
                slot("B", 0)
                slot("A", 1)
                slot("C", 0)
                slot("B", 1)
                slot("C", 1)
                for i in () if last else END.get(n, ()):
                    split_lo(g + 1, i)

            step(0, 0, False)
            with pool.Fori(0, KVH - 1) as g:
                for n in steps(False):
                    step(g, n, False)
            for n in steps(True):
                step(KVH - 1, n, True)
            pool.wait_ge(attn_done.sem, 1)
            for f in range(NB, 2 * NB):
                ffn_pool(pool, f, False)

        @block.vector
        def _(dve):
            for signal in (p_ready, qf_ready, ring_free, turn_free, z_ready, wol_ready, f_l,
                           f_xtl, inter_read, y_ready, ss_ready, st_ready, stl_ready):
                dve.sem_inc(signal.sem, signal.free)
            dve.wait_ge(c_landed.sem, 16 * 10)
            nc.vector.tensor_copy(MB[:, :, :], MASKS[:, :, :]).then_inc(const_dve.sem, 1)
            nc.vector.tensor_copy(NEGM[:, :], NEGF[:, :]).then_inc(const_dve.sem, 1)
            nc.vector.memset(ONES[:, :], 1.0).then_inc(const_dve.sem, 1)
            nc.vector.tensor_scalar(GNH[:, :], GN[:, :], 0.5, None, ALU.mult).then_inc(const_dve.sem, 1)
            dve.wait_ge(const_act.sem, 2)
            nc.vector.tensor_tensor(EBL[:, :], EBF[:, :], EBH[:, :], ALU.subtract).then_inc(const_dve.sem, 1)
            nc.vector.tensor_tensor(WINL[:, :, :], WINF[:, :, :], WINH[:, :, :], ALU.subtract).then_inc(const_dve.sem, 2)
            for k in range(NB):
                dve.wait_ge(x_landed[k].sem, 16)
                ffn_dve(dve, k, k, True)

            dve.wait_ge(f_dt.sem, f_dt.at(NB - 1, 3))
            by_chunk = BANK[6][:, :].rearrange("p (c g h) -> p g c h", c=NCH, g=KVH)
            def spt(i):
                return SP[:, i, :]

            def spv(i):
                return SP[:, i, :].rearrange("p (g c h) -> p g c h", g=KVH, c=NCH)
            cnt = [0]
            def link(ins):
                ins.then_inc(prep_chain.sem, 1)
                cnt[0] += 1
                dve.wait_ge(prep_chain.sem, cnt[0])
            for g in range(KVH):
                ins = nc.vector.tensor_tensor(spv(0)[:, g], by_chunk[:, g],
                                              DTB[:, None, g * G:(g + 1) * G].broadcast_to([P, NCH, G]), ALU.add)
            link(ins)
            nc.vector.scalar_tensor_tensor(spt(1), spt(0), -1.0, spt(0), ALU.mult, ALU.max).then_inc(prep_abs.sem, 1)
            dve.wait_ge(prep_act.sem, 2)
            link(nc.vector.tensor_scalar(spt(3), spt(2), 2.0, None, ALU.add))
            link(nc.vector.reciprocal(spt(4), spt(3)))
            link(nc.vector.tensor_tensor(spt(3), spt(2), spt(4), ALU.mult))
            link(nc.vector.tensor_tensor(spt(4), spt(3), spt(3), ALU.mult))
            link(nc.vector.tensor_scalar(spt(5), spt(4), 1.0 / 17, None, ALU.mult))
            for d in (15, 13, 11, 9, 7, 5, 3):
                link(nc.vector.scalar_tensor_tensor(spt(5), spt(5), 1.0 / d, spt(4), ALU.add, ALU.mult))
            link(nc.vector.scalar_tensor_tensor(spt(5), spt(5), 1.0, spt(3), ALU.add, ALU.mult))
            link(nc.vector.tensor_scalar(spt(0), spt(0), 0.0, None, ALU.max))
            dtf = DT[:, :, :, :].rearrange("p g c h -> p (g c h)")
            link(nc.vector.scalar_tensor_tensor(dtf, spt(5), 2.0, spt(0), ALU.mult, ALU.add))
            for g in range(KVH):
                ins = nc.vector.scalar_tensor_tensor(spv(5)[:, g], DT[:, g], -1.0,
                                                     ALOG[:, None, g * G:(g + 1) * G].broadcast_to([P, NCH, G]),
                                                     ALU.mult, ALU.mult)
            ins.then_inc(prep_dve.sem, 1)
            dve.wait_ge(prep_dve.sem, 1)
            ghf, glf = (T[:, :, :, :].rearrange("p g c h -> p (g c h)") for T in (GH, GL))
            nc.vector.tensor_copy(ghf, spt(5)).then_inc(prep_dve.sem, 1)
            dve.wait_ge(prep_dve.sem, 2)
            nc.vector.tensor_tensor(glf, spt(5), ghf, ALU.subtract).then_inc(prep_dve.sem, 1)
            dve.wait_ge(prep_act.sem, 5)
            nc.vector.tensor_tensor(WJ[:, :, :, :].rearrange("p g c h -> p (g c h)"),
                                    WJ[:, :, :, :].rearrange("p g c h -> p (g c h)"), dtf, ALU.mult).then_inc(prep_dve.sem, 1)
            dve.wait_ge(rope_landed.sem, 32)

            def tab(T, g, n):
                flat = T[:, :, :, :].rearrange("p g c h -> p (g c h)")
                if isinstance(g, int):
                    return flat[:, (g * NCH + n) * G:(g * NCH + n + 1) * G]
                return flat[:, bass.ds(g * (NCH * G) + n * G, G)]

            def rotate(g, b, j, use, part):
                dst = QF[:, (j - 1) % 2, :] if j else KF[:, :]
                t0 = b % NB * TB
                if part == 0:
                    dve.wait_ge(swap_ready.sem, swap_ready.at(g, 5 * b + j))
                    dve.wait_ge(qh_ready.sem, qh_ready.at(g, 5 * b + j - 2))
                    dve.wait_ge(ql_ready.sem, ql_ready.at(g, 5 * b + j - 2))
                    if j == 0:
                        dve.wait_ge(kt_full.sem, kt_full.at(g, b - 1))
                    nc.vector.tensor_tensor(dst, bank(use)[:, :], COS[:, t0:t0 + TB], ALU.mult).then_inc(ring_free.sem, 1)
                else:
                    dve.wait_ge(ring_free.sem, ring_free.at(g, use))
                    dve.wait_ge(sin_ready.sem, sin_ready.at(g, 5 * b + j))
                    nc.vector.tensor_tensor(dst, dst, QS[:, (j + 1) % 2, :], ALU.add).then_inc(qf_ready.sem, 1)

            def v_lo(g, b, use):
                dve.wait_ge(v_ready.sem, v_ready.at(g, b))
                dve.wait_ge(intra_full.sem, intra_full.at(g, 4 * (b - 1) - 1))
                nc.vector.tensor_tensor(VL[:, b % 2, :], bank(use)[:, :], VH[:, b % 2, :], ALU.subtract).then_inc(ring_free.sem, 1)

            def silu2(g, b, s, use):
                dve.wait_ge(tanh_ready.sem, tanh_ready.at(g, 4 * b + s))
                slot_of = s + b % 2 * (s == BLK - 1)
                dve.wait_ge(z_ready.sem, z_ready.at(g, 4 * (b - (2 if s == BLK - 1 else 1)) + s))
                nc.vector.scalar_tensor_tensor(G2[:, slot_of, :], TH[:, :], 1.0, bank(use)[:, :], ALU.add, ALU.mult).then_inc(ring_free.sem, 1)

            def keys_lo(g, b):
                dve.wait_ge(kdh_ready.sem, kdh_ready.at(g, b))
                dve.wait_ge(cs_full.sem, cs_full.at(g, cs_event(4 * (b - 1) - 1)))
                nc.vector.tensor_tensor(KDL[:, b % 2, :], B_T[:, :], KDH[:, b % 2, :], ALU.subtract).then_inc(turn_free.sem, 1)

            def decayed(g, n):
                dve.wait_ge(scores_full.sem, scores_full.at(g, n))
                dve.wait_ge(decay_ready.sem, decay_ready.at(g, n))
                dt = tab(DT, g, n)
                for h in range(G):
                    c = slice(h * P, (h + 1) * P)
                    ins = nc.vector.scalar_tensor_tensor(PF[:, c], B_S[:, c], dt[:, h:h + 1], PF[:, c], ALU.mult, ALU.mult)
                ins.then_inc(p_ready.sem, 1)

            def combine(g, n):
                if n % NCH == 0:
                    dve.wait_ge(zt_full.sem, zt_full.at(g, n - 1))
                    dve.wait_ge(intra_full.sem, intra_full.at(g, n))
                    nc.vector.tensor_copy(YF[:, :], B_PV[:, :]).then_inc(y_ready.sem, 1)
                    return
                dve.wait_ge(inter_full.sem, inter_full.at(g, in_event(n)))
                dve.wait_ge(zt_full.sem, zt_full.at(g, n - 1))
                nc.vector.tensor_tensor(YF[:, :].rearrange("p (h e) -> p h e", h=G), B_IN[:, :].rearrange("p (h e) -> p h e", h=G),
                                            tab(EG, g, n)[:, :, None].broadcast_to([P, G, P]), ALU.mult).then_inc(inter_read.sem, 1)
                dve.wait_ge(inter_read.sem, inter_read.at(g, in_event(n)))
                dve.wait_ge(intra_full.sem, intra_full.at(g, n))
                nc.vector.tensor_tensor(YF[:, :], B_PV[:, :], YF[:, :], ALU.add).then_inc(y_ready.sem, 1)

            def update_state(g, n):
                if n % NCH == NCH - 1:
                    return
                dve.wait_ge(cs_full.sem, cs_full.at(g, cs_event(n)))
                dve.wait_ge(sth_ready.sem, sth_ready.at(g, cs_event(n - 1)))
                dve.wait_ge(stl_ready.sem, stl_ready.at(g, cs_event(n - 1)))
                if n % NCH == 0:
                    nc.vector.tensor_copy(ST[:, :], B_CS[:, :]).then_inc(st_ready.sem, 1)
                    return
                dc = tab(DCH, g, n)
                for h in range(G):
                    c = slice(h * P, (h + 1) * P)
                    ins = nc.vector.scalar_tensor_tensor(ST[:, c], ST[:, c], dc[:, h:h + 1], B_CS[:, c], ALU.mult, ALU.add)
                ins.then_inc(st_ready.sem, 1)

            def state_lo(g, n):
                if n % NCH == NCH - 1:
                    return
                dve.wait_ge(sth_ready.sem, sth_ready.at(g, cs_event(n)))
                dve.wait_ge(inter_full.sem, inter_full.at(g, in_event(n)))
                nc.vector.tensor_tensor(STL[:, :], ST[:, :], STH[:, :], ALU.subtract).then_inc(stl_ready.sem, 1)

            def sum_squares(g, n):
                dve.wait_ge(sq_ready.sem, sq_ready.at(g, n))
                dve.wait_ge(rm_ready.sem, rm_ready.at(g, n - 1))
                nc.vector.tensor_reduce(SS[:, :], SQ[:, :, :], AX.X, ALU.add).then_inc(ss_ready.sem, 1)

            def gated(g, n):
                b, s = divmod(n, BLK)
                dve.wait_ge(rr_ready.sem, rr_ready.at(g, n))
                if s == 0:
                    dve.wait_ge(ring_free.sem, ring_free.at(g, gate_use(b)))
                for h in range(G):
                    c = slice(h * P, (h + 1) * P)
                    ins = nc.vector.scalar_tensor_tensor(YF[:, c], YF[:, c], RR[:, h:h + 1], G2[:, s + b % 2 * (s == BLK - 1), c],
                                                         ALU.mult, ALU.mult)
                ins.then_inc(z_ready.sem, 1)

            def wo_lo(g, k):
                act_hi, stage = WH[:, PO + k, :], STAGEO[:, k % 2, :]
                dve.wait_ge(woh_ready.sem, woh_ready.at(g, k))
                nc.vector.scalar_tensor_tensor(WL[:, PO + k, :], stage, GNH[:, 0:1], act_hi, ALU.mult, ALU.subtract).then_inc(wol_ready.sem, 1)

            def zt_lo(g, n, before):
                dve.wait_ge(zth_ready.sem, zth_ready.at(g, n))
                dve.wait_ge(ring_full.sem, ring_full.at(g, before))
                nc.vector.tensor_tensor(ZTL[:, :], B_T[:, :], ZTH[:, :], ALU.subtract).then_inc(turn_free.sem, 1)

            def add_out(g, n, use):
                dve.wait_ge(ring_full.sem, ring_full.at(g, use))
                nc.vector.tensor_tensor(ACC[:, n % NCH, :], ACC[:, n % NCH, :], bank(use)[:, :], ALU.add).then_inc(ring_free.sem, 1)

            for item in range(NFILL):
                use = item - NFILL - FIRST
                if item < PV_:
                    rotate(0, 0, item, use, 0)
                if 0 < item <= PV_:
                    rotate(0, 0, item - 1, use - 1, 1)
                if item == PV_:
                    v_lo(0, 0, use)
                elif item > PV_:
                    silu2(0, 0, item - PG, use)
            keys_lo(0, 0)
            decayed(0, 0)

            def step(g, n, last, first=False):
                b, s = divmod(n, BLK)
                ring = ring_order(last)

                def slot(x, part):
                    if x not in filled(n, last):
                        return
                    item = filled(n, last)[x]
                    use = item - FIRST if first else ring[("F", b, item)]
                    if item < PV_:
                        rotate(g, b + 1, item, use, part)
                    elif part == 0 and item == PV_:
                        v_lo(g, b + 1, use)
                    elif part == 0:
                        silu2(g, b + 1, item - PG, use)
                if not (last and n == NCH - 1):
                    decayed(g, n + 1)
                if n == 1:
                    for k in range(2):
                        wo_lo(g, k)
                if not first:
                    zt_lo(g, n - 1, ring[("W", n - 2)])
                slot("A", 0)
                combine(g, n)
                update_state(g, n)
                sum_squares(g, n)
                state_lo(g, n)
                slot("B", 0)
                slot("A", 1)
                if n == 1:
                    for k in range(2, G):
                        wo_lo(g, k)
                if "B" in filled(n, last):
                    gated(g, n)
                slot("C", 0)
                if "B" not in filled(n, last):
                    gated(g, n)
                slot("B", 1)
                slot("C", 1)
                if s == 1 and filled(n, last):
                    keys_lo(g, b + 1)
                if not first:
                    add_out(g, n - 1, ring[("W", n - 1)])

            step(0, 0, False, True)
            with dve.Fori(0, KVH - 1) as g:
                for n in steps(False):
                    step(g, n, False)
            for n in steps(True):
                step(KVH - 1, n, True)
            zt_lo(KVH - 1, NCH - 1, ring_order(True)[("W", NCH - 2)])
            add_out(KVH - 1, NCH - 1, ring_order(True)[("W", NCH - 1)])
            dve.wait_ge(ring_free.sem, ring_free.at(KVH - 1, ring_order(True)[("W", NCH - 1)]))
            nc.vector.engine_nop().then_inc(attn_done.sem, 1)
            for k in range(NB):
                ffn_dve(dve, k, k + NB, False)


def constants():
    f = np.float32
    inv = f(1.0) / np.power(f(10000.0), np.arange(0, P, 2, dtype=f) / f(P), dtype=f)
    ang = np.arange(L, dtype=f)[None, :] * np.concatenate([inv, inv])[:, None]
    cos, sin = np.cos(ang, dtype=f), np.sin(ang, dtype=f)
    sin[:P // 2] *= f(-1.0)
    t = np.arange(P)
    masks = np.concatenate([(t[:, None] > t[None, :]), (t[:, None] <= t[None, :]), (t[:, None] == t[None, :])], 1).astype(f)
    neg = np.tile(np.where(t[None, :] < t[:, None], f(BIGNEG), f(0)), (1, G))
    return cos, sin, np.concatenate([masks, neg], 1).astype(f)


def kernel(**inputs):
    import concourse.bacc as bacc
    from concourse.bass_utils import run_bass_kernel_spmd

    a = {k.replace("L0_attn_", "").replace("L0_ffn_", ""): np.asarray(v) for k, v in inputs.items()}

    def by_tile(w):
        return w.reshape(w.shape[0], KT, P).transpose(2, 1, 0)
    cos, sin, masks = constants()
    wall = np.empty((KVH, NPIECE, P, HID), a["Wq"].dtype)
    for g in range(KVH):
        wall[g, PK] = by_tile(a["Wk"][g * P:(g + 1) * P]).reshape(P, HID)
        wall[g, PV_] = by_tile(a["Wv"][g * P:(g + 1) * P]).reshape(P, HID)
        for h in range(G):
            c = slice((g * G + h) * P, (g * G + h + 1) * P)
            wall[g, PQ + h] = by_tile(a["Wq"][c]).reshape(P, HID)
            wall[g, PO + h] = a["Wo"][:, c].T
        wall[g, PG:PG + KT] = by_tile(a["Wg"][g * GW:(g + 1) * GW]).transpose(1, 0, 2)
    rep = lambda v: np.broadcast_to(v[None, :], (P, v.shape[0]))
    xs = a["hidden_states"].reshape(NB, BLK, P, HID).transpose(0, 2, 1, 3)
    arrays = {
        "x": xs, "cos": cos, "sin": sin, "masks": masks, "wall": wall, "rwt": by_tile(a["router_weight"]), "rb": rep(a["router_bias"]),
        "eb2": np.concatenate([a["expert_bias"]] * 2, 0), "wint": by_tile(a["Win"]), "dtb": rep(a["dt_bias"]),
        "alog": rep(a["A_log_bias"]), "gn": a["gnorm_w"].reshape(P, 1),
    }
    arrays = {f"in_{k}": np.ascontiguousarray(v) for k, v in arrays.items()}
    nc = bacc.Bacc("TRN2", target_bir_lowering=False, num_devices=1)
    aps = [nc.dram_tensor(k, v.shape, mybir.dt.from_np(v.dtype), kind="ExternalInput").ap() for k, v in arrays.items()]
    o = nc.dram_tensor("out", (NB, P, BLK, HID), F32, kind="ExternalOutput").ap()
    build(nc, *aps, o)
    r = run_bass_kernel_spmd(nc, [arrays], core_ids=[0])
    return r.results[0]["out"].transpose(0, 2, 1, 3).reshape(1, L, HID)
```

```python
from contextlib import ExitStack

import numpy as np

import concourse.bass as bass
from concourse import mybir

F32 = mybir.dt.float32
BF16 = mybir.dt.bfloat16
ALU = mybir.AluOpType
ACT = mybir.ActivationFunctionType
AX = mybir.AxisListType

P = 128
HID = 512
KT = HID // P
H, KVH = 32, 8
G = H // KVH
L = 2048
NCH = L // P
BLK = 4
TB = BLK * P
NB = L // TB
NE = 64
TOPK = 8
EPS = 1e-5
GW = G * P
NPIECE = 2 + 3 * G
PK, PQ, PV_, PG, PO = 0, 1, 1 + G, 2 + G, 2 + 2 * G
NFILL = 2 + 2 * G

FILLS = {0: {"A": 0, "B": 1, "C": 2}, 1: {"A": 3, "B": 4, "C": 5}, 2: {"A": 6, "B": 7}, 3: {"A": 8, "C": 9}}
EARLY = {10: (0, 1), 11: (3, 4), 12: (6,), 13: (8,)}
MID = {10: (2,), 11: (5,), 12: (7,), 13: (9,)}
N_EARLY = sum(len(i) for i in EARLY.values())
FIRST = len(FILLS[0])


def steps(last):
    return range(1, NCH if last else NCH + 1)


def filled(n, last):
    return {} if last and n // BLK == NB - 1 else FILLS[n % BLK]


def ring_order(last):
    seq = []
    for n in steps(last):
        f = filled(n, last)
        seq += [("F", n // BLK, f[x]) for x in "ABC" if x in f] + [("W", n - 1)]
    if last:
        seq.append(("W", NCH - 1))
    order = {u: r for r, u in enumerate(seq)}
    order[("W", -1)] = -1
    return order


def turn_order(last):
    seq = []
    for n in steps(last):
        seq.append(("Z", n - 1))
        if n % BLK == 1 and filled(n, last):
            seq.append(("K", n // BLK))
    if last:
        seq.append(("Z", NCH - 1))
    return {u: r for r, u in enumerate(seq)}


def cs_event(n):
    return n - (n + 1) // NCH


def in_event(n):
    return n - n // NCH - 1


def build(nc, x, cos, sin, masks, wall, rwt, rb, eb2, wint, dtb, alog, gn, out):
    with ExitStack() as ctx:
        def sb(name, shape, dt=F32):
            return ctx.enter_context(nc.sbuf_tensor(name, shape, dt))

        class Sem:

            def __init__(self, name, per=0, before=0, free=0):
                self.sem = ctx.enter_context(nc.semaphore(name))
                self.per, self.base, self.free = per, before + free, free

            def at(self, g, idx):
                assert self.base + idx >= 0 or (isinstance(g, int) and g * self.per + self.base + idx >= 0), "waits are above zero"
                return g * self.per + (self.base + idx + 1)

        ACC = sb("ACC", [P, NCH, HID])
        XTH = sb("XTH", [P, KT, L], BF16)
        XTL = sb("XTL", [P, KT, L], BF16)
        COS = sb("COS", [P, L])
        SIN = sb("SIN", [P, L])
        WH = sb("WH", [P, NPIECE, HID], BF16)
        WL = sb("WL", [P, NPIECE, HID], BF16)
        STAGE = sb("STAGE", [P, 2, HID])
        EG = sb("EG", [P, NCH * H])
        WJ = sb("WJ", [P, NCH * H])
        DT = sb("DT", [P, NCH * H])
        DCH = sb("DCH", [P, NCH * H])
        GH = sb("GH", [P, NCH * H], BF16)
        GL = sb("GL", [P, NCH * H], BF16)
        IDF = sb("IDF", [P, P])
        MB = sb("MB", [P, 3, P], BF16)
        DM = sb("DM", [P, G, P])
        HALF = sb("HALF", [P, G])
        EPSC = sb("EPSC", [P, G])
        GNH = sb("GNH", [P, 1])
        RWT = sb("RWT", [P, KT, NE])
        RB = sb("RB", [P, NE])
        EBH = sb("EBH", [P, HID], BF16)
        EBL = sb("EBL", [P, HID], BF16)
        BS = sb("BS", [P, 2, BLK, 6])
        MV = sb("MV", [P, 2, BLK, 2])
        VE = sb("VE", [P, 2, BLK])
        RSTD = sb("RSTD", [P, 2, BLK])
        NMR = sb("NMR", [P, 2, BLK])

        BANK = [ctx.enter_context(nc.psum_tensor(f"B{i}", [P, 512], F32)) for i in range(8)]
        RING = BANK[0:2]
        B_S, B_D, B_PV, B_IN, B_CS, B_T = BANK[2:8]
        LOGITS, TURNED, MIX, DOTS = BANK[0], BANK[1], BANK[2:6], BANK[6]

        def memory(stack, tensors):
            return [stack.enter_context(nc.sbuf_tensor(name, shape, dt)) for name, shape, dt in tensors]

        with ExitStack() as over:
            MASKS, ONES, DTB, ALOG, SPD, GF = memory(over, (
                ("MASKS", [P, 3, P], F32), ("ONES", [P, P], F32), ("DTB", [P, H], F32), ("ALOG", [P, H], F32),
                ("SPD", [P, 2, 7, BLK * H], F32), ("GF", [P, NCH * H], F32)))

        MH = sb("MH", [P, G, P], BF16)
        ML = sb("ML", [P, G, P], BF16)
        PF = sb("PF", [P, GW])
        PH = sb("PH", [P, 2, GW], BF16)
        PL = sb("PL", [P, 2, GW], BF16)
        WVF = sb("WVF", [P, G, P])
        WVH = sb("WVH", [P, GW], BF16)
        WVL = sb("WVL", [P, GW], BF16)
        YF = sb("YF", [P, GW])
        SQ = sb("SQ", [P, G, P])
        SS = sb("SS", [P, G])
        RM = sb("RM", [P, G])
        RR = sb("RR", [P, G])
        ZTH = sb("ZTH", [P, GW], BF16)
        ZTL = sb("ZTL", [P, GW], BF16)
        ST = sb("ST", [P, GW])
        STH = sb("STH", [P, GW], BF16)
        STL = sb("STL", [P, GW], BF16)

        with ExitStack() as over:
            (XN, XNT, LG, MX, MR, NM, EX, SUM, MK, WU, S8, RC, HRC, WS, WN, WHL, WT, WINF, WINH, WINL,
             EBF, GN) = memory(over, (
                ("XN", [P, 2, BLK, HID], F32), ("XNT", [P, BLK, HID], F32),
                ("LG", [P, BLK, NE], F32), ("MX", [P, BLK, TOPK], F32), ("MR", [P, BLK, NE], F32), ("NM", [P, BLK], F32),
                ("EX", [P, BLK, NE], F32), ("SUM", [P, BLK], F32), ("MK", [P, BLK, NE], F32), ("WU", [P, BLK, NE], F32),
                ("S8", [P, BLK], F32), ("RC", [P, BLK], F32), ("HRC", [P, BLK], F32), ("WS", [P, BLK], F32),
                ("WN", [P, BLK, NE], F32), ("WHL", [P, BLK, 2 * NE], BF16), ("WT", [P, BLK, P], BF16),
                ("WINF", [P, KT, H], F32), ("WINH", [P, KT, H], BF16), ("WINL", [P, KT, H], BF16),
                ("EBF", [P, HID], F32), ("GN", [P, 1], F32)))

        QS = sb("QS", [P, 2, TB])
        QF = sb("QF", [P, 2, TB])
        QH = sb("QH", [P, 2, G, TB], BF16)
        QL = sb("QL", [P, 2, G, TB], BF16)
        KH = sb("KH", [P, 2, TB], BF16)
        KL = sb("KL", [P, 2, TB], BF16)
        KDH = sb("KDH", [P, 2, TB], BF16)
        KDL = sb("KDL", [P, 2, TB], BF16)
        VF = sb("VF", [P, 2, TB])
        VH = sb("VH", [P, 2, TB], BF16)
        VL = sb("VL", [P, 2, TB], BF16)
        G2 = sb("G2", [P, BLK + 1, GW])
        KF = sb("KF", [P, TB])
        TH = sb("TH", [P, GW])

        LTF, TRIF = MASKS[:, 0, :], MASKS[:, 1, :]
        LTB, TRIB, IDB = MB[:, 0, :], MB[:, 1, :], MB[:, 2, :]

        n_ring, n_turn = len(ring_order(False)) - 1, len(turn_order(False))
        ring_full = Sem("ring_full", n_ring, NFILL + FIRST)
        ring_free = Sem("ring_free", n_ring, NFILL + FIRST, free=2)
        turn_free = Sem("turn_free", n_turn, 1, free=1)
        scores_full = Sem("scores_full", NCH)
        logdecay_full = Sem("logdecay_full", NCH, free=1)
        inter_full = Sem("inter_full", NCH - 1, free=5)
        intra_full = Sem("intra_full", NCH, free=5)
        cs_full = Sem("cs_full", NCH - 1, free=4)
        zt_full = Sem("zt_full", NCH, free=1)
        kt_full = Sem("kt_full", NB, free=1)
        swap_ready = Sem("swap_ready", NB * 5)
        qh_ready = Sem("qh_ready", NB * 5, free=2)
        v_ready = Sem("v_ready", NB)
        tanh_ready = Sem("tanh_ready", NCH)
        decay_ready = Sem("decay_ready", NCH, free=1)
        ph_ready = Sem("ph_ready", NCH, free=1)
        wvh_ready = Sem("wvh_ready", NCH - 1, free=1)
        sth_ready = Sem("sth_ready", NCH - 1, free=1)
        sq_ready = Sem("sq_ready", NCH, free=1)
        zth_ready = Sem("zth_ready", NCH)
        kdh_ready = Sem("kdh_ready", NB)
        qf_ready = Sem("qf_ready", NB * 5, free=1)
        s_ready = Sem("s_ready", NCH, free=1)
        ql2_ready = Sem("ql2_ready", NB * 3, free=1)
        p_ready = Sem("p_ready", NCH, free=1)
        inter_read = Sem("inter_read", NCH - 1, free=1)
        y_ready = Sem("y_ready", NCH, free=1)
        ss_ready = Sem("ss_ready", NCH, free=1)
        z_ready = Sem("z_ready", NCH, free=5)
        st_ready = Sem("st_ready", NCH - 1, free=1)
        stl_ready = Sem("stl_ready", NCH - 1, free=1)
        sin_ready = Sem("sin_ready", NB * 5)
        ql_ready = Sem("ql_ready", NB * 2, free=2)
        m_ready = Sem("m_ready", NCH)
        dm_ready = Sem("dm_ready", NCH)
        wvf_ready = Sem("wvf_ready", NCH - 1, free=4)
        wvl_ready = Sem("wvl_ready", NCH - 1, free=1)
        pl_ready = Sem("pl_ready", NCH, free=1)
        rm_ready = Sem("rm_ready", NCH, free=1)
        rr_ready = Sem("rr_ready", NCH)
        wh_ready, wl_early, wl_mid = Sem("wh_ready", PO), Sem("wl_early", N_EARLY), Sem("wl_mid", PO - N_EARLY)
        woh_ready, wol_ready = Sem("woh_ready", G), Sem("wol_ready", G, free=2)
        w_landed = [Sem(f"w_landed{i}") for i in range(2)]

        f_mv, f_ve, f_rstd, f_nmr = ([Sem(f"{n}{w}", 1) for w in range(2)] for n in ("f_mv", "f_ve", "f_rstd", "f_nmr"))
        f_bs, f_xn = ([Sem(f"{n}{w}", 4) for w in range(2)] for n in ("f_bs", "f_xn"))
        f_tp, f_xnt, f_lg, f_mx, f_mr, f_nm, f_ex = (Sem(n, k) for n, k in (
            ("f_tp", 4), ("f_xnt", 4), ("f_lg", 1), ("f_mx", 1), ("f_mr", 1), ("f_nm", 1), ("f_ex", 1)))
        f_gate, f_l = Sem("f_gate", 9), Sem("f_l", 1)
        f_wt, f_wtc, f_mix, f_ax, f_acc = (Sem(n, k) for n, k in (
            ("f_wt", 1), ("f_wtc", 1), ("f_mix", 4), ("f_ax", 4), ("f_acc", 4)))
        f_tp2, f_xth, f_xtl = (Sem(n, 4) for n in ("f_tp2", "f_xth", "f_xtl"))
        d_dot, d_x, d_abs, d_e, d_e2, d_g, d_gh, d_gl, d_cum, d_exp, d_wj = (Sem(n, 1) for n in (
            "d_dot", "d_x", "d_abs", "d_e", "d_e2", "d_g", "d_gh", "d_gl", "d_cum", "d_exp", "d_wj"))
        d_series = Sem("d_series", 13)
        a_ready = Sem("a_ready")
        x_landed = [Sem(f"x_landed{i}") for i in range(NB)]
        c_landed = Sem("c_landed")
        rope_landed = Sem("rope_landed")
        out_sent = Sem("out_sent")
        const_pool, const_dve, const_act = Sem("const_pool"), Sem("const_dve"), Sem("const_act")

        block = ctx.enter_context(nc.Block())

        def wl_of(piece):
            for signal, when in ((wl_early, EARLY), (wl_mid, MID)):
                order = [i for n in sorted(when) for i in when[n]]
                if piece in order:
                    return signal, order.index(piece)

        def mm3(out_, ah, al, bh, bl, first, last):
            nc.tensor.matmul(out_, ah, bh, start=first, stop=False)
            nc.tensor.matmul(out_, ah, bl, start=False, stop=False)
            return nc.tensor.matmul(out_, al, bh, start=False, stop=last)

        def bank(use):
            return RING[(use + NFILL + FIRST) % 2]

        def v_use(b):
            return ring_order(False)[("F", b - 1, PV_)] if b else PV_ - NFILL - FIRST

        def gate_use(b):
            return ring_order(False)[("F", b - 1, NFILL - 1)] if b else -1 - FIRST

        def k_use(b):
            return turn_order(False)[("K", b - 1)] if b else -1

        @block.sync
        def _(sp):
            for k in range(NB):
                sp.dma_start(ACC[:, k * BLK:(k + 1) * BLK, :], x[k]).then_inc(x_landed[k].sem, 16)
                if k == 0:
                    for dst, src in ((MASKS[:, :, :], masks), (IDF[:, :], masks[:, 2 * P:3 * P]), (RWT[:, :, :], rwt),
                                     (RB[:, :], rb), (EBF[:, :], eb2), (WINF[:, :, :], wint), (DTB[:, :], dtb),
                                     (ALOG[:, :], alog), (GN[:, :], gn)):
                        sp.dma_start(dst, src).then_inc(c_landed.sem, 16)
            sp.dma_start(COS[:, :], cos).then_inc(rope_landed.sem, 16)
            sp.dma_start(SIN[:, :], sin).then_inc(rope_landed.sem, 16)

            def load_weights(g):
                for i in range(NPIECE):
                    if 2 <= i < PO + 2:
                        signal, k = wl_of(i - 2)
                        sp.wait_ge(signal.sem, signal.at(g, k))
                    else:
                        sp.wait_ge(wol_ready.sem, wol_ready.at(g, (i - 2 - PO) if i > PO else i - 2))
                    sp.dma_start(STAGE[:, i % 2, :], wall[g, i] if isinstance(g, int)
                                 else wall[bass.ds(g, 1), i].rearrange("a p n -> (a p) n")).then_inc(w_landed[i % 2].sem, 16)
            load_weights(0)
            with sp.Fori(1, KVH) as g:
                load_weights(g)
            for k in range(NB - 1):
                sp.wait_ge(f_acc.sem, f_acc.at(NB + k, 3))
                sp.dma_start(out[k], ACC[:, k * BLK:(k + 1) * BLK, :]).then_inc(out_sent.sem, 16)
            for i in range(BLK):
                sp.wait_ge(f_acc.sem, f_acc.at(2 * NB - 1, i))
                sp.dma_start(out[NB - 1][:, i, :], ACC[:, (NB - 1) * BLK + i, :]).then_inc(out_sent.sem, 16)
            sp.wait_ge(out_sent.sem, 16 * (NB - 1 + BLK))

        def chunks_of(f):
            return ACC[:, f % NB * BLK:(f % NB + 1) * BLK, :]

        def dve_stats(dve, w, f, chunks=range(BLK)):
            if w == 0 and f < NB:
                dve.wait_ge(x_landed[f].sem, 16)
            if w == 1:
                dve.wait_ge(f_acc.sem, f_acc.at(f, 3))
            if f:
                dve.wait_ge(f_nmr[w].sem, f_nmr[w].at(f - 1, 0))
            A = chunks_of(f)
            for i in chunks:
                nc.vector.bn_stats(BS[:, w, i, :], A[:, i, :]).then_inc(f_bs[w].sem, 1)
            if BLK - 1 not in chunks:
                return
            dve.wait_ge(f_bs[w].sem, f_bs[w].at(f, BLK - 1))
            for i in range(BLK):
                ins = nc.vector.bn_aggr(MV[:, w, i, :], BS[:, w, i, :])
            ins.then_inc(f_mv[w].sem, 1)

        def pool_rstd(pool, w, f):
            pool.wait_ge(f_mv[w].sem, f_mv[w].at(f, 0))
            if f:
                pool.wait_ge(f_xn[w].sem, f_xn[w].at(f - 1, 3))
            nc.gpsimd.tensor_tensor(VE[:, w, :], MV[:, w, :, 1], EPSC[:, :], ALU.add)
            nc.gpsimd.tensor_scalar(NMR[:, w, :], MV[:, w, :, 0], -1.0, None, ALU.mult).then_inc(f_ve[w].sem, 1)
            pool.wait_ge(f_ve[w].sem, f_ve[w].at(f, 0))
            nc.gpsimd.tensor_tensor(RSTD[:, w, :], VE[:, w, :], HALF[:, 0:BLK], ALU.pow).then_inc(f_rstd[w].sem, 1)
            pool.wait_ge(f_rstd[w].sem, f_rstd[w].at(f, 0))
            nc.gpsimd.tensor_tensor(NMR[:, w, :], NMR[:, w, :], RSTD[:, w, :], ALU.mult).then_inc(f_nmr[w].sem, 1)

        def act_normalise(act, w, f):
            act.wait_ge(f_nmr[w].sem, f_nmr[w].at(f, 0))
            if w == 1:
                act.wait_ge(f_ax.sem, f_ax.at(f, 3))
            elif 2 <= f < NB + 2:
                act.wait_ge(f_tp2.sem, f_tp2.at(min(f - 2, NB - 1), 3))
            elif f >= NB + 2:
                act.wait_ge(f_acc.sem, f_acc.at(f - 2, 3))
            A = chunks_of(f)
            for i in range(BLK):
                nc.scalar.activation(XN[:, f % 2, i, :], A[:, i, :], ACT.Identity, bias=NMR[:, w, i:i + 1],
                                     scale=RSTD[:, w, i:i + 1]).then_inc(f_xn[w].sem, 1)

        def pe_turn(pe, f):
            for i in range(BLK):
                pe.wait_ge(f_xn[0].sem, f_xn[0].at(f, i))
                if 2 <= f < NB:
                    pe.wait_ge(f_xtl.sem, f_xtl.at(f - 2, i))
                elif f >= NB + 2:
                    pe.wait_ge(f_ax.sem, f_ax.at(f - 2, i))
                elif f % NB:
                    pe.wait_ge(f_xnt.sem, f_xnt.at(f - 1, i))
                for k in range(KT):
                    ins = nc.tensor.transpose(MIX[i][:, k * P:(k + 1) * P], XN[:, f % 2, i, k * P:(k + 1) * P], IDF[:, :])
                ins.then_inc(f_tp.sem, 1)

        def act_turned(act, f):
            for i in range(BLK):
                act.wait_ge(f_tp.sem, f_tp.at(f, i))
                nc.scalar.activation(XNT[:, i, :], MIX[i][:, :], ACT.Copy).then_inc(f_xnt.sem, 1)

        def pe_logits(pe, f):
            if f:
                pe.wait_ge(f_l.sem, f_l.at(f - 1, 0))
            for i in range(BLK):
                pe.wait_ge(f_xnt.sem, f_xnt.at(f, i))
                for k in range(KT):
                    ins = nc.tensor.matmul(LOGITS[:, i * NE:(i + 1) * NE], XNT[:, i, k * P:(k + 1) * P], RWT[:, k, :],
                                           start=(k == 0), stop=(k == KT - 1))
            ins.then_inc(f_lg.sem, 1)

        def dve_gate(dve, f):
            dve.wait_ge(f_lg.sem, f_lg.at(f, 0))
            nc.vector.tensor_tensor(LG[:, :, :], LOGITS[:, 0:BLK * NE].rearrange("p (b e) -> p b e", b=BLK),
                                    RB[:, None, :].broadcast_to([P, BLK, NE]), ALU.add).then_inc(f_l.sem, 1)
            dve.wait_ge(f_l.sem, f_l.at(f, 0))
            for i in range(BLK):
                ins = nc.vector.max(MX[:, i, :], LG[:, i, :])
            ins.then_inc(f_mx.sem, 1)
            dve.wait_ge(f_mx.sem, f_mx.at(f, 0))
            nc.vector.tensor_scalar(NM[:, :], MX[:, :, 0], -1.0, None, ALU.mult).then_inc(f_nm.sem, 1)
            for i in range(BLK):
                ins = nc.vector.match_replace(MR[:, i, :], MX[:, i, :], LG[:, i, :], -3.0e38)
            ins.then_inc(f_mr.sem, 1)
            dve.wait_ge(f_mr.sem, f_mr.at(f, 0))
            nc.vector.tensor_tensor(MK[:, :, :], LG[:, :, :], MR[:, :, :], ALU.not_equal).then_inc(f_gate.sem, 1)
            dve.wait_ge(f_gate.sem, f_gate.at(f, 0))
            dve.wait_ge(f_ex.sem, f_ex.at(f, 0))
            nc.vector.tensor_reduce(SUM[:, :], EX[:, :, :], AX.X, ALU.add).then_inc(f_gate.sem, 1)
            nc.vector.tensor_tensor(WU[:, :, :], MK[:, :, :], EX[:, :, :], ALU.mult).then_inc(f_gate.sem, 1)
            dve.wait_ge(f_gate.sem, f_gate.at(f, 1))
            nc.vector.reciprocal(RC[:, :], SUM[:, :]).then_inc(f_gate.sem, 1)
            dve.wait_ge(f_gate.sem, f_gate.at(f, 2))
            nc.vector.tensor_reduce(S8[:, :], WU[:, :, :], AX.X, ALU.add).then_inc(f_gate.sem, 1)
            dve.wait_ge(f_gate.sem, f_gate.at(f, 3))
            nc.vector.tensor_scalar(HRC[:, :], RC[:, :], 0.5, None, ALU.mult).then_inc(f_gate.sem, 1)
            dve.wait_ge(f_gate.sem, f_gate.at(f, 5))
            nc.vector.tensor_tensor(WN[:, :, :], WU[:, :, :], HRC[:, :, None].broadcast_to([P, BLK, NE]), ALU.mult).then_inc(f_gate.sem, 1)
            nc.vector.tensor_tensor(WS[:, :], S8[:, :], HRC[:, :], ALU.mult)
            dve.wait_ge(f_gate.sem, f_gate.at(f, 6))
            nc.vector.tensor_copy(WHL[:, :, 0:NE], WN[:, :, :]).then_inc(f_gate.sem, 1)
            dve.wait_ge(f_gate.sem, f_gate.at(f, 7))
            nc.vector.tensor_tensor(WHL[:, :, NE:2 * NE], WN[:, :, :], WHL[:, :, 0:NE], ALU.subtract).then_inc(f_gate.sem, 1)

        def act_exp(act, f):
            act.wait_ge(f_nm.sem, f_nm.at(f, 0))
            act.wait_ge(f_l.sem, f_l.at(f, 0))
            for i in range(BLK):
                ins = nc.scalar.activation(EX[:, i, :], LG[:, i, :], ACT.Exp, bias=NM[:, i:i + 1])
            ins.then_inc(f_ex.sem, 1)

        def pe_weights(pe, f):
            pe.wait_ge(f_gate.sem, f_gate.at(f, 8))
            WTP = TURNED[:, 0:256].bitcast(BF16)
            for i in range(BLK):
                ins = nc.tensor.transpose(WTP[:, i * P:(i + 1) * P], WHL[:, i, :], IDB)
            ins.then_inc(f_wt.sem, 1)

        def act_weights(act, f):
            act.wait_ge(f_wt.sem, f_wt.at(f, 0))
            nc.scalar.activation(WT[:, :, :], TURNED[:, 0:256].bitcast(BF16).rearrange("p (b t) -> p b t", b=BLK),
                                 ACT.Copy).then_inc(f_wtc.sem, 1)

        def pe_mix(pe, f):
            pe.wait_ge(f_wtc.sem, f_wtc.at(f, 0))
            for i in range(BLK):
                if (f + 1) % NB:
                    pe.wait_ge(f_xnt.sem, f_xnt.at(f + 1, i))
                nc.tensor.matmul(MIX[i][:, :], WT[:, i, :], EBH[:, :], start=True, stop=False)
                nc.tensor.matmul(MIX[i][:, :], WT[:, i, :], EBL[:, :], start=False, stop=True).then_inc(f_mix.sem, 1)

        def dve_scaled(dve, f):
            A = chunks_of(f)
            dve.wait_ge(f_xn[0].sem, f_xn[0].at(f, 3))
            for i in range(BLK):
                nc.vector.scalar_tensor_tensor(A[:, i, :], XN[:, f % 2, i, :], WS[:, i:i + 1], A[:, i, :],
                                               ALU.mult, ALU.add).then_inc(f_ax.sem, 1)

        def dve_add(dve, f):
            A = chunks_of(f)
            for i in range(BLK):
                dve.wait_ge(f_ax.sem, f_ax.at(f, i))
                dve.wait_ge(f_mix.sem, f_mix.at(f, i))
                nc.vector.tensor_tensor(A[:, i, :], A[:, i, :], MIX[i][:, :], ALU.add).then_inc(f_acc.sem, 1)

        def dve_mixed(dve, f):
            dve.wait_ge(f_xn[0].sem, f_xn[0].at(f, 3))
            for i in range(BLK):
                dve.wait_ge(f_mix.sem, f_mix.at(f, i))
                nc.vector.scalar_tensor_tensor(XN[:, f % 2, i, :], XN[:, f % 2, i, :], WS[:, i:i + 1], MIX[i][:, :],
                                               ALU.mult, ALU.add).then_inc(f_ax.sem, 1)

        def pool_sum(pool, f, i):
            pool.wait_ge(f_ax.sem, f_ax.at(f, i))
            A = chunks_of(f)
            nc.gpsimd.tensor_tensor(A[:, i, :], A[:, i, :], XN[:, f % 2, i, :], ALU.add).then_inc(f_acc.sem, 1)

        def pe_turn2(pe, f):
            for i in range(BLK):
                pe.wait_ge(f_xn[1].sem, f_xn[1].at(f, i))
                pe.wait_ge(f_acc.sem, f_acc.at(f, i))
                for k in range(KT):
                    ins = nc.tensor.transpose(MIX[i][:, k * P:(k + 1) * P], XN[:, f % 2, i, k * P:(k + 1) * P], IDF[:, :])
                ins.then_inc(f_tp2.sem, 1)

        def pe_dt(pe, f):
            for i in range(BLK):
                pe.wait_ge(f_xtl.sem, f_xtl.at(f, i))
                tok = f * TB + i * P
                for k in range(KT):
                    ins = mm3(DOTS[:, (f * BLK + i) * H:(f * BLK + i + 1) * H],
                              XTH[:, k, tok:tok + P], XTL[:, k, tok:tok + P], WINH[:, k, :], WINL[:, k, :],
                              k == 0, k == KT - 1)
            ins.then_inc(d_dot.sem, 1)

        def act_turned2(act, f):
            for i in range(BLK):
                act.wait_ge(f_tp2.sem, f_tp2.at(f, i))
                nc.scalar.activation(XTH[:, :, f * TB + i * P:f * TB + (i + 1) * P],
                                     MIX[i][:, :].rearrange("p (k t) -> p k t", k=KT), ACT.Copy).then_inc(f_xth.sem, 1)

        def dve_turned2(dve, f):
            for i in range(BLK):
                dve.wait_ge(f_xth.sem, f_xth.at(f, i))
                tok = f * TB + i * P
                nc.vector.tensor_tensor(XTL[:, :, tok:tok + P], MIX[i][:, :].rearrange("p (k t) -> p k t", k=KT),
                                        XTH[:, :, tok:tok + P], ALU.subtract).then_inc(f_xtl.sem, 1)

        BH = BLK * H
        SPX, SPA, SPE, SP2, SPR, SPS, SPY = (SPD[:, :, i, :] for i in range(7))

        def by_head(T):
            return T[:, None, :].broadcast_to([P, BLK, H])

        def rows(ap):
            return ap.rearrange("p (c h) -> p c h", c=BLK)

        def dve_dt_in(dve, f):
            dve.wait_ge(d_dot.sem, d_dot.at(f, 0))
            nc.vector.tensor_tensor(rows(SPX[:, f % 2]), rows(DOTS[:, f * BH:(f + 1) * BH]), by_head(DTB), ALU.add).then_inc(d_x.sem, 1)
            dve.wait_ge(d_x.sem, d_x.at(f, 0))
            nc.vector.scalar_tensor_tensor(SPA[:, f % 2], SPX[:, f % 2], -1.0, SPX[:, f % 2], ALU.mult, ALU.max).then_inc(d_abs.sem, 1)

        def act_dt_exp(act, f):
            act.wait_ge(d_abs.sem, d_abs.at(f, 0))
            nc.scalar.activation(SPE[:, f % 2], SPA[:, f % 2], ACT.Exp, scale=-1.0).then_inc(d_e.sem, 1)

        def dve_dt(dve, f):
            dve.wait_ge(d_e.sem, d_e.at(f, 0))
            nc.vector.tensor_scalar(SP2[:, f % 2], SPE[:, f % 2], 2.0, None, ALU.add).then_inc(d_e2.sem, 1)
            dve.wait_ge(d_e2.sem, d_e2.at(f, 0))
            nc.vector.reciprocal(SPR[:, f % 2], SP2[:, f % 2]).then_inc(d_series.sem, 1)
            x_, e, r, y, p, s = (T[:, f % 2] for T in (SPX, SPE, SPR, SPY, SP2, SPS))
            cols = slice(f * BH, (f + 1) * BH)
            dve.wait_ge(d_series.sem, d_series.at(f, 0))
            nc.vector.tensor_tensor(s, e, r, ALU.mult).then_inc(d_series.sem, 1)
            nc.vector.tensor_scalar(x_, x_, 0.0, None, ALU.max)
            dve.wait_ge(d_series.sem, d_series.at(f, 1))
            nc.vector.tensor_tensor(y, s, s, ALU.mult).then_inc(d_series.sem, 1)
            dve.wait_ge(d_series.sem, d_series.at(f, 2))
            nc.vector.tensor_scalar(p, y, 1.0 / 17, None, ALU.mult).then_inc(d_series.sem, 1)
            for i, d in enumerate((15, 13, 11, 9, 7, 5, 3)):
                dve.wait_ge(d_series.sem, d_series.at(f, 3 + i))
                nc.vector.scalar_tensor_tensor(p, p, 1.0 / d, y, ALU.add, ALU.mult).then_inc(d_series.sem, 1)
            dve.wait_ge(d_series.sem, d_series.at(f, 10))
            nc.vector.scalar_tensor_tensor(p, p, 1.0, s, ALU.add, ALU.mult).then_inc(d_series.sem, 1)
            dve.wait_ge(d_series.sem, d_series.at(f, 11))
            nc.vector.scalar_tensor_tensor(DT[:, cols], p, 2.0, x_, ALU.mult, ALU.add).then_inc(d_series.sem, 1)
            dve.wait_ge(d_series.sem, d_series.at(f, 12))
            dve.wait_ge(a_ready.sem, 1)
            nc.vector.scalar_tensor_tensor(rows(GF[:, cols]), rows(DT[:, cols]), -1.0, by_head(ALOG), ALU.mult, ALU.mult).then_inc(d_g.sem, 1)

        def pool_dt(pool, f):
            cols = slice(f * BH, (f + 1) * BH)
            pool.wait_ge(d_g.sem, d_g.at(f, 0))
            nc.gpsimd.tensor_copy(GH[:, cols], GF[:, cols]).then_inc(d_gh.sem, 1)
            pool.wait_ge(d_gh.sem, d_gh.at(f, 0))
            nc.gpsimd.tensor_tensor(GL[:, cols], GF[:, cols], GH[:, cols], ALU.subtract).then_inc(d_gl.sem, 1)

        def pe_sums(pe, f):
            pe.wait_ge(d_g.sem, d_g.at(f, 0))
            if f:
                pe.wait_ge(d_exp.sem, d_exp.at(f - 1, 0))
            for j, lhs in enumerate((TRIF, LTF, ONES[:, :])):
                ins = nc.tensor.matmul(B_T[:, j * BH:(j + 1) * BH], lhs, GF[:, f * BH:(f + 1) * BH], start=True, stop=True)
            ins.then_inc(d_cum.sem, 1)

        def act_sums(act, f):
            act.wait_ge(d_cum.sem, d_cum.at(f, 0))
            for j, dst in enumerate((EG, WJ, DCH)):
                ins = nc.scalar.activation(dst[:, f * BH:(f + 1) * BH], B_T[:, j * BH:(j + 1) * BH], ACT.Exp)
            ins.then_inc(d_exp.sem, 1)

        def pool_wj(pool, f):
            cols = slice(f * BH, (f + 1) * BH)
            pool.wait_ge(d_exp.sem, d_exp.at(f, 0))
            nc.gpsimd.tensor_tensor(WJ[:, cols], WJ[:, cols], DT[:, cols], ALU.mult).then_inc(d_wj.sem, 1)

        @block.tensor
        def _(pe):
            for signal in (cs_full, inter_full, intra_full, kt_full, logdecay_full, zt_full):
                pe.sem_inc(signal.sem, signal.free)
            pe.wait_ge(const_dve.sem, 6)
            pe.wait_ge(const_act.sem, 2)
            pe_turn(pe, 0)
            pe_logits(pe, 0)
            for k in range(NB):
                if k + 1 < NB:
                    pe_turn(pe, k + 1)
                if k >= 2:
                    pe_sums(pe, k - 2)
                pe_weights(pe, k)
                pe_mix(pe, k)
                if k + 1 < NB:
                    pe_logits(pe, k + 1)
                pe_turn2(pe, k)
                pe_dt(pe, k)

            def wkt(piece, k):
                return WH[:, piece, k * P:(k + 1) * P], WL[:, piece, k * P:(k + 1) * P]

            def fill(g, b, item, use, fresh, gw):
                out_bank = bank(use)
                pe.wait_ge(ring_free.sem, ring_free.at(g, use - 2))
                t0 = b % NB * TB
                if fresh:
                    piece = item if item <= PV_ else PG + KT - 1
                    pe.wait_ge(wh_ready.sem, wh_ready.at(gw, piece))
                    signal, k = wl_of(piece)
                    pe.wait_ge(signal.sem, signal.at(gw, k))
                if item < PV_:
                    for k in range(KT):
                        wh, wl = wkt(item, k)
                        ins = mm3(out_bank[:, :], wh, wl, XTH[:, k, t0:t0 + TB], XTL[:, k, t0:t0 + TB], k == 0, k == KT - 1)
                elif item == PV_:
                    for s in range(BLK):
                        for k in range(KT):
                            t = t0 + s * P
                            wh, wl = wkt(item, k)
                            ins = mm3(out_bank[:, s * P:(s + 1) * P], XTH[:, k, t:t + P], XTL[:, k, t:t + P], wh, wl,
                                      k == 0, k == KT - 1)
                else:
                    t = t0 + (item - PG) * P
                    for k in range(KT):
                        ins = mm3(out_bank[:, :], XTH[:, k, t:t + P], XTL[:, k, t:t + P], WH[:, PG + k, :], WL[:, PG + k, :],
                                  k == 0, k == KT - 1)
                ins.then_inc(ring_full.sem, 1)

            def turn_keys(g, b, use):
                pe.wait_ge(turn_free.sem, turn_free.at(g, use - 1))
                pe.wait_ge(qf_ready.sem, qf_ready.at(g, 5 * b))
                for s in range(BLK):
                    ins = nc.tensor.transpose(B_T[:, s * P:(s + 1) * P], KF[:, s * P:(s + 1) * P], IDF[:, :])
                ins.then_inc(kt_full.sem, 1)

            def scores(g, n):
                b, s = divmod(n, BLK)
                par, t = b % 2, s * P
                if s == 0:
                    pe.wait_ge(qh_ready.sem, qh_ready.at(g, 5 * b + 4))
                    pe.wait_ge(ql_ready.sem, ql_ready.at(g, 2 * b + 1))
                    pe.wait_ge(ql2_ready.sem, ql2_ready.at(g, 3 * b + 2))
                pe.wait_ge(s_ready.sem, s_ready.at(g, n - 1))
                mm3(B_S[:, :], KH[:, par, t:t + P], KL[:, par, t:t + P], QH[:, par, :, t:t + P], QL[:, par, :, t:t + P],
                        True, True).then_inc(scores_full.sem, 1)
                pe.wait_ge(m_ready.sem, m_ready.at(g, n))
                pe.wait_ge(decay_ready.sem, decay_ready.at(g, n - 1))
                nc.tensor.matmul(B_D[:, :], LTB, MH[:, :, :], start=True, stop=False)
                nc.tensor.matmul(B_D[:, :], LTB, ML[:, :, :], start=False, stop=True).then_inc(logdecay_full.sem, 1)

            def read_state(g, n):
                b, s = divmod(n, BLK)
                par, t = b % 2, s * P
                if n % NCH:
                    pe.wait_ge(inter_read.sem, inter_read.at(g, in_event(n - 1)))
                    pe.wait_ge(sth_ready.sem, sth_ready.at(g, cs_event(n - 1)))
                    pe.wait_ge(stl_ready.sem, stl_ready.at(g, cs_event(n - 1)))
                    for h in range(G):
                        c = slice(h * P, (h + 1) * P)
                        ins = mm3(B_IN[:, c], QH[:, par, h, t:t + P], QL[:, par, h, t:t + P], STH[:, c], STL[:, c], True, True)
                    ins.then_inc(inter_full.sem, 1)

            def attend(g, n):
                b, s = divmod(n, BLK)
                par, t = b % 2, s * P
                pe.wait_ge(y_ready.sem, y_ready.at(g, n - 1))
                pe.wait_ge(ph_ready.sem, ph_ready.at(g, n))
                pe.wait_ge(pl_ready.sem, pl_ready.at(g, n))
                if s == 0:
                    pe.wait_ge(v_ready.sem, v_ready.at(g, b))
                    pe.wait_ge(ring_free.sem, ring_free.at(g, v_use(b)))
                for h in range(G):
                    c = slice(h * P, (h + 1) * P)
                    ins = mm3(B_PV[:, c], PH[:, n % 2, c], PL[:, n % 2, c], VH[:, par, t:t + P], VL[:, par, t:t + P], True, True)
                ins.then_inc(intra_full.sem, 1)
                if n % NCH == NCH - 1:
                    return
                pe.wait_ge(st_ready.sem, st_ready.at(g, cs_event(n - 1)))
                pe.wait_ge(wvh_ready.sem, wvh_ready.at(g, cs_event(n)))
                pe.wait_ge(wvl_ready.sem, wvl_ready.at(g, cs_event(n)))
                if s == 0:
                    pe.wait_ge(kdh_ready.sem, kdh_ready.at(g, b))
                    pe.wait_ge(turn_free.sem, turn_free.at(g, k_use(b)))
                mm3(B_CS[:, :], KDH[:, par, t:t + P], KDL[:, par, t:t + P], WVH[:, :], WVL[:, :], True, True).then_inc(cs_full.sem, 1)

            def turn_z(g, n, use):
                pe.wait_ge(turn_free.sem, turn_free.at(g, use - 1))
                pe.wait_ge(z_ready.sem, z_ready.at(g, n))
                for h in range(G):
                    ins = nc.tensor.transpose(B_T[:, h * P:(h + 1) * P], YF[:, h * P:(h + 1) * P], IDF[:, :])
                ins.then_inc(zt_full.sem, 1)

            def project_out(g, n, use, turn_use):
                pe.wait_ge(ring_free.sem, ring_free.at(g, use - 2))
                pe.wait_ge(zth_ready.sem, zth_ready.at(g, n))
                pe.wait_ge(turn_free.sem, turn_free.at(g, turn_use))
                for h in range(G):
                    if n % NCH == 0:
                        pe.wait_ge(woh_ready.sem, woh_ready.at(g, n // NCH * G + h))
                        pe.wait_ge(wol_ready.sem, wol_ready.at(g, n // NCH * G + h))
                    c = slice(h * P, (h + 1) * P)
                    ins = mm3(bank(use)[:, :], ZTH[:, c], ZTL[:, c], WH[:, PO + h, :], WL[:, PO + h, :], h == 0, h == G - 1)
                ins.then_inc(ring_full.sem, 1)

            for item in range(NFILL):
                fill(0, 0, item, item - NFILL - FIRST, True, 0)
                if item in (0, 4):
                    pe_sums(pe, NB - 2 + item // 4)
            pe.wait_ge(d_exp.sem, d_exp.at(NB - 1, 0))
            turn_keys(0, 0, -1)
            scores(0, 0)

            def step(g, n, last, first=False):
                b, s = divmod(n, BLK)
                ring, turn = ring_order(last), turn_order(last)

                def slot(x):
                    if x in filled(n, last):
                        item = filled(n, last)[x]
                        fill(g, b + 1, item, item - FIRST if first else ring[("F", b, item)], b == NB - 1, g + 1)
                if not (last and n == NCH - 1):
                    scores(g, n + 1)
                slot("A")
                read_state(g, n)
                if not first:
                    turn_z(g, n - 1, turn[("Z", n - 1)])
                attend(g, n)
                slot("B")
                slot("C")
                if s == 1 and filled(n, last):
                    turn_keys(g, b + 1, turn[("K", b)])
                if not first:
                    project_out(g, n - 1, ring[("W", n - 1)], turn[("Z", n - 1)])

            step(0, 0, False, True)
            with pe.Fori(0, KVH - 1) as g:
                for n in steps(False):
                    step(g, n, False)
            for n in steps(True):
                step(KVH - 1, n, True)
            turn_z(KVH - 1, NCH - 1, turn_order(True)[("Z", NCH - 1)])
            pe_turn(pe, NB)
            project_out(KVH - 1, NCH - 1, ring_order(True)[("W", NCH - 1)], turn_order(True)[("Z", NCH - 1)])
            pe.wait_ge(ring_free.sem, ring_free.at(KVH - 1, ring_order(True)[("W", NCH - 2)]))
            pe_logits(pe, NB)
            for f in range(NB, 2 * NB):
                if f + 1 < 2 * NB:
                    pe_turn(pe, f + 1)
                if f == NB:
                    pe.wait_ge(ring_free.sem, ring_free.at(KVH - 1, ring_order(True)[("W", NCH - 1)]))
                pe_weights(pe, f)
                pe_mix(pe, f)
                if f + 1 < 2 * NB:
                    pe_logits(pe, f + 1)

        @block.scalar
        def _(act):
            for signal in (decay_ready, ph_ready, qh_ready, sq_ready, sth_ready, wvh_ready):
                act.sem_inc(signal.sem, signal.free)
            act.wait_ge(c_landed.sem, 16 * 9)
            nc.scalar.activation(EBH[:, :], EBF[:, :], ACT.Copy).then_inc(const_act.sem, 1)
            nc.scalar.activation(WINH[:, :, :], WINF[:, :, :], ACT.Copy).then_inc(const_act.sem, 1)
            nc.scalar.activation(ALOG[:, :], ALOG[:, :], ACT.Exp).then_inc(a_ready.sem, 1)

            def split_hi(g, i):
                act.wait_ge(w_landed[i % 2].sem, g * (NPIECE // 2 * 16) + (i // 2 + 1) * 16)
                if i < PO:
                    nc.scalar.activation(WH[:, i, :], STAGE[:, i % 2, :], ACT.Copy).then_inc(wh_ready.sem, 1)
                else:
                    k = i - PO
                    nc.scalar.activation(WH[:, i, :], STAGE[:, k % 2, :], ACT.Copy, scale=GNH[:, 0:1]).then_inc(woh_ready.sem, 1)

            def last_use(g, i):
                order = ring_order(False)
                act.wait_ge(ring_full.sem, ring_full.at(g, order[("F", NB - 2, i if i <= PV_ else NFILL - 1)]))

            def swap(g, b, j, use):
                sl = (j + 1) % 2
                act.wait_ge(ring_full.sem, ring_full.at(g, use))
                act.wait_ge(qf_ready.sem, qf_ready.at(g, 5 * b + j - (2 if j else 1)))
                nc.scalar.activation(QS[0:64, sl, :], bank(use)[64:128, :], ACT.Copy)
                nc.scalar.activation(QS[64:128, sl, :], bank(use)[0:64, :], ACT.Copy).then_inc(swap_ready.sem, 1)

            def hi(g, b, j):
                act.wait_ge(qf_ready.sem, qf_ready.at(g, 5 * b + j))
                act.wait_ge(inter_full.sem, inter_full.at(g, in_event(4 * (b - 1) - 1)))
                if j:
                    ins = nc.scalar.activation(QH[:, b % 2, j - 1, :], QF[:, (j - 1) % 2, :], ACT.Copy)
                else:
                    ins = nc.scalar.activation(KH[:, b % 2, :], KF[:, :], ACT.Copy)
                ins.then_inc(qh_ready.sem, 1)

            def values(g, b, use):
                act.wait_ge(ring_full.sem, ring_full.at(g, use))
                act.wait_ge(intra_full.sem, intra_full.at(g, 4 * (b - 1) - 1))
                act.wait_ge(wvf_ready.sem, wvf_ready.at(g, cs_event(4 * (b - 1) - 1)))
                nc.scalar.activation(VF[:, b % 2, :], bank(use)[:, :], ACT.Copy)
                nc.scalar.activation(VH[:, b % 2, :], bank(use)[:, :], ACT.Copy).then_inc(v_ready.sem, 1)

            def gate(g, b, s, use, before):
                act.wait_ge(ring_full.sem, ring_full.at(g, use))
                act.wait_ge(ring_free.sem, ring_free.at(g, before))
                nc.scalar.activation(TH[:, :], bank(use)[:, :], ACT.Tanh, scale=0.5).then_inc(tanh_ready.sem, 1)

            def keys_hi(g, b):
                act.wait_ge(kt_full.sem, kt_full.at(g, b))
                act.wait_ge(cs_full.sem, cs_full.at(g, cs_event(4 * (b - 1) - 1)))
                nc.scalar.activation(KDH[:, b % 2, :], B_T[:, :], ACT.Copy).then_inc(kdh_ready.sem, 1)

            def decay(g, n):
                act.wait_ge(logdecay_full.sem, logdecay_full.at(g, n))
                act.wait_ge(ph_ready.sem, ph_ready.at(g, n - 1))
                act.wait_ge(pl_ready.sem, pl_ready.at(g, n - 1))
                nc.scalar.activation(PF[:, :], B_D[:, :], ACT.Exp).then_inc(decay_ready.sem, 1)

            def p_hi(g, n):
                act.wait_ge(p_ready.sem, p_ready.at(g, n))
                act.wait_ge(intra_full.sem, intra_full.at(g, n - 2))
                nc.scalar.activation(PH[:, n % 2, :], PF[:, :], ACT.Copy).then_inc(ph_ready.sem, 1)

            def wv_hi(g, n):
                if n % NCH == NCH - 1:
                    return
                act.wait_ge(wvf_ready.sem, wvf_ready.at(g, cs_event(n)))
                act.wait_ge(cs_full.sem, cs_full.at(g, cs_event(n - 1)))
                nc.scalar.activation(WVH[:, :], WVF[:, :, :].rearrange("p h e -> p (h e)"), ACT.Copy).then_inc(wvh_ready.sem, 1)

            def state_hi(g, n):
                if n % NCH == NCH - 1:
                    return
                act.wait_ge(st_ready.sem, st_ready.at(g, cs_event(n)))
                act.wait_ge(inter_full.sem, inter_full.at(g, in_event(n)))
                nc.scalar.activation(STH[:, :], ST[:, :], ACT.Copy).then_inc(sth_ready.sem, 1)

            def square(g, n):
                act.wait_ge(y_ready.sem, y_ready.at(g, n))
                act.wait_ge(ss_ready.sem, ss_ready.at(g, n - 1))
                nc.scalar.activation(SQ[:, :, :].rearrange("p h e -> p (h e)"), YF[:, :], ACT.Square,
                                         scale=float(P) ** -0.5).then_inc(sq_ready.sem, 1)

            def zt_hi(g, n, before):
                act.wait_ge(zt_full.sem, zt_full.at(g, n))
                act.wait_ge(ring_full.sem, ring_full.at(g, before))
                nc.scalar.activation(ZTH[:, :], B_T[:, :], ACT.Copy).then_inc(zth_ready.sem, 1)

            act_normalise(act, 0, 0)
            act_turned(act, 0)
            act_normalise(act, 0, 1)
            for k in range(NB):
                act_exp(act, k)
                if k + 1 < NB:
                    act_turned(act, k + 1)
                act_weights(act, k)
                if k >= 1:
                    act_dt_exp(act, k - 1)
                if k >= 2:
                    act_sums(act, k - 2)
                if k:
                    for i in range(3 * k - 2, 3 * k):
                        split_hi(0, i)
                split_hi(0, 3 * k)
                act_normalise(act, 1, k)
                act_turned2(act, k)
                if k + 2 < NB:
                    act_normalise(act, 0, k + 2)
            act_dt_exp(act, NB - 1)
            for item in range(NFILL):
                use = item - NFILL - FIRST
                if item < PV_:
                    swap(0, 0, item, use)
                if 0 < item <= PV_:
                    hi(0, 0, item - 1)
                if item in (0, 4):
                    act_sums(act, NB - 2 + item // 4)
                if item == PV_:
                    values(0, 0, use)
                elif item > PV_:
                    gate(0, 0, item - PG, use, use - 1)
            keys_hi(0, 0)
            decay(0, 0)
            p_hi(0, 0)
            wv_hi(0, 0)

            def step(g, n, last, first=False):
                b, s = divmod(n, BLK)
                ring = ring_order(last)

                def slot(x, part):
                    if x not in filled(n, last):
                        return
                    item = filled(n, last)[x]
                    use = item - FIRST if first else ring[("F", b, item)]
                    if item < PV_:
                        (swap(g, b + 1, item, use) if part == 0 else hi(g, b + 1, item))
                    elif part == 0 and item == PV_:
                        values(g, b + 1, use)
                    elif part == 0:
                        gate(g, b + 1, item - PG, use, use - 1)

                def next_weights(when):
                    for i in () if last else when.get(n, ()):
                        last_use(g, i)
                        split_hi(g + 1, i)
                nxt = not (last and n == NCH - 1)
                if nxt:
                    decay(g, n + 1)
                if n == 1:
                    act.wait_ge(ring_full.sem, ring_full.at(g, -1))
                    for i in range(PO, PO + 2):
                        split_hi(g, i)
                if not filled(n, last):
                    zt_hi(g, n - 1, ring[("W", n - 2)])
                if nxt:
                    p_hi(g, n + 1)
                if not first and (n - 1) % BLK == 0 and filled(n - 1, last):
                    hi(g, (n - 1) // BLK + 1, filled(n - 1, last)["C"])
                next_weights(EARLY)
                slot("A", 0)
                if not first and filled(n, last):
                    zt_hi(g, n - 1, ring[("W", n - 2)])
                if not filled(n, last):
                    square(g, n)
                if nxt:
                    wv_hi(g, n + 1)
                if filled(n, last).get("B", PG) < PG:
                    slot("B", 0)
                if filled(n, last):
                    square(g, n)
                state_hi(g, n)
                next_weights(MID)
                if n == 1:
                    for i in range(PO + 2, NPIECE):
                        split_hi(g, i)
                if filled(n, last).get("B", 0) >= PG:
                    slot("B", 0)
                slot("A", 1)
                slot("C", 0)
                slot("B", 1)
                if s == 1 and filled(n, last):
                    keys_hi(g, b + 1)

            step(0, 0, False, True)
            with act.Fori(0, KVH - 1) as g:
                for n in steps(False):
                    step(g, n, False)
            for n in steps(True):
                step(KVH - 1, n, True)
            act_normalise(act, 0, NB)
            zt_hi(KVH - 1, NCH - 1, ring_order(True)[("W", NCH - 2)])
            act_turned(act, NB)
            act_normalise(act, 0, NB + 1)
            for f in range(NB, 2 * NB):
                act_exp(act, f)
                if NB + 1 < f + 1 < 2 * NB:
                    act_normalise(act, 0, f + 1)
                if f + 1 < 2 * NB:
                    act_turned(act, f + 1)
                act_weights(act, f)

        @block.gpsimd
        def _(pool):
            for signal in (pl_ready, ql_ready, wvf_ready, wvl_ready, rm_ready):
                pool.sem_inc(signal.sem, signal.free)
            nc.gpsimd.memset(HALF[:, :], -0.5).then_inc(const_pool.sem, 1)
            nc.gpsimd.memset(EPSC[:, :], EPS).then_inc(const_pool.sem, 1)
            pool.wait_ge(const_pool.sem, 2)
            def split_lo(g, i):
                pool.wait_ge(wh_ready.sem, wh_ready.at(g, i))
                nc.gpsimd.tensor_tensor(WL[:, i, :], STAGE[:, i % 2, :], WH[:, i, :], ALU.subtract).then_inc(wl_of(i)[0].sem, 1)

            def times_sin(g, b, j):
                sl = (j + 1) % 2
                pool.wait_ge(swap_ready.sem, swap_ready.at(g, 5 * b + j))
                t0 = b % NB * TB
                nc.gpsimd.tensor_tensor(QS[:, sl, :], QS[:, sl, :], SIN[:, t0:t0 + TB], ALU.mult).then_inc(sin_ready.sem, 1)

            def lo(g, b, j):
                pool.wait_ge(qh_ready.sem, qh_ready.at(g, 5 * b + j))
                if j:
                    ins = nc.gpsimd.tensor_tensor(QL[:, b % 2, j - 1, :], QF[:, (j - 1) % 2, :], QH[:, b % 2, j - 1, :], ALU.subtract)
                else:
                    ins = nc.gpsimd.tensor_tensor(KL[:, b % 2, :], KF[:, :], KH[:, b % 2, :], ALU.subtract)
                ins.then_inc(ql_ready.sem, 1)

            def tab(T, g, n):
                at = n % NCH * H + n // NCH * G
                return T[:, at + g * G:at + (g + 1) * G] if isinstance(g, int) else T[:, bass.ds(g * G + at, G)]

            def masked_g(g, n):
                pool.wait_ge(logdecay_full.sem, logdecay_full.at(g, n - 1))
                tri = TRIB[:, None, :].broadcast_to([P, G, P])
                nc.gpsimd.tensor_tensor(MH[:, :, :], tri, tab(GH, g, n)[:, :, None].broadcast_to([P, G, P]), ALU.mult)
                nc.gpsimd.tensor_tensor(ML[:, :, :], tri, tab(GL, g, n)[:, :, None].broadcast_to([P, G, P]), ALU.mult).then_inc(m_ready.sem, 1)

            def masked_dt(g, n):
                pool.wait_ge(p_ready.sem, p_ready.at(g, n - 1))
                nc.gpsimd.tensor_tensor(DM[:, :, :], TRIB[:, None, :].broadcast_to([P, G, P]),
                                        tab(DT, g, n)[:, :, None].broadcast_to([P, G, P]), ALU.mult).then_inc(dm_ready.sem, 1)

            def weighted_v(g, n):
                if n % NCH == NCH - 1:
                    return
                b, s = divmod(n, BLK)
                pool.wait_ge(wvh_ready.sem, wvh_ready.at(g, cs_event(n - 1)))
                pool.wait_ge(wvl_ready.sem, wvl_ready.at(g, cs_event(n - 1)))
                if s == 0:
                    pool.wait_ge(v_ready.sem, v_ready.at(g, b))
                nc.gpsimd.tensor_tensor(WVF[:, :, :], VF[:, b % 2, None, s * P:(s + 1) * P].broadcast_to([P, G, P]),
                                            tab(WJ, g, n)[:, :, None].broadcast_to([P, G, P]), ALU.mult).then_inc(wvf_ready.sem, 1)

            def wv_lo(g, n):
                if n % NCH == NCH - 1:
                    return
                pool.wait_ge(wvh_ready.sem, wvh_ready.at(g, cs_event(n)))
                pool.wait_ge(cs_full.sem, cs_full.at(g, cs_event(n - 1)))
                nc.gpsimd.tensor_tensor(WVL[:, :], WVF[:, :, :].rearrange("p h e -> p (h e)"), WVH[:, :], ALU.subtract).then_inc(wvl_ready.sem, 1)

            def p_lo(g, n):
                pool.wait_ge(ph_ready.sem, ph_ready.at(g, n))
                nc.gpsimd.tensor_tensor(PL[:, n % 2, :], PF[:, :], PH[:, n % 2, :], ALU.subtract).then_inc(pl_ready.sem, 1)

            def inv_rms(g, n):
                pool.wait_ge(ss_ready.sem, ss_ready.at(g, n))
                nc.gpsimd.tensor_tensor(RM[:, :], SS[:, :], EPSC[:, :], ALU.add).then_inc(rm_ready.sem, 1)
                pool.wait_ge(rm_ready.sem, rm_ready.at(g, n))
                pool.wait_ge(z_ready.sem, z_ready.at(g, n - 1))
                nc.gpsimd.tensor_tensor(RR[:, :], RM[:, :], HALF[:, :], ALU.pow).then_inc(rr_ready.sem, 1)

            pool_rstd(pool, 0, 0)
            pool_rstd(pool, 0, 1)
            for k in range(NB):
                if k >= 2:
                    pool_wj(pool, k - 2)
                for i in range(max(3 * k - 2, 0), 3 * k + 1):
                    split_lo(0, i)
                pool_rstd(pool, 1, k)
                if k + 2 < NB:
                    pool_rstd(pool, 0, k + 2)
                if k:
                    pool_dt(pool, k - 1)
            pool_dt(pool, NB - 1)
            pool.wait_ge(rope_landed.sem, 32)
            for item in range(PV_):
                times_sin(0, 0, item)
                if item in (0, 4):
                    pool_wj(pool, NB - 2 + item // 4)
                if item in (1, 4):
                    lo(0, 0, item - 1)
            pool.wait_ge(d_wj.sem, d_wj.at(NB - 1, 0))
            pool.wait_ge(d_gl.sem, d_gl.at(NB - 1, 0))
            masked_g(0, 0)
            masked_dt(0, 0)
            masked_g(0, 1)
            p_lo(0, 0)
            masked_dt(0, 1)
            weighted_v(0, 0)
            wv_lo(0, 0)

            def step(g, n, last):
                b, s = divmod(n, BLK)

                def sine(x):
                    if filled(n, last).get(x, PV_) < PV_:
                        times_sin(g, b + 1, filled(n, last)[x])
                nxt = not (last and n == NCH - 1)
                if not (last and n >= NCH - 2):
                    masked_g(g, n + 2)
                if nxt:
                    p_lo(g, n + 1)
                if n and (n - 1) % BLK <= 1 and filled(n - 1, last):
                    lo(g, (n - 1) // BLK + 1, filled(n - 1, last)["A"])
                if nxt:
                    weighted_v(g, n + 1)
                sine("A")
                if not filled(n, last):
                    inv_rms(g, n)
                if nxt and filled(n, last):
                    wv_lo(g, n + 1)
                if not (last and n >= NCH - 2):
                    masked_dt(g, n + 2)
                if nxt and not filled(n, last):
                    wv_lo(g, n + 1)
                sine("B")
                if filled(n, last):
                    inv_rms(g, n)
                for i in () if last else MID.get(n, ()):
                    split_lo(g + 1, i)
                sine("C")

            step(0, 0, False)
            with pool.Fori(0, KVH - 1) as g:
                for n in steps(False):
                    step(g, n, False)
            for n in steps(True):
                step(KVH - 1, n, True)
            pool_rstd(pool, 0, NB)
            pool_rstd(pool, 0, NB + 1)
            for f in range(NB, 2 * NB):
                if f + 2 < 2 * NB:
                    pool_rstd(pool, 0, f + 2)
                for i in range(BLK if f + 1 < 2 * NB else 0):
                    pool_sum(pool, f, i)

        @block.vector
        def _(dve):
            for signal in (ql2_ready, s_ready, p_ready, qf_ready, ring_free, turn_free, z_ready, wol_ready, inter_read, y_ready, ss_ready,
                           st_ready, stl_ready):
                dve.sem_inc(signal.sem, signal.free)
            dve_stats(dve, 0, 0)
            dve.wait_ge(c_landed.sem, 16 * 9)
            nc.vector.tensor_copy(MB[:, :, :], MASKS[:, :, :]).then_inc(const_dve.sem, 1)
            nc.vector.memset(ONES[:, :], 1.0).then_inc(const_dve.sem, 1)
            nc.vector.tensor_scalar(GNH[:, :], GN[:, :], 0.5, None, ALU.mult).then_inc(const_dve.sem, 1)
            dve.wait_ge(const_act.sem, 2)
            nc.vector.tensor_tensor(EBL[:, :], EBF[:, :], EBH[:, :], ALU.subtract).then_inc(const_dve.sem, 1)
            nc.vector.tensor_tensor(WINL[:, :, :], WINF[:, :, :], WINH[:, :, :], ALU.subtract).then_inc(const_dve.sem, 2)
            dve_stats(dve, 0, 1)
            for k in range(NB):
                dve_gate(dve, k)
                if k:
                    dve_dt_in(dve, k - 1)
                dve_scaled(dve, k)
                dve_add(dve, k)
                dve_stats(dve, 1, k)
                if k:
                    dve_dt(dve, k - 1)
                if k + 2 < NB:
                    dve_stats(dve, 0, k + 2)
                dve_turned2(dve, k)
            dve_dt_in(dve, NB - 1)
            dve_dt(dve, NB - 1)
            dve.wait_ge(rope_landed.sem, 32)

            def tab(T, g, n):
                at = n % NCH * H + n // NCH * G
                return T[:, at + g * G:at + (g + 1) * G] if isinstance(g, int) else T[:, bass.ds(g * G + at, G)]

            def rotate(g, b, j, use, part):
                dst = QF[:, (j - 1) % 2, :] if j else KF[:, :]
                t0 = b % NB * TB
                if part == 0:
                    dve.wait_ge(swap_ready.sem, swap_ready.at(g, 5 * b + j))
                    dve.wait_ge(qh_ready.sem, qh_ready.at(g, 5 * b + j - 2))
                    if j <= 1:
                        dve.wait_ge(ql_ready.sem, ql_ready.at(g, 2 * b - 2 + j))
                    else:
                        dve.wait_ge(ql2_ready.sem, ql2_ready.at(g, 3 * b + j - 3))
                    if j == 0:
                        dve.wait_ge(kt_full.sem, kt_full.at(g, b - 1))
                    nc.vector.tensor_tensor(dst, bank(use)[:, :], COS[:, t0:t0 + TB], ALU.mult).then_inc(ring_free.sem, 1)
                else:
                    dve.wait_ge(ring_free.sem, ring_free.at(g, use))
                    dve.wait_ge(sin_ready.sem, sin_ready.at(g, 5 * b + j))
                    nc.vector.tensor_tensor(dst, dst, QS[:, (j + 1) % 2, :], ALU.add).then_inc(qf_ready.sem, 1)

            def q_lo(g, b, j):
                dve.wait_ge(qh_ready.sem, qh_ready.at(g, 5 * b + j))
                nc.vector.tensor_tensor(QL[:, b % 2, j - 1, :], QF[:, (j - 1) % 2, :], QH[:, b % 2, j - 1, :],
                                        ALU.subtract).then_inc(ql2_ready.sem, 1)

            def v_lo(g, b, use):
                dve.wait_ge(v_ready.sem, v_ready.at(g, b))
                dve.wait_ge(intra_full.sem, intra_full.at(g, 4 * (b - 1) - 1))
                nc.vector.tensor_tensor(VL[:, b % 2, :], bank(use)[:, :], VH[:, b % 2, :], ALU.subtract).then_inc(ring_free.sem, 1)

            def silu2(g, b, s, use):
                dve.wait_ge(tanh_ready.sem, tanh_ready.at(g, 4 * b + s))
                slot_of = s + b % 2 * (s == BLK - 1)
                dve.wait_ge(z_ready.sem, z_ready.at(g, 4 * (b - (2 if s == BLK - 1 else 1)) + s))
                nc.vector.scalar_tensor_tensor(G2[:, slot_of, :], TH[:, :], 1.0, bank(use)[:, :], ALU.add, ALU.mult).then_inc(ring_free.sem, 1)

            def keys_lo(g, b):
                dve.wait_ge(kdh_ready.sem, kdh_ready.at(g, b))
                dve.wait_ge(cs_full.sem, cs_full.at(g, cs_event(4 * (b - 1) - 1)))
                nc.vector.tensor_tensor(KDL[:, b % 2, :], B_T[:, :], KDH[:, b % 2, :], ALU.subtract).then_inc(turn_free.sem, 1)

            def decayed(g, n):
                dve.wait_ge(scores_full.sem, scores_full.at(g, n))
                dve.wait_ge(dm_ready.sem, dm_ready.at(g, n))
                dm = DM[:, :, :].rearrange("p h i -> p (h i)")
                nc.vector.tensor_tensor(dm, B_S[:, :], dm, ALU.mult).then_inc(s_ready.sem, 1)
                dve.wait_ge(s_ready.sem, s_ready.at(g, n))
                dve.wait_ge(decay_ready.sem, decay_ready.at(g, n))
                nc.vector.tensor_tensor(PF[:, :], dm, PF[:, :], ALU.mult).then_inc(p_ready.sem, 1)

            def combine(g, n):
                if n % NCH == 0:
                    dve.wait_ge(zt_full.sem, zt_full.at(g, n - 1))
                    dve.wait_ge(intra_full.sem, intra_full.at(g, n))
                    nc.vector.tensor_copy(YF[:, :], B_PV[:, :]).then_inc(y_ready.sem, 1)
                    return
                dve.wait_ge(inter_full.sem, inter_full.at(g, in_event(n)))
                dve.wait_ge(zt_full.sem, zt_full.at(g, n - 1))
                nc.vector.tensor_tensor(YF[:, :].rearrange("p (h e) -> p h e", h=G), B_IN[:, :].rearrange("p (h e) -> p h e", h=G),
                                            tab(EG, g, n)[:, :, None].broadcast_to([P, G, P]), ALU.mult).then_inc(inter_read.sem, 1)
                dve.wait_ge(inter_read.sem, inter_read.at(g, in_event(n)))
                dve.wait_ge(intra_full.sem, intra_full.at(g, n))
                nc.vector.tensor_tensor(YF[:, :], B_PV[:, :], YF[:, :], ALU.add).then_inc(y_ready.sem, 1)

            def update_state(g, n):
                if n % NCH == NCH - 1:
                    return
                dve.wait_ge(cs_full.sem, cs_full.at(g, cs_event(n)))
                dve.wait_ge(sth_ready.sem, sth_ready.at(g, cs_event(n - 1)))
                dve.wait_ge(stl_ready.sem, stl_ready.at(g, cs_event(n - 1)))
                if n % NCH == 0:
                    nc.vector.tensor_copy(ST[:, :], B_CS[:, :]).then_inc(st_ready.sem, 1)
                    return
                dc = tab(DCH, g, n)
                for h in range(G):
                    c = slice(h * P, (h + 1) * P)
                    ins = nc.vector.scalar_tensor_tensor(ST[:, c], ST[:, c], dc[:, h:h + 1], B_CS[:, c], ALU.mult, ALU.add)
                ins.then_inc(st_ready.sem, 1)

            def state_lo(g, n):
                if n % NCH == NCH - 1:
                    return
                dve.wait_ge(sth_ready.sem, sth_ready.at(g, cs_event(n)))
                dve.wait_ge(inter_full.sem, inter_full.at(g, in_event(n)))
                nc.vector.tensor_tensor(STL[:, :], ST[:, :], STH[:, :], ALU.subtract).then_inc(stl_ready.sem, 1)

            def sum_squares(g, n):
                dve.wait_ge(sq_ready.sem, sq_ready.at(g, n))
                dve.wait_ge(rm_ready.sem, rm_ready.at(g, n - 1))
                nc.vector.tensor_reduce(SS[:, :], SQ[:, :, :], AX.X, ALU.add).then_inc(ss_ready.sem, 1)

            def gated(g, n):
                b, s = divmod(n, BLK)
                dve.wait_ge(rr_ready.sem, rr_ready.at(g, n))
                if s == 0:
                    dve.wait_ge(ring_free.sem, ring_free.at(g, gate_use(b)))
                for h in range(G):
                    c = slice(h * P, (h + 1) * P)
                    ins = nc.vector.scalar_tensor_tensor(YF[:, c], YF[:, c], RR[:, h:h + 1], G2[:, s + b % 2 * (s == BLK - 1), c],
                                                         ALU.mult, ALU.mult)
                ins.then_inc(z_ready.sem, 1)

            def wo_lo(g, k):
                act_hi, stage = WH[:, PO + k, :], STAGE[:, k % 2, :]
                dve.wait_ge(woh_ready.sem, woh_ready.at(g, k))
                nc.vector.scalar_tensor_tensor(WL[:, PO + k, :], stage, GNH[:, 0:1], act_hi, ALU.mult, ALU.subtract).then_inc(wol_ready.sem, 1)

            def w_lo(g, i):
                dve.wait_ge(wh_ready.sem, wh_ready.at(g, i))
                nc.vector.tensor_tensor(WL[:, i, :], STAGE[:, i % 2, :], WH[:, i, :], ALU.subtract).then_inc(wl_early.sem, 1)

            def zt_lo(g, n, before):
                dve.wait_ge(zth_ready.sem, zth_ready.at(g, n))
                dve.wait_ge(ring_full.sem, ring_full.at(g, before))
                nc.vector.tensor_tensor(ZTL[:, :], B_T[:, :], ZTH[:, :], ALU.subtract).then_inc(turn_free.sem, 1)

            def add_out(g, n, use):
                dve.wait_ge(ring_full.sem, ring_full.at(g, use))
                nc.vector.tensor_tensor(ACC[:, n % NCH, :], ACC[:, n % NCH, :], bank(use)[:, :], ALU.add).then_inc(ring_free.sem, 1)

            for item in range(NFILL):
                use = item - NFILL - FIRST
                if item - 2 in (1, 2, 4):
                    q_lo(0, 0, item - 2)
                if item < PV_:
                    rotate(0, 0, item, use, 0)
                if 0 < item <= PV_:
                    rotate(0, 0, item - 1, use - 1, 1)
                if item == PV_:
                    v_lo(0, 0, use)
                elif item > PV_:
                    silu2(0, 0, item - PG, use)
            keys_lo(0, 0)
            dve.wait_ge(d_wj.sem, d_wj.at(NB - 1, 0))
            decayed(0, 0)

            def step(g, n, last, first=False):
                b, s = divmod(n, BLK)
                ring = ring_order(last)

                def slot(x, part):
                    if x not in filled(n, last):
                        return
                    item = filled(n, last)[x]
                    use = item - FIRST if first else ring[("F", b, item)]
                    if item < PV_:
                        rotate(g, b + 1, item, use, part)
                    elif part == 0 and item == PV_:
                        v_lo(g, b + 1, use)
                    elif part == 0:
                        silu2(g, b + 1, item - PG, use)
                if not (last and n == NCH - 1):
                    decayed(g, n + 1)
                if not first and filled(n - 1, last):
                    before = filled(n - 1, last)
                    if (n - 1) % BLK == 0:
                        rotate(g, (n - 1) // BLK + 1, before["C"], -1 if n == 1 else ring[("F", (n - 1) // BLK, before["C"])], 1)
                        q_lo(g, (n - 1) // BLK + 1, before["B"])
                        q_lo(g, (n - 1) // BLK + 1, before["C"])
                    elif (n - 1) % BLK == 1:
                        q_lo(g, (n - 1) // BLK + 1, before["B"])
                for i in () if last else EARLY.get(n, ()):
                    w_lo(g + 1, i)
                if n == 1:
                    for k in range(2):
                        wo_lo(g, k)
                if not filled(n, last):
                    combine(g, n)
                if not first:
                    zt_lo(g, n - 1, ring[("W", n - 2)])
                slot("A", 0)
                if filled(n, last):
                    combine(g, n)
                if not filled(n, last):
                    sum_squares(g, n)
                update_state(g, n)
                slot("A", 1)
                if filled(n, last).get("B", PG) < PG:
                    slot("B", 0)
                if filled(n, last):
                    sum_squares(g, n)
                state_lo(g, n)
                if last and n >= NCH - BLK:
                    dve_stats(dve, 0, NB, (n - NCH + BLK,))
                if filled(n, last).get("B", 0) >= PG:
                    slot("B", 0)
                if n == 1:
                    for k in range(2, G):
                        wo_lo(g, k)
                slot("C", 0)
                slot("B", 1)
                gated(g, n)
                if s == 1 and filled(n, last):
                    keys_lo(g, b + 1)
                if not first:
                    add_out(g, n - 1, ring[("W", n - 1)])

            step(0, 0, False, True)
            with dve.Fori(0, KVH - 1) as g:
                for n in steps(False):
                    step(g, n, False)
            for n in steps(True):
                step(KVH - 1, n, True)
            zt_lo(KVH - 1, NCH - 1, ring_order(True)[("W", NCH - 2)])
            dve_stats(dve, 0, NB + 1)
            add_out(KVH - 1, NCH - 1, ring_order(True)[("W", NCH - 1)])
            for f in range(NB, 2 * NB):
                dve_gate(dve, f)
                if f + 2 < 2 * NB:
                    dve_stats(dve, 0, f + 2)
                if f + 1 < 2 * NB:
                    dve_mixed(dve, f)
            dve_scaled(dve, 2 * NB - 1)
            dve.wait_ge(f_acc.sem, f_acc.at(2 * NB - 2, 3))
            dve_add(dve, 2 * NB - 1)


def constants():
    f = np.float32
    inv = f(1.0) / np.power(f(10000.0), np.arange(0, P, 2, dtype=f) / f(P), dtype=f)
    ang = np.arange(L, dtype=f)[None, :] * np.concatenate([inv, inv])[:, None]
    cos, sin = np.cos(ang, dtype=f), np.sin(ang, dtype=f)
    sin[:P // 2] *= f(-1.0)
    t = np.arange(P)
    masks = np.concatenate([(t[:, None] > t[None, :]), (t[:, None] <= t[None, :]), (t[:, None] == t[None, :])], 1).astype(f)
    return cos, sin, masks


def kernel(**inputs):
    import concourse.bacc as bacc
    from concourse.bass_utils import run_bass_kernel_spmd

    a = {k.replace("L0_attn_", "").replace("L0_ffn_", ""): np.asarray(v) for k, v in inputs.items()}

    def by_tile(w):
        return w.reshape(w.shape[0], KT, P).transpose(2, 1, 0)
    cos, sin, masks = constants()
    wall = np.empty((KVH, NPIECE, P, HID), a["Wq"].dtype)
    for g in range(KVH):
        wall[g, PK] = by_tile(a["Wk"][g * P:(g + 1) * P]).reshape(P, HID)
        wall[g, PV_] = by_tile(a["Wv"][g * P:(g + 1) * P]).reshape(P, HID)
        for h in range(G):
            c = slice((g * G + h) * P, (g * G + h + 1) * P)
            wall[g, PQ + h] = by_tile(a["Wq"][c]).reshape(P, HID)
            wall[g, PO + h] = a["Wo"][:, c].T
        wall[g, PG:PG + KT] = by_tile(a["Wg"][g * GW:(g + 1) * GW]).transpose(1, 0, 2)
    rep = lambda v: np.broadcast_to(v[None, :], (P, v.shape[0]))
    xs = a["hidden_states"].reshape(NB, BLK, P, HID).transpose(0, 2, 1, 3)
    arrays = {
        "x": xs, "cos": cos, "sin": sin, "masks": masks, "wall": wall, "rwt": by_tile(a["router_weight"]), "rb": rep(a["router_bias"]),
        "eb2": np.concatenate([a["expert_bias"]] * 2, 0), "wint": by_tile(a["Win"]), "dtb": rep(a["dt_bias"]),
        "alog": rep(a["A_log_bias"]), "gn": a["gnorm_w"].reshape(P, 1),
    }
    arrays = {f"in_{k}": np.ascontiguousarray(v) for k, v in arrays.items()}
    nc = bacc.Bacc("TRN2", target_bir_lowering=False, num_devices=1)
    aps = [nc.dram_tensor(k, v.shape, mybir.dt.from_np(v.dtype), kind="ExternalInput").ap() for k, v in arrays.items()]
    o = nc.dram_tensor("out", (NB, P, BLK, HID), F32, kind="ExternalOutput").ap()
    build(nc, *aps, o)
    r = run_bass_kernel_spmd(nc, [arrays], core_ids=[0])
    return r.results[0]["out"].transpose(0, 2, 1, 3).reshape(1, L, HID)
```
